# Optimizing a Trainium2 kernel written in Bass

```python
import numpy as np
import jax
import jax.numpy as jnp

def _softmax(x, axis=-1):
    return jax.nn.softmax(x, axis=axis)

def _gelu(x):
    return jax.nn.gelu(x, approximate=True)

def _silu(x):
    return jax.nn.silu(x)

def _sigmoid(x):
    return jax.nn.sigmoid(x)

def _layernorm(x, axis=-1, eps=1e-05):
    m = jnp.mean(x, axis=axis, keepdims=True)
    v = jnp.var(x, axis=axis, keepdims=True)
    return (x - m) / jnp.sqrt(v + eps)

def _scatter_add(tgt, idx, src, axis=0):
    return tgt.at[idx].add(src)

def _segment_sum(src, seg, n):
    return jax.ops.segment_sum(src, seg, n)
kernel_name = 'mk_gnn_preln_d2_gnn_r16_a24de4'

def setup_inputs(seed: int=0):
    np.random.seed(seed)
    _w = jnp.asarray

    def _rec_inputs():
        import jax
        import jax.numpy as jnp
        _gk = jax.random.key(seed)
        x = -0.0002117 + 1 * jax.random.normal(jax.random.fold_in(_gk, 1), (6250, 256), jnp.float32)
        src = jax.random.randint(jax.random.fold_in(_gk, 2), (100000,), 0, 6250, jnp.int32)
        dst = jax.random.randint(jax.random.fold_in(_gk, 3), (100000,), 0, 6250, jnp.int32)
        _o = jnp.argsort(dst, stable=True)
        src = src[_o]
        dst = dst[_o]
        return (x, src, dst)
    x, src, dst = _rec_inputs()

    def _L0_gnn_setup():
        import jax, jax.numpy as jnp
        import numpy as np
        N_NODES = 6250
        N_EDGES = 100000
        D = 256

        def _sage_layer(x, src, dst, inv_deg, W_self, W_neigh, b):
            agg = jax.ops.segment_sum(x[src], dst, num_segments=N_NODES)
            mean = agg * inv_deg[:, None]
            return x @ W_self + mean @ W_neigh + b
        key = jax.random.key(seed)
        ks = jax.random.split(key, 16)
        inp = {'features': jax.random.normal(ks[0], (N_NODES, D), dtype=jnp.float32), 'src': jax.random.randint(ks[1], (N_EDGES,), 0, N_NODES, dtype=jnp.int32), 'dst': jax.random.randint(ks[2], (N_EDGES,), 0, N_NODES, dtype=jnp.int32)}
        scale = 1.0 / np.sqrt(D)
        for i in range(3):
            inp[f'W{i}_self'] = jax.random.normal(ks[3 + 4 * i], (D, D), dtype=jnp.float32) * scale
            inp[f'W{i}_neigh'] = jax.random.normal(ks[4 + 4 * i], (D, D), dtype=jnp.float32) * scale
            inp[f'b{i}'] = jnp.zeros((D,), dtype=jnp.float32)
        return inp
    _L0_gnn_all = _L0_gnn_setup()
    _L0_gnn_in = {k: v for k, v in _L0_gnn_all.items() if k in ('W0_self', 'W0_neigh', 'b0', 'W1_self', 'W1_neigh', 'b1', 'W2_self', 'W2_neigh', 'b2')}
    del _L0_gnn_all

    def _L1_gnn_setup():
        import jax, jax.numpy as jnp
        import numpy as np
        N_NODES = 3125
        N_EDGES = 50000
        D_MODEL = 256
        NUM_HEADS = 8
        HEAD_DIM = D_MODEL // NUM_HEADS
        D_FF = 2 * D_MODEL
        NEG_SLOPE = 0.2
        BN_EPS = 1e-05

        def _batch_norm(h, g, b):
            mean = jnp.mean(h, axis=0)
            var = jnp.mean((h - mean) ** 2, axis=0)
            return (h - mean) * jax.lax.rsqrt(var + BN_EPS) * g + b
        key = jax.random.key(seed)
        ks = jax.random.split(key, 16)
        x = jax.random.normal(ks[0], (N_NODES, D_MODEL), dtype=jnp.float32)
        src = jax.random.randint(ks[1], (N_EDGES,), 0, N_NODES)
        off = jax.random.randint(ks[2], (N_EDGES,), 1, N_NODES)
        dst = (src + off) % N_NODES
        edge_index = jnp.stack([src, dst]).astype(jnp.int64)

        def lin(k, fi, fo):
            s = 1.0 / np.sqrt(fi)
            return jax.random.uniform(k, (fi, fo), jnp.float32, -s, s)
        inp = {'x': x, 'edge_index': edge_index, 'Wq': lin(ks[3], D_MODEL, D_MODEL), 'bq': jnp.zeros((D_MODEL,), jnp.float32), 'Wk': lin(ks[4], D_MODEL, D_MODEL), 'bk': jnp.zeros((D_MODEL,), jnp.float32), 'Wv': lin(ks[5], D_MODEL, D_MODEL), 'bv': jnp.zeros((D_MODEL,), jnp.float32), 'Wo': lin(ks[6], D_MODEL, D_MODEL), 'bo': jnp.zeros((D_MODEL,), jnp.float32), 'W1': lin(ks[7], D_MODEL, D_FF), 'b1': jnp.zeros((D_FF,), jnp.float32), 'W2': lin(ks[8], D_FF, D_MODEL), 'b2': jnp.zeros((D_MODEL,), jnp.float32), 'bn1_g': jnp.ones((D_MODEL,), jnp.float32), 'bn1_b': jnp.zeros((D_MODEL,), jnp.float32), 'bn2_g': jnp.ones((D_MODEL,), jnp.float32), 'bn2_b': jnp.zeros((D_MODEL,), jnp.float32)}
        return inp
    _L1_gnn_all = _L1_gnn_setup()
    _L1_gnn_in = {k: v for k, v in _L1_gnn_all.items() if k in ('Wq', 'bq', 'Wk', 'bk', 'Wv', 'bv', 'Wo', 'bo', 'W1', 'b1', 'W2', 'b2', 'bn1_g', 'bn1_b', 'bn2_g', 'bn2_b')}
    del _L1_gnn_all
    return {'x': x, 'src': src, 'dst': dst, 'L0_gnn_W0_self': _L0_gnn_in['W0_self'], 'L0_gnn_W0_neigh': _L0_gnn_in['W0_neigh'], 'L0_gnn_b0': _L0_gnn_in['b0'], 'L0_gnn_W1_self': _L0_gnn_in['W1_self'], 'L0_gnn_W1_neigh': _L0_gnn_in['W1_neigh'], 'L0_gnn_b1': _L0_gnn_in['b1'], 'L0_gnn_W2_self': _L0_gnn_in['W2_self'], 'L0_gnn_W2_neigh': _L0_gnn_in['W2_neigh'], 'L0_gnn_b2': _L0_gnn_in['b2'], 'L1_gnn_Wq': _L1_gnn_in['Wq'], 'L1_gnn_bq': _L1_gnn_in['bq'], 'L1_gnn_Wk': _L1_gnn_in['Wk'], 'L1_gnn_bk': _L1_gnn_in['bk'], 'L1_gnn_Wv': _L1_gnn_in['Wv'], 'L1_gnn_bv': _L1_gnn_in['bv'], 'L1_gnn_Wo': _L1_gnn_in['Wo'], 'L1_gnn_bo': _L1_gnn_in['bo'], 'L1_gnn_W1': _L1_gnn_in['W1'], 'L1_gnn_b1': _L1_gnn_in['b1'], 'L1_gnn_W2': _L1_gnn_in['W2'], 'L1_gnn_b2': _L1_gnn_in['b2'], 'L1_gnn_bn1_g': _L1_gnn_in['bn1_g'], 'L1_gnn_bn1_b': _L1_gnn_in['bn1_b'], 'L1_gnn_bn2_g': _L1_gnn_in['bn2_g'], 'L1_gnn_bn2_b': _L1_gnn_in['bn2_b']}

def reference(x, src, dst, L0_gnn_W0_self, L0_gnn_W0_neigh, L0_gnn_b0, L0_gnn_W1_self, L0_gnn_W1_neigh, L0_gnn_b1, L0_gnn_W2_self, L0_gnn_W2_neigh, L0_gnn_b2, L1_gnn_Wq, L1_gnn_bq, L1_gnn_Wk, L1_gnn_bk, L1_gnn_Wv, L1_gnn_bv, L1_gnn_Wo, L1_gnn_bo, L1_gnn_W1, L1_gnn_b1, L1_gnn_W2, L1_gnn_b2, L1_gnn_bn1_g, L1_gnn_bn1_b, L1_gnn_bn2_g, L1_gnn_bn2_b):
    import jax
    import jax.numpy as jnp

    def _L0_gnn_ref(features, src, dst, W0_self, W0_neigh, b0, W1_self, W1_neigh, b1, W2_self, W2_neigh, b2):
        import jax, jax.numpy as jnp
        import numpy as np
        N_NODES = 6250
        N_EDGES = 100000
        D = 256

        def _sage_layer(x, src, dst, inv_deg, W_self, W_neigh, b):
            agg = jax.ops.segment_sum(x[src], dst, num_segments=N_NODES)
            mean = agg * inv_deg[:, None]
            return x @ W_self + mean @ W_neigh + b
        deg = jax.ops.segment_sum(jnp.ones_like(src, dtype=features.dtype), dst, num_segments=N_NODES)
        inv_deg = 1.0 / jnp.maximum(deg, 1.0)
        h = _sage_layer(features, src, dst, inv_deg, W0_self, W0_neigh, b0)
        h = jax.nn.relu(h)
        h = _sage_layer(h, src, dst, inv_deg, W1_self, W1_neigh, b1)
        h = jax.nn.relu(h)
        h = _sage_layer(h, src, dst, inv_deg, W2_self, W2_neigh, b2)
        return h

    def _L1_gnn_ref(x, edge_index, Wq, bq, Wk, bk, Wv, bv, Wo, bo, W1, b1, W2, b2, bn1_g, bn1_b, bn2_g, bn2_b):
        import jax, jax.numpy as jnp
        import numpy as np
        N_NODES = 3125
        N_EDGES = 50000
        D_MODEL = 256
        NUM_HEADS = 8
        HEAD_DIM = D_MODEL // NUM_HEADS
        D_FF = 2 * D_MODEL
        NEG_SLOPE = 0.2
        BN_EPS = 1e-05

        def _batch_norm(h, g, b):
            mean = jnp.mean(h, axis=0)
            var = jnp.mean((h - mean) ** 2, axis=0)
            return (h - mean) * jax.lax.rsqrt(var + BN_EPS) * g + b
        N = x.shape[0]
        Qh = (x @ Wq + bq).reshape(N, NUM_HEADS, HEAD_DIM)
        Kh = (x @ Wk + bk).reshape(N, NUM_HEADS, HEAD_DIM)
        Vh = (x @ Wv + bv).reshape(N, NUM_HEADS, HEAD_DIM)
        s = jnp.einsum('nhc,nhc->nh', Qh, Kh) / jnp.sqrt(jnp.float32(HEAD_DIM))
        loops = jnp.arange(N, dtype=edge_index.dtype)
        src = jnp.concatenate([edge_index[0], loops])
        dst = jnp.concatenate([edge_index[1], loops])
        alpha = jax.nn.leaky_relu(s[src] + s[dst], NEG_SLOPE)
        m = jax.ops.segment_max(alpha, dst, num_segments=N)
        e = jnp.exp(alpha - m[dst])
        denom = jax.ops.segment_sum(e, dst, num_segments=N)
        a = e / denom[dst]
        msg = Vh[src] * a[:, :, None]
        attn = jax.ops.segment_sum(msg, dst, num_segments=N).reshape(N, D_MODEL)
        h = attn @ Wo + bo
        h = x + h
        h = _batch_norm(h, bn1_g, bn1_b)
        h2 = jax.nn.relu(h @ W1 + b1) @ W2 + b2
        h = _batch_norm(h + h2, bn2_g, bn2_b)
        return h
    edge_index = jnp.stack([src, dst])
    h = jnp.maximum(_layernorm(x, axis=-1), 0.0)
    x = x + _L0_gnn_ref(h, src, dst, L0_gnn_W0_self, L0_gnn_W0_neigh, L0_gnn_b0, L0_gnn_W1_self, L0_gnn_W1_neigh, L0_gnn_b1, L0_gnn_W2_self, L0_gnn_W2_neigh, L0_gnn_b2)
    h = jnp.maximum(_layernorm(x, axis=-1), 0.0)
    x = x + _L1_gnn_ref(h, edge_index, L1_gnn_Wq, L1_gnn_bq, L1_gnn_Wk, L1_gnn_bk, L1_gnn_Wv, L1_gnn_bv, L1_gnn_Wo, L1_gnn_bo, L1_gnn_W1, L1_gnn_b1, L1_gnn_W2, L1_gnn_b2, L1_gnn_bn1_g, L1_gnn_bn1_b, L1_gnn_bn2_g, L1_gnn_bn2_b)
    return x

_drawn_inputs = setup_inputs


def setup_inputs(seed=0):
    import zlib

    import numpy as np

    out = dict(_drawn_inputs(seed))
    spreads = {'L0_gnn_b0': (0.0, 0.1),
     'L0_gnn_b1': (0.0, 0.1),
     'L0_gnn_b2': (0.0, 0.1),
     'L1_gnn_bq': (0.0, 0.8),
     'L1_gnn_bk': (0.0, 0.8),
     'L1_gnn_bv': (0.0, 0.8),
     'L1_gnn_bo': (0.0, 0.8),
     'L1_gnn_b1': (0.0, 0.579),
     'L1_gnn_b2': (0.0, 0.8),
     'L1_gnn_bn1_g': (1.0, 0.2),
     'L1_gnn_bn1_b': (0.0, 0.8),
     'L1_gnn_bn2_g': (1.0, 0.2),
     'L1_gnn_bn2_b': (0.0, 0.1)}
    factors = {'L1_gnn_Wq': 8.0, 'L1_gnn_Wk': 8.0}
    for name, (base, spread) in spreads.items():
        noise = np.random.default_rng([zlib.crc32(name.encode()), seed]).standard_normal(out[name].shape)
        drawn = base * np.exp(spread * noise) if base else spread * noise
        out[name] = jnp.asarray(drawn.astype(out[name].dtype))
    for name, factor in factors.items():
        out[name] = (out[name] * factor).astype(out[name].dtype)
    return out
```

```python
from contextlib import ExitStack

import concourse.bass as bass
from concourse import mybir

P = 128
ALU = mybir.AluOpType
ACT = mybir.ActivationFunctionType
AX = mybir.AxisListType
F32 = mybir.dt.float32
BF16 = mybir.dt.bfloat16
I32 = mybir.dt.int32

BIG = 1.0e30
EPS = 1e-5
SLOPE = 0.2
HEADS = 8
BJ = 4
BE = P * BJ
SLOTS = 7
AHEAD = 4
CHUNKS = 14


def gnn_kernel(nc, x, src, dst, sage_w, sage_b, Wq, bq, Wk, bk, Wv, bv, Wo, bo, W1, b1, W2, b2,
               bn1_g, bn1_b, bn2_g, bn2_b, out):
    N, D = x.shape
    E = src.shape[0]
    DF = W1.shape[1]
    C = D // HEADS
    KD, KF = D // P, DF // P
    NT = -(-N // P)
    NP = NT * P
    NL = N - (NT - 1) * P
    NB = -(-E // BE)
    EP = NB * BE
    VS = D + HEADS
    AUX = 2 * HEADS + 1
    CB = NB // CHUNKS
    CE = CB * BE
    CP = CHUNKS * HEADS
    COLS = NB * BJ
    ROUNDS = NB // SLOTS
    assert NB % SLOTS == 0 and NB % CHUNKS == 0 and KD == 2 and CP <= P

    def dram(name, shape, dt=F32):
        return nc.dram_tensor(name, shape, dt, kind="Internal").ap()

    x_pad = dram("x_pad", (NT, P, D))
    tables = [dram(f"h_table{i}", (NP, D)) for i in range(3)]
    x1_dram = dram("x1_dram", (NT, P, D))
    hln_dram = dram("hln_dram", (NT, P, D))
    vs_table = dram("vs_table", (NP, VS))
    v_edges = dram("v_edges", (NB, P, BJ * D))
    dst_ext = dram("dst_ext", (1, EP + 2), I32)
    src_ext = dram("src_ext", (1, EP), I32)

    with ExitStack() as ctx:
        def sb(name, shape, dt=F32):
            return ctx.enter_context(nc.sbuf_tensor(name, shape, dt))

        def ps(name, shape):
            return ctx.enter_context(nc.psum_tensor(name, shape, F32))

        def sem(name):
            return ctx.enter_context(nc.semaphore(name))

        hN_words, ring_words = NT * D, SLOTS * BJ * VS
        T = CE + 2
        arena_words = 4 * T + T // 2 + 2 * COLS * HEADS
        arena = sb("arena", [P, arena_words])
        o_late = 2 * T
        h_nodes = arena[:, 0:hN_words].rearrange("p (t d) -> p t d", d=D)
        o_ring = hN_words
        ring = arena[:, o_ring:o_ring + ring_words].rearrange("p (s w) -> p s w", w=VS)
        o_w = o_ring + ring_words
        w_sage = arena[:, o_w:o_w + 3 * 2 * KD * D].rearrange("p (l k d) -> p l k d", l=3, k=2 * KD)
        o_q = o_w + 3 * 2 * KD * D
        w_qkv = arena[:, o_q:o_q + KD * 3 * D].rearrange("p (k d) -> p k d", k=KD)
        x_rows_o = o_q + KD * 3 * D
        dst_b = arena[:, 0:SLOTS * BE].bitcast(I32).rearrange("p (s e) -> p s e", e=BE)
        alpha_t = arena[0:CP, 0:CE]
        fwd_t = arena[0:CP, T:T + CE]
        bwd_t = arena[0:CP, 2 * T:2 * T + CE]
        dst_t = arena[0:CP, 3 * T:4 * T].bitcast(I32)
        keep_t = arena[0:CP, 4 * T:4 * T + T // 2].bitcast(BF16)
        alpha_k = arena[:, T:T + COLS * HEADS].rearrange("p (k q) -> p k q", q=CP)
        max_e = arena[:, 2 * T:2 * T + COLS * HEADS].rearrange("p (k h) -> p k h", h=HEADS)
        o_se = 4 * T + T // 2
        s_src = arena[:, o_se:o_se + COLS * HEADS].rearrange("p (k h) -> p k h", h=HEADS)
        s_dst = arena[:, o_se + COLS * HEADS:o_se + 2 * COLS * HEADS].rearrange("p (k h) -> p k h", h=HEADS)
        aux_e = arena[:, 0:COLS * AUX].rearrange("p (k a) -> p k a", a=AUX)
        assert COLS * AUX <= 2 * T and x_rows_o + 7 * D <= o_se and ring_words <= 2 * COLS * HEADS
        h_cols = arena[:, o_late:o_late + hN_words].rearrange("p (t f n) -> p t f n", f=KD, n=P)
        v_ring = arena[:, o_se:o_se + SLOTS * BJ * D].rearrange("p (s w) -> p s w", w=D)
        assert o_late + hN_words <= o_se

        o_late_w = o_se + SLOTS * BJ * D
        w_o = arena[:, o_late_w:o_late_w + KD * D].rearrange("p (k d) -> p k d", k=KD)
        w_1 = arena[:, o_late_w + KD * D:o_late_w + KD * (D + DF)].rearrange("p (k d) -> p k d", k=KD)
        w_2 = arena[:, o_late_w + KD * (D + DF):o_late_w + KD * (D + DF) + KF * D].rearrange("p (k d) -> p k d", k=KF)
        assert o_late_w + KD * (D + DF) + KF * D <= arena_words
        b_sage = sb("b_sage", [1, 3, D])
        b_qkv = arena[:, x_rows_o:x_rows_o + 3 * D]
        cols = sb("cols", [P, 5 * KD + KF + KD])
        ident = sb("ident", [P, P])
        iota_n = sb("iota_n", [P, P])
        part = sb("part", [P, 1])
        tile_base = sb("tile_base", [P, NT])
        node_id = sb("node_id", [P, NT])
        iota_t = sb("iota_t", [P, P])
        zero_l = sb("zero_l", [P, P], BF16)
        zero_r = sb("zero_r", [P, VS], BF16)
        ones_row = sb("ones_row", [1, P])
        src_e = sb("src_e", [P, COLS + SLOTS * BJ], I32)
        dst_i = sb("dst_i", [P, COLS], I32)
        dst_e = sb("dst_e", [P, COLS])
        idx = sb("idx", [P, 2, SLOTS * BJ], I32)
        onehot = sb("onehot", [P, BJ, P])
        s_node = sb("s_node", [P, NT, HEADS])
        tile_block = sb("tile_block", [1, NT + 1], I32)
        need = sb("need", [1, NB + SLOTS], I32)
        n_row = NT + 1 + NB + SLOTS
        row_f = arena[0:1, hN_words - n_row:hN_words]
        tiles3 = sb("tiles3", [P, 3 * D])
        mean, h_self, x_tile = (tiles3[:, i * D:(i + 1) * D] for i in range(3))
        lhs = sb("lhs", [P, 2 * KD, P])
        qk = sb("qk", [P, 2 * D])
        vs_tile = sb("vs_tile", [P, VS])
        small = sb("small", [P, 64])
        bn6 = sb("bn6", [P, KD, NT, 6])
        bn2 = sb("bn2", [P, NT, 2])
        rstd = sb("rstd", [P, NT])
        shift = sb("shift", [P, NT])
        f1 = onehot[:]
        hb = qk[:, 0:D].rearrange("p (k n) -> p k n", k=KD)
        assert KF == BJ
        crow = tiles3[0:1, 0:6 * CP].rearrange("a (k q) -> a k q", k=6)
        ccol = sb("ccol", [P, 8])

        agg = ps("agg", [P, 512])
        tp = ps("tp", [P, 2 * KD, P])
        dense = ps("dense", [P, 512])
        dense2 = ps("dense2", [P, 512])
        aux_ps = ps("aux_ps", [P, 512])

        col_of, at = {}, 0
        for name, v, k in (("bo", bo, KD), ("g1", bn1_g, KD), ("b1n", bn1_b, KD), ("g2", bn2_g, KD),
                           ("b2n", bn2_b, KD), ("b2", b2, KD), ("b1", b1, KF)):
            col_of[name] = (at, k, v)
            at += k

        def col(name, k):
            return cols[:, col_of[name][0] + k:col_of[name][0] + k + 1]

        const_in = sem("const_in")
        ext_in = sem("ext_in")
        edges_in = sem("edges_in")
        pads_made = sem("pads_made")
        passed = sem("passed")
        consts_made = sem("consts_made")
        ident_made = sem("ident_made")
        walk_made = sem("walk_made")
        WALK = 9
        block = ctx.enter_context(nc.Block())
        def wait(eng, semaphore, value):
            if not isinstance(value, int) or value > 0:
                eng.wait_ge(semaphore, value)

        def first_and_rest(eng, n, body):
            body(0)
            with eng.Fori(1, n) as t:
                body(t)

        def apart(eng):
            eng.sem_inc(passed, 1)

        setup_dmas = []
        for l in range(3):
            for m in range(2):
                setup_dmas.append((w_sage[:, l, m * KD:(m + 1) * KD, :], sage_w[l][m].rearrange("(k p) n -> p k n", p=P)))
            setup_dmas.append((b_sage[0:1, l, :], sage_b[l].rearrange("(a d) -> a d", a=1)))
        for i, (w, b) in enumerate(((Wq, bq), (Wk, bk), (Wv, bv))):
            setup_dmas.append((w_qkv[:, :, i * D:(i + 1) * D], w.rearrange("(k p) n -> p k n", p=P)))
            setup_dmas.append((b_qkv[:, i * D:(i + 1) * D], b.rearrange("(a d) -> a d", a=1).broadcast_to([P, D])))
        for name, (at, k, v) in col_of.items():
            for i in range(k):
                setup_dmas.append((cols[:, at + i:at + i + 1], v[i * P:(i + 1) * P].rearrange("(p a) -> p a", a=1)))
        CONSTS = 16 * len(setup_dmas)

        def setup_sync(sp):
            sp.dma_start(dst_ext[0:1, 1:1 + E].rearrange("a (r c) -> (a r) c", r=32),
                         dst.rearrange("(r c) -> r c", r=32)).then_inc(ext_in, 16)
            sp.dma_start(src_ext[0:1, 0:E].rearrange("a (r c) -> (a r) c", r=32),
                         src.rearrange("(r c) -> r c", r=32)).then_inc(ext_in, 16)
            sp.wait_ge(pads_made, 3)
            sp.dma_start(dst_ext[0:1, 0:1], dst_b[0:1, 1, 0:1]).then_inc(ext_in, 16)
            sp.dma_start(dst_ext[0:1, 1 + EP:2 + EP], dst_b[0:1, 1, 0:1]).then_inc(ext_in, 16)
            sp.dma_start(dst_ext[0:1, 1 + E:1 + EP], dst_b[0:1, 0, 0:EP - E]).then_inc(ext_in, 16)
            sp.dma_start(src_ext[0:1, E:EP], dst_b[0:1, 2, 0:EP - E]).then_inc(ext_in, 16)
            sp.wait_ge(ext_in, 16 * 6)
            sp.dma_start(dst_i[:].rearrange("p (b j) -> p b j", j=BJ),
                         dst_ext[0:1, 1:1 + EP].rearrange("a (b p j) -> (a p) b j", p=P, j=BJ)).then_inc(edges_in, 16)
            sp.dma_start(src_e[:, 0:COLS].rearrange("p (b j) -> p b j", j=BJ),
                         src_ext[0:1, :].rearrange("a (b p j) -> (a p) b j", p=P, j=BJ)).then_inc(edges_in, 16)

        def setup_scalar(act):
            for to, of in setup_dmas:
                act.dma_start(to, of).then_inc(const_in, 16)

        def setup_gpsimd(pool):
            pool.memset(dst_b[0:1, 0, :], NP).then_inc(pads_made, 1)
            pool.memset(dst_b[0:1, 1, :], -1).then_inc(pads_made, 1)
            pool.memset(dst_b[0:1, 2, :], 0).then_inc(pads_made, 1)
            pool.iota(iota_n[:], [[1, P]], 0, 0, allow_small_or_imprecise_dtypes=True).then_inc(consts_made, 1)
            pool.iota(part[:], [[0, 1]], 0, 1, allow_small_or_imprecise_dtypes=True).then_inc(consts_made, 1)
            pool.iota(tile_base[:], [[P, NT]], 0, 0, allow_small_or_imprecise_dtypes=True).then_inc(consts_made, 1)
            pool.iota(node_id[:], [[P, NT]], 0, 1, allow_small_or_imprecise_dtypes=True).then_inc(consts_made, 1)
            pool.memset(zero_l[:], 0.0).then_inc(consts_made, 1)
            pool.memset(zero_r[:], 0.0).then_inc(consts_made, 1)
            pool.memset(src_e[:, COLS:], 0).then_inc(consts_made, 1)
            pool.memset(ones_row[:], 1.0).then_inc(consts_made, 1)
            pool.memset(ring[:, :, D:D + 1], 1.0).then_inc(consts_made, 1)
            pool.iota(row_f[0:1, 0:NT + 1], [[P, NT + 1]], 0, 0, allow_small_or_imprecise_dtypes=True).then_inc(consts_made, 1)
            pool.iota(row_f[0:1, NT + 1:], [[1, NB + SLOTS]], -SLOTS, 0, allow_small_or_imprecise_dtypes=True).then_inc(consts_made, 1)
        NCONST = 11

        def setup_vector(dve):
            dve.wait_ge(consts_made, NCONST)
            dve.tensor_scalar(ident[:], iota_n[:], part[:, 0:1], None, ALU.is_equal).then_inc(ident_made, 1)
            dve.wait_ge(edges_in, 32)
            step = [0]

            def link(ins):
                step[0] += 1
                ins.then_inc(walk_made, 1)
                dve.wait_ge(walk_made, step[0])

            link(dve.tensor_copy(dst_e[:], dst_i[:]))
            cmp = arena[0:1, 0:(NT + 1) * NB].rearrange("a (t b) -> a t b", b=NB)
            firsts = dst_e[0:1, 0:COLS:BJ].rearrange("a (o b) -> a o b", o=1).broadcast_to([1, NT + 1, NB])
            starts = row_f[0:1, 0:NT + 1].rearrange("a (t o) -> a t o", o=1).broadcast_to([1, NT + 1, NB])
            link(dve.tensor_tensor(cmp, firsts, starts, ALU.is_lt))
            cnt = small[0:1, 0:NT + 1]
            link(dve.tensor_reduce(cnt, cmp, AX.X, ALU.add))
            link(dve.tensor_scalar(cnt, cnt, -1.0, 0.0, ALU.add, ALU.max))
            link(dve.tensor_copy(tile_block[:], cnt))
            NI = NB + SLOTS
            cmp2 = arena[0:1, 0:NI * NT].rearrange("a (b t) -> a b t", t=NT)
            blocks_row = row_f[0:1, NT + 1:]
            b_b = blocks_row.rearrange("a (b o) -> a b o", o=1).broadcast_to([1, NI, NT])
            t_b = cnt[0:1, 0:NT].rearrange("a (o t) -> a o t", o=1).broadcast_to([1, NI, NT])
            link(dve.tensor_tensor(cmp2, t_b, b_b, ALU.is_le))
            cnt2 = arena[0:1, NI * NT:NI * NT + NI]
            link(dve.tensor_reduce(cnt2, cmp2, AX.X, ALU.add))
            link(dve.tensor_tensor(cnt2, cnt2, blocks_row, ALU.add))
            link(dve.tensor_scalar(cnt2, cnt2, float(BJ), float(BJ), ALU.mult, ALU.add))
            assert step[0] == WALK
            dve.tensor_scalar(need[:], cnt2, float(BJ), None, ALU.max).then_inc(walk_made, 1)

        WALKED = WALK + 1

        ln_loaded = sem("ln_loaded")
        ln_stats = sem("ln_stats")
        ln_aggr = sem("ln_aggr")
        ln_var = sem("ln_var")
        ln_sqrt = sem("ln_sqrt")
        ln_fold = sem("ln_fold")
        ln_done = sem("ln_done")
        x_padded = sem("x_padded")
        pad_zero = sem("pad_zero")
        stored0 = sem("stored0")
        G = 7

        def norm_x_sync(sp):
            sp.wait_ge(walk_made, WALKED)
            xt = x[0:(NT - 1) * P, :].rearrange("(t p) d -> p t d", p=P)
            for g in range(0, NT - 1, 12):
                sp.dma_start(h_nodes[:, g:g + 12, :], xt[:, g:g + 12, :]).then_inc(ln_loaded, 16)
            sp.wait_ge(pad_zero, 1)
            sp.dma_start(h_nodes[0:NL, NT - 1, :], x[(NT - 1) * P:N, :]).then_inc(ln_loaded, 16)
            sp.wait_ge(ln_loaded, 16 * ((NT - 1) // 12 + 1))
            sp.dma_start(x_pad.rearrange("t p d -> p t d"), h_nodes[:, :, :]).then_inc(x_padded, 16)

        def rstd_and_shift(dve, var_sem, sqrt_sem, fold_sem):
            dve.tensor_scalar(rstd[:], bn2[:, :, 1], EPS, None, ALU.add).then_inc(var_sem, 1)
            dve.wait_ge(sqrt_sem, 1)
            dve.reciprocal(rstd[:], rstd[:]).then_inc(fold_sem, 1)
            dve.wait_ge(fold_sem, 1)
            dve.scalar_tensor_tensor(shift[:], bn2[:, :, 0], -1.0, rstd[:], ALU.mult, ALU.mult).then_inc(fold_sem, 1)

        def norm_x_vector(dve):
            dve.wait_ge(walk_made, WALKED)
            dve.memset(h_nodes[:, NT - 1, :], 0.0).then_inc(pad_zero, 1)
            dve.wait_ge(ln_loaded, 16 * ((NT - 1) // 12 + 1))
            with dve.Fori(0, NT) as t:
                dve.bn_stats(bn6[:, 0, t, :], h_nodes[:, t, :]).then_inc(ln_stats, 1)
            dve.wait_ge(ln_stats, NT)
            for t in range(NT):
                dve.bn_aggr(bn2[:, t, :], bn6[:, 0, t, :]).then_inc(ln_aggr, 1)
            dve.wait_ge(ln_aggr, NT)
            rstd_and_shift(dve, ln_var, ln_sqrt, ln_fold)

        def norm_x_scalar(act):
            act.wait_ge(ln_var, 1)
            act.activation(rstd[:], rstd[:], ACT.Sqrt).then_inc(ln_sqrt, 1)
            act.wait_ge(ln_fold, 2)
            act.wait_ge(x_padded, 16)
            with act.Fori(0, NT) as t:
                act.activation(h_nodes[:, t, :], h_nodes[:, t, :], ACT.Relu,
                               bias=shift[:, bass.ds(t, 1)], scale=rstd[:, bass.ds(t, 1)]).then_inc(ln_done, 1)
                act.wait_ge(ln_done, t + 1)
                act.dma_start(tables[0].rearrange("(t p) d -> t p d", p=P)[t], h_nodes[:, t, :]).then_inc(stored0, 16)

        PAIRS = NB + NT - 1
        TOTAL = dict(staged=ROUNDS + 1, slots_free=AHEAD + NB, rows_ready=NB, onehot_used=BJ * PAIRS,
                     onehot_made=BJ * PAIRS, base_moved=NT, agg_done=NT, deg=2 * NT, mean_made=NT, self_made=NT,
                     turned=NT, lhs_made=NT, out_done=NT, h_made=NT, stored=16 * NT, landed=16 * BJ * ROUNDS)
        W = {n: sem(n) for n in TOTAL if n != "landed"}
        landed = [sem(f"landed{s}") for s in range(SLOTS)]
        x_in = sem("x_in")
        x1_stats = sem("x1_stats")

        def since(name, w, v):
            return v + w * TOTAL[name]

        def gathers(pool, w, table, width, may_fill):
            IR = SLOTS * BJ

            def stage_indices(first, half):
                pool.tensor_copy(idx[:, half, :], src_e[:, bass.ds(first, IR)]).then_inc(W["staged"], 1)
            if w:
                pool.wait_ge(W["staged"], since("staged", w, 0))
            stage_indices(0, 0)
            def rounds(i2):
                for half in range(2):
                    i = i2 * 2 + half
                    pool.wait_ge(W["staged"], since("staged", w, i + 1))
                    for s in range(SLOTS):
                        may_fill(i, s)
                        apart(pool)
                        for j in range(BJ):
                            k = s * BJ + j
                            pool.indirect_dma_start(ring[:, k, 0:width], None, table,
                                                    bass.IndirectOffsetOnAxis(idx[:, half, k:k + 1], 0)).then_inc(landed[s], 16)
                    stage_indices((i + 1) * IR, 1 - half)
            first_and_rest(pool, ROUNDS // 2, rounds)

        def pairs_of(eng, i):
            return eng.value_load(need[0:1, bass.ds(i, 1)], min_val=0, max_val=BJ * (NB + NT + 1))

        def relay(sp, w):
            sp.sem_inc(W["slots_free"], AHEAD)
            with sp.Fori(0, ROUNDS) as i:
                for s in range(SLOTS):
                    sp.wait_ge(W["onehot_used"], since("onehot_used", w, pairs_of(sp, i * SLOTS + s + AHEAD)))
                    sp.sem_inc(W["slots_free"], 1)
                    sp.wait_ge(landed[s], since("landed", w, (i + 1) * (16 * BJ)))
                    sp.sem_inc(W["rows_ready"], 1)

        def span(eng, t):
            b0 = eng.value_load(tile_block[0:1, bass.ds(t, 1)], min_val=0, max_val=NB - 1)
            b1 = eng.value_load(tile_block[0:1, bass.ds(t + 1, 1)], min_val=0, max_val=NB - 1)
            return b0, b1

        def onehots(dve, w, t):
            dve.tensor_scalar(iota_t[:], iota_n[:], tile_base[:, bass.ds(t, 1)], None, ALU.add).then_inc(W["base_moved"], 1)
            dve.wait_ge(W["base_moved"], since("base_moved", min(w, 3), t + 1))
            b0, b1 = span(dve, t)
            with dve.Fori(b0, b1 + 1) as b:
                for j in range(BJ):
                    dve.wait_ge(W["onehot_used"], since("onehot_used", w, (b + t) * BJ + j + 1))
                    dve.tensor_scalar(onehot[:, j, :], iota_t[:], dst_e[:, bass.ds(b * BJ + j, 1)], None,
                                      ALU.is_equal).then_inc(W["onehot_made"], 1)

        def sage_gpsimd(pool, l):
            pool.wait_ge(*((stored0, 16 * NT) if l == 0 else (W["stored"], l * TOTAL["stored"])))
            pool.wait_ge(consts_made, NCONST)

            def may_fill(i, s):
                pool.wait_ge(W["slots_free"], since("slots_free", l, i * SLOTS + s + 1))
            gathers(pool, l, tables[l], D, may_fill)

        def sage_sync(sp, l):
            relay(sp, l)

        def sage_tensor(pe, l):
            if l == 0:
                pe.wait_ge(walk_made, WALKED)
                pe.wait_ge(ident_made, 1)
                pe.wait_ge(consts_made, NCONST)
                pe.wait_ge(const_in, CONSTS)
                pe.sem_inc(W["onehot_used"], BJ)
            def tile(t):
                b0, b1 = span(pe, t)
                wait(pe, W["mean_made"], since("mean_made", l, t))
                pe.matmul(agg[:, 0:D + 1], zero_l[:], zero_r[:, 0:D + 1], start=True, stop=False)
                with pe.Fori(b0, b1 + 1) as b:
                    pe.wait_ge(W["rows_ready"], since("rows_ready", l, b + 1))
                    for j in range(BJ):
                        pe.wait_ge(W["onehot_made"], since("onehot_made", l, (b + t) * BJ + j + 1))
                        pe.matmul(agg[:, 0:D + 1], onehot[:, j, :], ring[:, (b % SLOTS) * BJ + j, 0:D + 1],
                                  start=False, stop=False).then_inc(W["onehot_used"], 1)
                pe.matmul(agg[:, 0:D + 1], zero_l[:], zero_r[:, 0:D + 1], start=False, stop=True).then_inc(W["agg_done"], 1)
                wait(pe, W["lhs_made"], since("lhs_made", l, t))
                pe.wait_ge(W["self_made"], since("self_made", l, t + 1))
                for k in range(KD):
                    pe.transpose(tp[:, KD + k, :], h_self[:, k * P:(k + 1) * P], ident[:])
                pe.wait_ge(W["mean_made"], since("mean_made", l, t + 1))
                for k in range(KD):
                    last = pe.transpose(tp[:, k, :], mean[:, k * P:(k + 1) * P], ident[:])
                last.then_inc(W["turned"], 1)
                wait(pe, W["h_made"], since("h_made", l, t))
                pe.matmul(dense[:, 0:D], ones_row[:], b_sage[0:1, l, :], start=True, stop=False)
                pe.wait_ge(W["lhs_made"], since("lhs_made", l, t + 1))
                for k in range(2 * KD):
                    last = pe.matmul(dense[:, 0:D], lhs[:, k, :], w_sage[:, l, k, :], start=False, stop=k == 2 * KD - 1)
                last.then_inc(W["out_done"], 1)
            first_and_rest(pe, NT, tile)

        def sage_vector(dve, l):
            def tile(t):
                onehots(dve, l, t)
                dve.wait_ge(W["agg_done"], since("agg_done", l, t + 1))
                dve.tensor_scalar(small[:, 0:1], agg[:, D:D + 1], 1.0, None, ALU.max).then_inc(W["deg"], 1)
                dve.wait_ge(W["deg"], since("deg", l, 2 * t + 1))
                dve.reciprocal(small[:, 1:2], small[:, 0:1]).then_inc(W["deg"], 1)
                dve.wait_ge(W["deg"], since("deg", l, 2 * t + 2))
                wait(dve, W["turned"], since("turned", l, t))
                dve.tensor_scalar(mean[:], agg[:, 0:D], small[:, 1:2], None, ALU.mult).then_inc(W["mean_made"], 1)
                if l == 2:
                    dve.wait_ge(x_in, 16 * t + 16)
                    dve.wait_ge(W["out_done"], since("out_done", l, t + 1))
                    dve.tensor_tensor(h_nodes[:, t, :], dense[:, 0:D], x_tile[:], ALU.add).then_inc(W["h_made"], 1)
                    dve.wait_ge(W["h_made"], since("h_made", l, t + 1))
                    dve.bn_stats(bn6[:, 0, t, :], h_nodes[:, t, :]).then_inc(x1_stats, 1)
            first_and_rest(dve, NT, tile)

        def sage_scalar(act, l):
            def tile(t):
                wait(act, W["turned"], since("turned", l, t))
                act.activation(h_self[:], h_nodes[:, t, :], ACT.Copy).then_inc(W["self_made"], 1)
                if l == 2:
                    wait(act, W["h_made"], since("h_made", l, t))
                    act.dma_start(x_tile[:], x_pad[t]).then_inc(x_in, 16)
                act.wait_ge(W["turned"], since("turned", l, t + 1))
                wait(act, W["out_done"], since("out_done", l, t))
                act.activation(lhs[:], tp[:], ACT.Copy).then_inc(W["lhs_made"], 1)
                act.wait_ge(W["out_done"], since("out_done", l, t + 1))
                if l < 2:
                    apart(act)
                    act.activation(h_nodes[:, t, :], dense[:, 0:D], ACT.Relu).then_inc(W["h_made"], 1)
                act.wait_ge(W["h_made"], since("h_made", l, t + 1))
                to = tables[l + 1].rearrange("(t p) d -> t p d", p=P)[t] if l < 2 else x1_dram[t]
                act.dma_start(to, h_nodes[:, t, :]).then_inc(W["stored"], 16)
            first_and_rest(act, NT, tile)


        Q = {n: sem(f"q_{n}") for n in ("aggr", "var", "sqrt", "fold", "h_made", "turned", "lhs_made", "out_done",
                                        "taken", "step", "s_made", "hln_out", "vs_out")}

        def project_vector(dve):
            dve.wait_ge(x1_stats, NT)
            for t in range(NT):
                dve.bn_aggr(bn2[:, t, :], bn6[:, 0, t, :]).then_inc(Q["aggr"], 1)
            dve.wait_ge(Q["aggr"], NT)
            rstd_and_shift(dve, Q["var"], Q["sqrt"], Q["fold"])
            def tile(t):
                dve.wait_ge(Q["out_done"], t + 1)
                dve.tensor_tensor(qk[:], dense[:], b_qkv[:, 0:2 * D], ALU.add).then_inc(Q["step"], 1)
                wait(dve, Q["vs_out"], 16 * t)
                dve.tensor_tensor(vs_tile[:, 0:D], dense2[:, 0:D], b_qkv[:, 2 * D:3 * D], ALU.add).then_inc(Q["taken"], 1)
                dve.wait_ge(Q["step"], t * 4 + 1)
                dve.tensor_tensor(qk[:, 0:D], qk[:, 0:D], qk[:, D:2 * D], ALU.mult).then_inc(Q["step"], 1)
                dve.wait_ge(Q["step"], t * 4 + 2)
                dve.tensor_reduce(small[:, 8:8 + HEADS], qk[:, 0:D].rearrange("p (h c) -> p h c", h=HEADS), AX.X,
                                  ALU.add).then_inc(Q["step"], 1)
                dve.wait_ge(Q["step"], t * 4 + 3)
                dve.tensor_scalar(s_node[:, t, :], small[:, 8:8 + HEADS], float(C) ** -0.5, None, ALU.mult).then_inc(Q["step"], 1)
                dve.wait_ge(Q["step"], t * 4 + 4)
                apart(dve)
                dve.tensor_copy(vs_tile[:, D:VS], s_node[:, t, :]).then_inc(Q["s_made"], 1)
            first_and_rest(dve, NT, tile)

        def project_scalar(act):
            act.wait_ge(Q["var"], 1)
            act.activation(rstd[:], rstd[:], ACT.Sqrt).then_inc(Q["sqrt"], 1)
            act.wait_ge(Q["fold"], 2)
            def tile(t):
                wait(act, Q["turned"], t)
                wait(act, Q["hln_out"], 16 * t)
                act.activation(h_self[:], h_nodes[:, t, :], ACT.Relu, bias=shift[:, bass.ds(t, 1)],
                               scale=rstd[:, bass.ds(t, 1)]).then_inc(Q["h_made"], 1)
                act.wait_ge(Q["h_made"], t + 1)
                act.dma_start(hln_dram[t], h_self[:]).then_inc(Q["hln_out"], 16)
                act.wait_ge(Q["turned"], t + 1)
                wait(act, Q["out_done"], t)
                act.activation(lhs[:, 0:KD, :], tp[:, 0:KD, :], ACT.Copy).then_inc(Q["lhs_made"], 1)
            first_and_rest(act, NT, tile)
            act.wait_ge(Q["hln_out"], 16 * NT)

        def project_sync(sp):
            with sp.Fori(0, NT) as t:
                sp.wait_ge(Q["s_made"], t + 1)
                sp.dma_start(vs_table.rearrange("(t p) d -> t p d", p=P)[t], vs_tile[:]).then_inc(Q["vs_out"], 16)

        def project_tensor(pe):
            def tile(t):
                pe.wait_ge(Q["h_made"], t + 1)
                wait(pe, Q["lhs_made"], t)
                for k in range(KD):
                    last = pe.transpose(tp[:, k, :], h_self[:, k * P:(k + 1) * P], ident[:])
                last.then_inc(Q["turned"], 1)
                pe.wait_ge(Q["lhs_made"], t + 1)
                wait(pe, Q["taken"], t)
                for k in range(KD):
                    pe.matmul(dense[:], lhs[:, k, :], w_qkv[:, k, 0:2 * D], start=k == 0, stop=k == KD - 1)
                for k in range(KD):
                    last = pe.matmul(dense2[:, 0:D], lhs[:, k, :], w_qkv[:, k, 2 * D:3 * D], start=k == 0, stop=k == KD - 1)
                last.then_inc(Q["out_done"], 1)
            first_and_rest(pe, NT, tile)

        A = {n: sem(f"a_{n}") for n in ("s_taken", "zeroed", "sd_added",
                                        "node_made", "dst_ready")}
        a_stored = [sem(f"a_stored{s}") for s in range(SLOTS)]
        sp_in = [sem(f"sp_in{s}") for s in range(SLOTS)]
        VS_DONE = 16 * NT

        def gather_values_gpsimd(pool):
            pool.wait_ge(Q["vs_out"], VS_DONE)

            def may_fill(i, s):
                wait(pool, a_stored[s], i * 16)
                pool.wait_ge(A["s_taken"], i * SLOTS + s + 1)
            gathers(pool, 3, vs_table, VS, may_fill)

        def gather_values_sync(sp):
            with sp.Fori(0, ROUNDS) as i:
                for s in range(SLOTS):
                    b = i * SLOTS + s
                    sp.wait_ge(W["onehot_used"], since("onehot_used", 3, pairs_of(sp, b)))
                    sp.dma_start(dst_b[:, s, :], dst_ext[0:1, bass.ds(b * BE + 1, BE)].broadcast_to([P, BE])).then_inc(sp_in[s], 16)
                    sp.wait_ge(sp_in[s], (i + 1) * 16)
                    sp.sem_inc(A["dst_ready"], 1)
                    sp.wait_ge(landed[s], since("landed", 3, (i + 1) * (16 * BJ)))
                    sp.dma_start(v_edges[i * SLOTS + s].rearrange("p (j d) -> p j d", d=D),
                                 ring[:, s * BJ:(s + 1) * BJ, 0:D]).then_inc(a_stored[s], 16)

        def gather_values_scalar(act):
            act.sem_inc(A["s_taken"], SLOTS)
            with act.Fori(0, ROUNDS) as i:
                for s in range(SLOTS):
                    act.wait_ge(landed[s], since("landed", 3, (i + 1) * (16 * BJ)))
                    act.activation(s_src[:, bass.ds((i * SLOTS + s) * BJ, BJ), :], ring[:, s * BJ:(s + 1) * BJ, D:VS],
                                   ACT.Copy).then_inc(A["s_taken"], 1)

        def gather_values_vector(dve):
            dve.memset(s_dst[:], 0.0).then_inc(A["zeroed"], 1)
            dve.wait_ge(A["zeroed"], 1)
            dve.sem_inc(A["sd_added"], 1)
            with dve.Fori(0, NT) as t:
                b0, b1 = span(dve, t)
                dve.tensor_copy(small[:, 16:17], node_id[:, bass.ds(t, 1)]).then_inc(A["node_made"], 1)
                dve.wait_ge(A["node_made"], t + 1)
                apart(dve)
                with dve.Fori(b0, b1 + 1) as b:
                    dve.wait_ge(A["dst_ready"], b + 1)
                    for j in range(BJ):
                        dve.wait_ge(W["onehot_used"], since("onehot_used", 3, (b + t) * BJ + j + 1))
                        dve.tensor_scalar(onehot[:, j, :], dst_b[:, b % SLOTS, j:BE:BJ], small[:, 16:17], None,
                                          ALU.is_equal).then_inc(W["onehot_made"], 1)
                    dve.wait_ge(W["onehot_used"], since("onehot_used", 3, (b + t) * BJ + 2 * BJ))
                    at_b = s_dst[:, bass.ds(b * BJ, BJ), :].rearrange("p k h -> p (k h)")
                    dve.tensor_tensor(at_b, at_b, aux_ps[:, 0:BJ * HEADS], ALU.add).then_inc(A["sd_added"], 1)

        def gather_values_tensor(pe):
            pe.wait_ge(Q["step"], 4 * NT)
            with pe.Fori(0, NT) as t:
                b0, b1 = span(pe, t)
                with pe.Fori(b0, b1 + 1) as b:
                    pe.wait_ge(A["sd_added"], b + t + 1)
                    for j in range(BJ):
                        pe.wait_ge(W["onehot_made"], since("onehot_made", 3, (b + t) * BJ + j + 1))
                        pe.matmul(aux_ps[:, j * HEADS:(j + 1) * HEADS], onehot[:, j, :], s_node[:, t, :],
                                  start=True, stop=True, skip_group_check=True).then_inc(W["onehot_used"], 1)

        B = {n: sem(f"b_{n}") for n in ("loaded", "step", "turned", "taken", "alpha", "keep", "scan", "row", "rowps",
                                        "colps", "max_made", "back", "back_taken", "args", "exps", "aux_made")}
        BG = CB

        def softmax_sync(sp):
            sp.wait_ge(A["s_taken"], SLOTS + NB)
            for s in range(SLOTS):
                sp.wait_ge(a_stored[s], 16 * ROUNDS)
            for c in range(CHUNKS):
                sp.dma_start(dst_t[c * HEADS:(c + 1) * HEADS, 0:T],
                             dst_ext[0:1, c * CE:c * CE + T].broadcast_to([HEADS, T])).then_inc(B["loaded"], 16)
            sp.dma_start(dst_i[:].rearrange("p (b j) -> p b j", j=BJ),
                         dst_ext[0:1, 0:EP].rearrange("a (b p j) -> (a p) b j", p=P, j=BJ)).then_inc(B["loaded"], 16)

        def softmax_tensor(pe):
            pe.wait_ge(B["alpha"], 1)
            for g in range(BG):
                if g >= 1:
                    pe.wait_ge(B["taken"], g)
                for j in range(BJ):
                    last = pe.transpose(tp[0:CP, j, :], alpha_k[:, g * BJ + j, :], ident[:])
                last.then_inc(B["turned"], 1)
            for d in range(2):
                pe.wait_ge(B["scan"], d + 1)
                for k in range(3):
                    last = pe.transpose(aux_ps[0:1, k * CP:(k + 1) * CP], ccol[0:CP, k:k + 1], ident[0:CP, 0:CP])
                last.then_inc(B["rowps"], 1)
                pe.wait_ge(B["row"], d + 1)
                pe.matmul(dense2[0:CP, 0:1], crow[0:1, 5, :], ones_row[0:1, 0:1], start=True, stop=True).then_inc(B["colps"], 1)
            pe.wait_ge(B["max_made"], 1)
            for g in range(BG):
                if g >= 1:
                    pe.wait_ge(B["back_taken"], g)
                for j in range(BJ):
                    last = pe.transpose(dense[:, j * CP:(j + 1) * CP], fwd_t[:, g * BE + j:(g + 1) * BE:BJ], ident[0:CP, 0:CP])
                last.then_inc(B["back"], 1)

        def softmax_scalar(act):
            for g in range(BG):
                act.wait_ge(B["turned"], g + 1)
                act.activation(alpha_t[:, g * BE:(g + 1) * BE].rearrange("q (p j) -> q p j", j=BJ),
                               tp[0:CP, :, :].rearrange("q j p -> q p j"), ACT.Copy).then_inc(B["taken"], 1)
            for g in range(BG):
                act.wait_ge(B["back"], g + 1)
                to = max_e.rearrange("p (c k) h -> p k c h", c=CHUNKS)[:, g * BJ:(g + 1) * BJ]
                act.activation(to, dense[:, 0:BJ * CP].rearrange("p (j c h) -> p j c h", j=BJ, h=HEADS), ACT.Copy).then_inc(B["back_taken"], 1)
            act.wait_ge(B["args"], 1)
            act.activation(aux_e[:, :, 0:HEADS], s_src[:], ACT.Exp).then_inc(B["exps"], 1)
            act.wait_ge(B["args"], 2)
            act.activation(aux_e[:, :, HEADS:2 * HEADS], s_dst[:], ACT.Exp).then_inc(B["exps"], 1)

        def softmax_vector(dve):
            steps = [0]

            def link(ins):
                steps[0] += 1
                ins.then_inc(B["step"], 1)
                dve.wait_ge(B["step"], steps[0])

            dve.wait_ge(A["sd_added"], NB + NT)
            dve.wait_ge(A["s_taken"], SLOTS + NB)
            link(dve.tensor_tensor(s_src[:], s_src[:], s_dst[:], ALU.add))
            link(dve.scalar_tensor_tensor(s_src[:], s_src[:], SLOPE, s_src[:], ALU.mult, ALU.max))
            dve.tensor_copy(alpha_k.rearrange("p k (c h) -> p c k h", c=CHUNKS),
                            s_src.rearrange("p (c k) h -> p c k h", c=CHUNKS)).then_inc(B["alpha"], 1)
            link(dve.tensor_tensor(s_dst[:], s_dst[:], s_dst[:], ALU.add))
            link(dve.scalar_tensor_tensor(s_dst[:], s_dst[:], SLOPE, s_dst[:], ALU.mult, ALU.max))
            dve.wait_ge(B["loaded"], 16 * (CHUNKS + 1))
            link(dve.tensor_tensor(keep_t[:, 0:CE + 1], dst_t[:, 1:T], dst_t[:, 0:T - 1], ALU.is_equal))
            link(dve.tensor_scalar(keep_t[:, 0:CE + 1], keep_t[:, 0:CE + 1], -1.0, BIG, ALU.add, ALU.mult))
            same, ends = ccol[0:CP, 3:4], (ccol[0:CP, 6:7], ccol[0:CP, 7:8])
            link(dve.tensor_copy(ends[0], dst_t[:, 1:2]))
            link(dve.tensor_copy(ends[1], dst_t[:, CE:CE + 1]))
            link(dve.tensor_tensor(same, ends[0], ends[1], ALU.is_equal))
            link(dve.tensor_scalar(same, same, -1.0, BIG, ALU.add, ALU.mult))
            dve.wait_ge(B["taken"], BG)
            for d in range(2):
                if d == 0:
                    run, flip = fwd_t, slice(None)
                    keep, out_edge, in_edge = keep_t[:, 0:CE], slice(CE - 1, CE), keep_t[:, 0:1]
                else:
                    run, flip = bwd_t, slice(None, None, -1)
                    keep, out_edge, in_edge = keep_t[:, 1:CE + 1], slice(0, 1), keep_t[:, CE:CE + 1]
                link(dve.tensor_tensor_scan(run[:, flip], keep[:, flip], alpha_t[:, flip], -BIG, ALU.add, ALU.max))
                link(dve.tensor_copy(ccol[0:CP, 0:1], run[:, out_edge]))
                link(dve.tensor_copy(ccol[0:CP, 2:3], in_edge))
                dve.tensor_tensor(ccol[0:CP, 1:2], in_edge, same, ALU.add).then_inc(B["scan"], 1)
                dve.wait_ge(B["rowps"], d + 1)
                link(dve.tensor_copy(crow[0:1, 0:3, :].rearrange("a k (h c) -> a k h c", h=HEADS),
                                     aux_ps[0:1, 0:3 * CP].rearrange("a (k c h) -> a k h c", k=3, h=HEADS)))
                link(dve.tensor_tensor_scan(crow[0:1, 3, flip], crow[0:1, 1, flip], crow[0:1, 0, flip], -BIG, ALU.add, ALU.max))
                link(dve.memset(crow[0:1, 4, :], -BIG))
                to, of = (slice(1, CP), slice(0, CP - 1)) if d == 0 else (slice(0, CP - 1), slice(1, CP))
                link(dve.tensor_tensor(crow[0:1, 4, to], crow[0:1, 3, of], crow[0:1, 2, to], ALU.add))
                dve.tensor_copy(crow[0:1, 5, :].rearrange("a (c h) -> a h c", h=HEADS),
                                crow[0:1, 4, :].rearrange("a (h c) -> a h c", h=HEADS)).then_inc(B["row"], 1)
                dve.wait_ge(B["colps"], d + 1)
                link(dve.tensor_copy(ccol[0:CP, 4:5], dense2[0:CP, 0:1]))
                tmp = bwd_t if d == 0 else alpha_t
                link(dve.tensor_scalar(tmp, dst_t[:, 1:CE + 1], ends[d], -1.0, ALU.is_equal, ALU.add))
                link(dve.tensor_scalar(tmp, tmp, BIG, ccol[0:CP, 4:5], ALU.mult, ALU.add))
                link(dve.tensor_tensor(run, run, tmp, ALU.max))
            dve.tensor_tensor(fwd_t, fwd_t, bwd_t, ALU.max).then_inc(B["max_made"], 1)
            dve.wait_ge(B["back_taken"], BG)
            link(dve.tensor_tensor(max_e[:], max_e[:], s_dst[:], ALU.max))
            dve.tensor_tensor(s_src[:], s_src[:], max_e[:], ALU.subtract).then_inc(B["args"], 1)
            dve.tensor_tensor(s_dst[:], s_dst[:], max_e[:], ALU.subtract).then_inc(B["args"], 1)
            link(dve.tensor_tensor(aux_e[:, :, 2 * HEADS], dst_i[:], dst_e[:], ALU.is_lt))
            dve.wait_ge(B["exps"], 2)
            own = aux_e[:, :, HEADS:2 * HEADS]
            dve.tensor_tensor(own, own, aux_e[:, :, 2 * HEADS:AUX].broadcast_to([P, COLS, HEADS]),
                              ALU.mult).then_inc(B["aux_made"], 1)

        C2 = {n: sem(f"c_{n}") for n in ("rows_ready", "agg_done", "step", "attn_made",
                                         "tiles_in", "turned", "lhs_made", "out_done", "h_made")}
        late_in = sem("late_in")

        def weigh_sync(sp):
            sp.wait_ge(B["exps"], 2)
            for to, of in ((w_o, Wo), (w_1, W1), (w_2, W2)):
                sp.dma_start(to, of.rearrange("(k p) n -> p k n", p=P)).then_inc(late_in, 16)
            with sp.Fori(0, ROUNDS) as i:
                for s in range(SLOTS):
                    b = i * SLOTS + s
                    sp.wait_ge(W["onehot_used"], since("onehot_used", 4, pairs_of(sp, b)))
                    sp.dma_start(v_ring[:, s * BJ:(s + 1) * BJ, :].rearrange("p j d -> p (j d)"), v_edges[b]).then_inc(sp_in[s], 16)

        def weigh_gpsimd(pool):
            pool.wait_ge(B["aux_made"], 1)
            with pool.Fori(0, ROUNDS) as i:
                for s in range(SLOTS):
                    pool.wait_ge(sp_in[s], (i + 1) * 16 + 16 * ROUNDS)
                    v = v_ring[:, s * BJ:(s + 1) * BJ, :].rearrange("p j (h c) -> p j h c", h=HEADS)
                    w = aux_e[:, bass.ds((i * SLOTS + s) * BJ, BJ), 0:HEADS].rearrange("p j (h o) -> p j h o", o=1)
                    pool.tensor_tensor(v, v, w.broadcast_to([P, BJ, HEADS, C]), ALU.mult).then_inc(C2["rows_ready"], 1)

        def weigh_tensor(pe):
            pe.wait_ge(late_in, 48)
            def tile(t):
                b0, b1 = span(pe, t)
                wait(pe, C2["attn_made"], t)
                pe.matmul(agg[:, 0:D], zero_l[:], zero_r[:, 0:D], start=True, stop=False)
                pe.matmul(aux_ps[:, 0:AUX], zero_l[:], zero_r[:, 0:AUX], start=True, stop=False)
                with pe.Fori(b0, b1 + 1) as b:
                    pe.wait_ge(C2["rows_ready"], b + 1)
                    for j in range(BJ):
                        pe.wait_ge(W["onehot_made"], since("onehot_made", 4, (b + t) * BJ + j + 1))
                        pe.matmul(agg[:, 0:D], onehot[:, j, :], v_ring[:, (b % SLOTS) * BJ + j, :],
                                  start=False, stop=False)
                        pe.matmul(aux_ps[:, 0:AUX], onehot[:, j, :], aux_e[:, b * BJ + j, :],
                                  start=False, stop=False).then_inc(W["onehot_used"], 1)
                pe.matmul(aux_ps[:, 0:AUX], zero_l[:], zero_r[:, 0:AUX], start=False, stop=True)
                pe.matmul(agg[:, 0:D], zero_l[:], zero_r[:, 0:D], start=False, stop=True).then_inc(C2["agg_done"], 1)
                pe.wait_ge(C2["attn_made"], t + 1)
                for k in range(KD):
                    last = pe.transpose(tp[:, k, :], mean[:, k * P:(k + 1) * P], ident[:])
                last.then_inc(C2["turned"], 1)
                pe.wait_ge(C2["lhs_made"], t + 1)
                wait(pe, C2["h_made"], 2 * t)
                pe.wait_ge(C2["tiles_in"], 32 * t + 32)
                for f in range(KD):
                    fs = slice(f * P, (f + 1) * P)
                    for k in range(KD):
                        pe.matmul(dense[:, fs], w_o[:, k, fs], lhs[:, k, :], start=k == 0, stop=False)
                    last = pe.matmul(dense[:, fs], h_self[:, fs], ident[:], start=False, stop=True)
                last.then_inc(C2["out_done"], 1)
            first_and_rest(pe, NT, tile)

        def weigh_vector(dve):
            def tile(t):
                onehots(dve, 4, t)
                dve.wait_ge(C2["agg_done"], t + 1)
                missing, own, den = small[:, 0:1], small[:, 8:16], small[:, 16:24]
                k = 6
                step = C2["step"]
                dve.tensor_scalar(missing, aux_ps[:, 2 * HEADS:AUX], -1.0, 1.0, ALU.mult, ALU.add).then_inc(step, 1)
                dve.wait_ge(step, t * k + 1)
                dve.tensor_scalar(own, aux_ps[:, HEADS:2 * HEADS], missing, None, ALU.add).then_inc(step, 1)
                dve.wait_ge(step, t * k + 2)
                dve.tensor_tensor(den, aux_ps[:, 0:HEADS], own, ALU.add).then_inc(step, 1)
                dve.wait_ge(step, t * k + 3)
                dve.reciprocal(den, den).then_inc(step, 1)
                dve.wait_ge(C2["tiles_in"], 32 * t + 32)

                def heads(a):
                    return a.rearrange("p (h c) -> p h c", h=HEADS)

                def spread(a):
                    return a.rearrange("p (h o) -> p h o", o=1).broadcast_to([P, HEADS, C])
                dve.tensor_tensor(heads(x_tile[:]), heads(x_tile[:]), spread(own), ALU.mult).then_inc(step, 1)
                dve.wait_ge(step, t * k + 5)
                dve.tensor_tensor(x_tile[:], x_tile[:], agg[:, 0:D], ALU.add).then_inc(step, 1)
                dve.wait_ge(step, t * k + 6)
                wait(dve, C2["turned"], t)
                dve.tensor_tensor(heads(mean[:]), heads(x_tile[:]), spread(den), ALU.mult).then_inc(C2["attn_made"], 1)
            first_and_rest(dve, NT, tile)

        def weigh_scalar(act):
            def tile(t):
                wait(act, C2["attn_made"], t)
                wait(act, C2["out_done"], t)
                act.dma_start(x_tile[:], vs_table.rearrange("(t p) d -> t p d", p=P)[t, :, 0:D]).then_inc(C2["tiles_in"], 16)
                act.dma_start(h_self[:], hln_dram[t]).then_inc(C2["tiles_in"], 16)
                act.wait_ge(C2["turned"], t + 1)
                act.activation(lhs[:, 0:KD, :], tp[:, 0:KD, :], ACT.Copy).then_inc(C2["lhs_made"], 1)
                act.wait_ge(C2["out_done"], t + 1)
                for f in range(KD):
                    act.activation(h_cols[:, t, f, :], dense[:, f * P:(f + 1) * P], ACT.Identity,
                                   bias=col("bo", f)).then_inc(C2["h_made"], 1)
            first_and_rest(act, NT, tile)

        F = {n: sem(f"f_{n}") for n in ("stats", "step", "var", "root", "hb_made", "f1_done", "f1_taken", "z_done", "z_made",
                                        "stats2", "step2", "var2", "root2", "x1_in", "zs_made", "turned", "o_made", "o_out")}

        def norm_columns(dve, gather_sem, step_sem, var_sem, root_sem, gname, bname):
            with dve.Fori(0, NT - 1) as t:
                for f in range(KD):
                    dve.bn_stats(bn6[:, f, t, :], h_cols[:, t, f, :]).then_inc(gather_sem, 1)
            for f in range(KD):
                dve.bn_stats(bn6[:, f, NT - 1, :], h_cols[:, NT - 1, f, 0:NL]).then_inc(gather_sem, 1)
            dve.wait_ge(gather_sem, KD * NT)
            n = 0
            for f in range(KD):
                mv = small[:, 32 + 8 * f:34 + 8 * f]
                dve.bn_aggr(mv, bn6[:, f, :, :].rearrange("p t s -> p (t s)")).then_inc(step_sem, 1)
                n += 1
                dve.wait_ge(step_sem, n)
                dve.tensor_scalar(small[:, 34 + 8 * f:35 + 8 * f], mv[:, 1:2], EPS, None, ALU.add).then_inc(var_sem, 1)
            dve.wait_ge(root_sem, KD)
            for f in range(KD):
                mv, r = small[:, 32 + 8 * f:34 + 8 * f], small[:, 34 + 8 * f:35 + 8 * f]
                sc, sh = small[:, 35 + 8 * f:36 + 8 * f], small[:, 36 + 8 * f:37 + 8 * f]
                for ins in (lambda: dve.reciprocal(r, r),
                            lambda: dve.tensor_tensor(sc, r, col(gname, f), ALU.mult),
                            lambda: dve.tensor_tensor(sh, mv[:, 0:1], sc, ALU.mult),
                            lambda: dve.tensor_tensor(sh, col(bname, f), sh, ALU.subtract)):
                    n += 1
                    ins().then_inc(step_sem, 1)
                    dve.wait_ge(step_sem, n)

        def roots(act, var_sem, root_sem):
            act.wait_ge(var_sem, KD)
            for f in range(KD):
                r = small[:, 34 + 8 * f:35 + 8 * f]
                act.activation(r, r, ACT.Sqrt).then_inc(root_sem, 1)

        def feed_forward_vector(dve):
            dve.wait_ge(C2["h_made"], KD * NT)
            norm_columns(dve, F["stats"], F["step"], F["var"], F["root"], "g1", "b1n")
            def tile(t):
                wait(dve, F["z_done"], t)
                for f in range(KD):
                    dve.tensor_scalar(hb[:, f, :], h_cols[:, t, f, :], small[:, 35 + 8 * f:36 + 8 * f],
                                      small[:, 36 + 8 * f:37 + 8 * f], ALU.mult, ALU.add).then_inc(F["hb_made"], 1)
            first_and_rest(dve, NT, tile)
            dve.wait_ge(F["z_made"], KD * NT)
            norm_columns(dve, F["stats2"], F["step2"], F["var2"], F["root2"], "g2", "b2n")
            def tile(t):
                wait(dve, F["turned"], t)
                for f in range(KD):
                    dve.tensor_scalar(hb[:, f, :], h_cols[:, t, f, :], small[:, 35 + 8 * f:36 + 8 * f],
                                      small[:, 36 + 8 * f:37 + 8 * f], ALU.mult, ALU.add).then_inc(F["zs_made"], 1)
                dve.wait_ge(F["turned"], t + 1)
                dve.wait_ge(F["x1_in"], 16 * t + 16)
                wait(dve, F["o_out"], 16 * t)
                dve.tensor_tensor(mean[:], tp[:, 0:KD, :].rearrange("p k n -> p (k n)"), x_tile[:], ALU.add).then_inc(F["o_made"], 1)
            first_and_rest(dve, NT, tile)

        def feed_forward_tensor(pe):
            def tile(t):
                pe.wait_ge(F["hb_made"], KD * t + KD)
                wait(pe, F["f1_taken"], KF * t)
                for m in range(KF):
                    for k in range(KD):
                        last = pe.matmul(dense[:, m * P:(m + 1) * P], w_1[:, k, m * P:(m + 1) * P], hb[:, k, :],
                                         start=k == 0, stop=k == KD - 1)
                last.then_inc(F["f1_done"], 1)
                pe.wait_ge(F["f1_taken"], KF * t + KF)
                wait(pe, F["z_made"], KD * t)
                for f in range(KD):
                    fs = slice(f * P, (f + 1) * P)
                    for m in range(KF):
                        pe.matmul(dense2[:, fs], w_2[:, m, fs], f1[:, m, :], start=m == 0, stop=False)
                    last = pe.matmul(dense2[:, fs], ident[:], hb[:, f, :], start=False, stop=True)
                last.then_inc(F["z_done"], 1)
            first_and_rest(pe, NT, tile)
            def tile(t):
                pe.wait_ge(F["zs_made"], KD * t + KD)
                wait(pe, F["o_made"], t)
                for f in range(KD):
                    last = pe.transpose(tp[:, f, :], hb[:, f, :], ident[:])
                last.then_inc(F["turned"], 1)
            first_and_rest(pe, NT, tile)

        def feed_forward_scalar(act):
            roots(act, F["var"], F["root"])
            def tile(t):
                act.wait_ge(F["f1_done"], t + 1)
                wait(act, F["z_done"], t)
                for m in range(KF):
                    act.activation(f1[:, m, :], dense[:, m * P:(m + 1) * P], ACT.Relu, bias=col("b1", m)).then_inc(F["f1_taken"], 1)
                act.wait_ge(F["z_done"], t + 1)
                for f in range(KD):
                    act.activation(h_cols[:, t, f, :], dense2[:, f * P:(f + 1) * P], ACT.Identity,
                                   bias=col("b2", f)).then_inc(F["z_made"], 1)
            first_and_rest(act, NT, tile)
            roots(act, F["var2"], F["root2"])

        def feed_forward_sync(sp):
            sp.wait_ge(C2["attn_made"], NT)
            out_t = out[0:(NT - 1) * P, :].rearrange("(t p) d -> t p d", p=P)

            def x1_load(t):
                wait(sp, F["o_made"], t)
                sp.dma_start(x_tile[:], x1_dram[t]).then_inc(F["x1_in"], 16)
                sp.wait_ge(F["o_made"], t + 1)
            def tile(t):
                x1_load(t)
                sp.dma_start(out_t[t], mean[:]).then_inc(F["o_out"], 16)
            first_and_rest(sp, NT - 1, tile)
            x1_load(NT - 1)
            sp.dma_start(out[(NT - 1) * P:N, :], mean[0:NL, :]).then_inc(F["o_out"], 16)
            sp.wait_ge(F["o_out"], 16 * NT)

        @block.sync
        def _(sp):
            setup_sync(sp)
            norm_x_sync(sp)
            for l in range(3):
                sage_sync(sp, l)
            project_sync(sp)
            gather_values_sync(sp)
            softmax_sync(sp)
            weigh_sync(sp)
            feed_forward_sync(sp)

        @block.scalar
        def _(act):
            setup_scalar(act)
            norm_x_scalar(act)
            for l in range(3):
                sage_scalar(act, l)
            project_scalar(act)
            gather_values_scalar(act)
            softmax_scalar(act)
            weigh_scalar(act)
            feed_forward_scalar(act)

        @block.vector
        def _(dve):
            setup_vector(dve)
            norm_x_vector(dve)
            for l in range(3):
                sage_vector(dve, l)
            project_vector(dve)
            gather_values_vector(dve)
            softmax_vector(dve)
            weigh_vector(dve)
            feed_forward_vector(dve)

        @block.tensor
        def _(pe):
            for l in range(3):
                sage_tensor(pe, l)
            project_tensor(pe)
            gather_values_tensor(pe)
            softmax_tensor(pe)
            weigh_tensor(pe)
            feed_forward_tensor(pe)

        @block.gpsimd
        def _(pool):
            setup_gpsimd(pool)
            for l in range(3):
                sage_gpsimd(pool, l)
            gather_values_gpsimd(pool)
            weigh_gpsimd(pool)


_INS = ["x", "src", "dst"] + [f"L0_gnn_{n}" for i in range(3) for n in (f"W{i}_self", f"W{i}_neigh", f"b{i}")] + [
    f"L1_gnn_{n}" for n in ("Wq", "bq", "Wk", "bk", "Wv", "bv", "Wo", "bo", "W1", "b1", "W2", "b2",
                            "bn1_g", "bn1_b", "bn2_g", "bn2_b")]


def kernel(**inputs):
    import numpy as _np
    import concourse.bacc as _bacc
    from concourse import mybir as _mybir
    from concourse.bass_utils import run_bass_kernel_spmd as _run

    nc = _bacc.Bacc("TRN2", target_bir_lowering=False, num_devices=1)
    arrays, a = {}, {}
    for name in _INS:
        v = _np.ascontiguousarray(inputs[name])
        arrays[f"in_{name}_dram"] = v
        a[name] = nc.dram_tensor(f"in_{name}_dram", v.shape, _mybir.dt.from_np(v.dtype), kind="ExternalInput").ap()
    out = nc.dram_tensor("out_0_dram", inputs["x"].shape, _mybir.dt.float32, kind="ExternalOutput").ap()
    g = {n[len("L1_gnn_"):]: a[n] for n in _INS if n.startswith("L1_gnn_")}
    gnn_kernel(nc, a["x"], a["src"], a["dst"],
               [(a[f"L0_gnn_W{i}_neigh"], a[f"L0_gnn_W{i}_self"]) for i in range(3)],
               [a[f"L0_gnn_b{i}"] for i in range(3)], out=out, **g)
    r = _run(nc, [arrays], core_ids=[0])
    return r.results[0]["out_0_dram"]
```

```python
from contextlib import ExitStack

import concourse.bass as bass
from concourse import mybir

P = 128
ALU = mybir.AluOpType
ACT = mybir.ActivationFunctionType
AX = mybir.AxisListType
F32 = mybir.dt.float32
BF16 = mybir.dt.bfloat16
I32 = mybir.dt.int32

BIG = 1.0e30
EPS = 1e-5
SLOPE = 0.2
HEADS = 8
BJ = 4
BE = P * BJ
SLOTS = 7
AHEAD = 4
CHUNKS = 14


def gnn_kernel(nc, x, src, dst, sage_w, sage_b, Wq, bq, Wk, bk, Wv, bv, Wo, bo, W1, b1, W2, b2,
               bn1_g, bn1_b, bn2_g, bn2_b, out):
    N, D = x.shape
    E = src.shape[0]
    DF = W1.shape[1]
    C = D // HEADS
    KD, KF = D // P, DF // P
    NT = -(-N // P)
    NP = NT * P
    NL = N - (NT - 1) * P
    NB = -(-E // BE)
    EP = NB * BE
    VS = D + HEADS
    AUX = 2 * HEADS + 1
    CB = NB // CHUNKS
    CE = CB * BE
    CP = CHUNKS * HEADS
    COLS = NB * BJ
    BT = 4
    BN = BT * P
    BATCHES = NT // BT
    GO = 7
    ROUNDS = NB // SLOTS
    assert NB % SLOTS == 0 and NB % CHUNKS == 0 and KD == 2 and CP <= P
    assert NT % GO == 0 and BATCHES % 2 == 0 and NT - BATCHES * BT == 1

    def dram(name, shape, dt=F32):
        return nc.dram_tensor(name, shape, dt, kind="Internal").ap()

    x_pad = dram("x_pad", (NT, P, D))
    tables = [dram(f"h_table{i}", (NP, D)) for i in range(3)]
    x1_dram = dram("x1_dram", (NT, P, D))
    hln_dram = dram("hln_dram", (NT, P, D))
    vs_table = dram("vs_table", (NP, VS))
    v_edges = dram("v_edges", (NB, P, BJ * D))
    dst_ext = dram("dst_ext", (1, EP + 2), I32)
    src_ext = dram("src_ext", (1, EP), I32)

    with ExitStack() as ctx:
        def sb(name, shape, dt=F32):
            return ctx.enter_context(nc.sbuf_tensor(name, shape, dt))

        def ps(name, shape):
            return ctx.enter_context(nc.psum_tensor(name, shape, F32))

        def sem(name):
            return ctx.enter_context(nc.semaphore(name))

        hN_words, ring_words = NT * D, SLOTS * BJ * VS
        T = CE + 2
        arena_words = 4 * T + T // 2 + 2 * COLS * HEADS
        arena = sb("arena", [P, arena_words])
        o_late = 2 * T
        h_nodes = arena[:, 0:hN_words].rearrange("p (t d) -> p t d", d=D)
        o_ring = hN_words
        ring = arena[:, o_ring:o_ring + ring_words].rearrange("p (s w) -> p s w", w=VS)
        o_w = o_ring + ring_words
        w_sage = arena[:, o_w:o_w + 3 * 2 * KD * D].rearrange("p (l k d) -> p l k d", l=3, k=2 * KD)
        o_q = o_w + 3 * 2 * KD * D
        w_qkv = arena[:, o_q:o_q + KD * 3 * D].rearrange("p (k d) -> p k d", k=KD)
        x_rows_o = o_q + KD * 3 * D
        dst_b = arena[:, 0:SLOTS * BE].bitcast(I32).rearrange("p (s e) -> p s e", e=BE)
        alpha_t = arena[0:CP, 0:CE]
        fwd_t = arena[0:CP, T:T + CE]
        bwd_t = arena[0:CP, 2 * T:2 * T + CE]
        dst_t = arena[0:CP, 3 * T:4 * T].bitcast(I32)
        keep_t = arena[0:CP, 4 * T:4 * T + T // 2].bitcast(BF16)
        alpha_k = arena[:, T:T + COLS * HEADS].rearrange("p (k q) -> p k q", q=CP)
        max_e = arena[:, 2 * T:2 * T + COLS * HEADS].rearrange("p (k h) -> p k h", h=HEADS)
        o_se = 4 * T + T // 2
        s_src = arena[:, o_se:o_se + COLS * HEADS].rearrange("p (k h) -> p k h", h=HEADS)
        s_dst = arena[:, o_se + COLS * HEADS:o_se + 2 * COLS * HEADS].rearrange("p (k h) -> p k h", h=HEADS)
        aux_e = arena[:, 0:COLS * AUX].rearrange("p (k a) -> p k a", a=AUX)
        assert COLS * AUX <= 2 * T and x_rows_o + 7 * D <= o_se and ring_words <= 2 * COLS * HEADS
        h_cols = arena[:, o_late:o_late + hN_words].rearrange("p (t f n) -> p t f n", f=KD, n=P)
        v_ring = arena[:, o_se:o_se + SLOTS * BJ * (D + AUX)].rearrange("p (s w) -> p s w", w=D + AUX)
        o_f1 = o_late + hN_words
        f1 = arena[:, o_f1:o_f1 + 2 * KF * BN].rearrange("p (i m n) -> p i m n", i=2, m=KF)
        sums = arena[:, COLS * AUX:COLS * AUX + D + AUX]
        assert o_f1 + 2 * KF * BN <= o_se and COLS * AUX + D + AUX <= o_late

        o_late_w = o_se + SLOTS * BJ * (D + AUX)
        w_o = arena[:, o_late_w:o_late_w + KD * D].rearrange("p (k d) -> p k d", k=KD)
        w_1 = arena[:, o_late_w + KD * D:o_late_w + KD * (D + DF)].rearrange("p (k d) -> p k d", k=KD)
        w_2 = arena[:, o_late_w + KD * (D + DF):o_late_w + KD * (D + DF) + KF * D].rearrange("p (k d) -> p k d", k=KF)
        assert o_late_w + KD * (D + DF) + KF * D <= arena_words
        b_sage = sb("b_sage", [1, 3, D])
        b_qkv = arena[:, x_rows_o:x_rows_o + 3 * D]
        hln = arena[:, x_rows_o + 3 * D:x_rows_o + 4 * D]
        lhs_q = arena[:, x_rows_o + 4 * D:x_rows_o + 5 * D].rearrange("p (k n) -> p k n", n=P)
        cols = sb("cols", [P, 5 * KD + KF + KD])
        ident = sb("ident", [P, P])
        iota_n = sb("iota_n", [P, P])
        part = sb("part", [P, 1])
        tile_base = sb("tile_base", [P, NT])
        node_id = sb("node_id", [P, NT])
        iota_t = sb("iota_t", [P, P])
        zero_l = sb("zero_l", [P, P], BF16)
        zero_r = sb("zero_r", [P, D + AUX], BF16)
        ones_row = sb("ones_row", [1, P])
        src_e = sb("src_e", [P, COLS + SLOTS * BJ], I32)
        dst_i = sb("dst_i", [P, COLS], I32)
        dst_e = sb("dst_e", [P, COLS])
        idx = sb("idx", [P, 2, SLOTS * BJ], I32)
        onehot = sb("onehot", [P, BJ, P])
        s_node = sb("s_node", [P, NT, HEADS])
        tile_block = sb("tile_block", [1, NT + 1], I32)
        need = sb("need", [1, NB + SLOTS], I32)
        n_row = NT + 1 + NB + SLOTS
        row_f = arena[0:1, hN_words - n_row:hN_words]
        tiles3 = sb("tiles3", [P, 3 * D])
        mean, h_self, x_tile = (tiles3[:, i * D:(i + 1) * D] for i in range(3))
        lhs = sb("lhs", [P, 2 * KD, P])
        qk = sb("qk", [P, 2 * D])
        vs_tile = sb("vs_tile", [P, VS])
        small = sb("small", [P, 64])
        bn6 = sb("bn6", [P, KD, NT, 6])
        bn2 = sb("bn2", [P, NT, 2])
        rstd = sb("rstd", [P, NT])
        shift = sb("shift", [P, NT])
        crow = tiles3[0:1, 0:6 * CP].rearrange("a (k q) -> a k q", k=6)
        ccol = sb("ccol", [P, 8])

        banks = ps("banks", [P, 8, 512])
        agg, dense, dense2, aux_ps = (banks[:, i, :] for i in (0, 2, 3, 4))
        tp, tp_q = (banks[:, i, :].rearrange("p (k n) -> p k n", n=P) for i in (1, 5))
        qk_ps = banks[:, 6, :]

        col_of, at = {}, 0
        for name, v, k in (("bo", bo, KD), ("g1", bn1_g, KD), ("b1n", bn1_b, KD), ("g2", bn2_g, KD),
                           ("b2n", bn2_b, KD), ("b2", b2, KD), ("b1", b1, KF)):
            col_of[name] = (at, k, v)
            at += k

        def col(name, k):
            return cols[:, col_of[name][0] + k:col_of[name][0] + k + 1]

        const_in = sem("const_in")
        ext_in = sem("ext_in")
        edges_in = sem("edges_in")
        pads_made = sem("pads_made")
        passed = sem("passed")
        consts_made = sem("consts_made")
        ident_made = sem("ident_made")
        walk_made = sem("walk_made")
        WALK = 9
        block = ctx.enter_context(nc.Block())
        def wait(eng, semaphore, value):
            if not isinstance(value, int) or value > 0:
                eng.wait_ge(semaphore, value)

        def first_and_rest(eng, n, body):
            body(0)
            with eng.Fori(1, n) as t:
                body(t)

        def pipeline(eng, n, depth, step):
            for t in range(depth):
                step(t)
            with eng.Fori(depth, n) as t:
                step(t)
            for t in range(n, n + depth):
                step(t)

        def there(t):
            return not isinstance(t, int) or 0 <= t < NT

        def apart(eng):
            eng.sem_inc(passed, 1)

        setup_dmas = []
        for l in range(3):
            for m in range(2):
                setup_dmas.append((w_sage[:, l, m * KD:(m + 1) * KD, :], sage_w[l][m].rearrange("(k p) n -> p k n", p=P)))
            setup_dmas.append((b_sage[0:1, l, :], sage_b[l].rearrange("(a d) -> a d", a=1)))
        for i, (w, b) in enumerate(((Wq, bq), (Wk, bk), (Wv, bv))):
            setup_dmas.append((w_qkv[:, :, i * D:(i + 1) * D], w.rearrange("(k p) n -> p k n", p=P)))
            setup_dmas.append((b_qkv[:, i * D:(i + 1) * D], b.rearrange("(a d) -> a d", a=1).broadcast_to([P, D])))
        for name, (at, k, v) in col_of.items():
            for i in range(k):
                setup_dmas.append((cols[:, at + i:at + i + 1], v[i * P:(i + 1) * P].rearrange("(p a) -> p a", a=1)))
        CONSTS = 16 * len(setup_dmas)

        def setup_sync(sp):
            sp.dma_start(dst_ext[0:1, 1:1 + E].rearrange("a (r c) -> (a r) c", r=32),
                         dst.rearrange("(r c) -> r c", r=32)).then_inc(ext_in, 16)
            sp.dma_start(src_ext[0:1, 0:E].rearrange("a (r c) -> (a r) c", r=32),
                         src.rearrange("(r c) -> r c", r=32)).then_inc(ext_in, 16)
            sp.wait_ge(pads_made, 3)
            sp.dma_start(dst_ext[0:1, 0:1], dst_b[0:1, 1, 0:1]).then_inc(ext_in, 16)
            sp.dma_start(dst_ext[0:1, 1 + EP:2 + EP], dst_b[0:1, 1, 0:1]).then_inc(ext_in, 16)
            sp.dma_start(dst_ext[0:1, 1 + E:1 + EP], dst_b[0:1, 0, 0:EP - E]).then_inc(ext_in, 16)
            sp.dma_start(src_ext[0:1, E:EP], dst_b[0:1, 2, 0:EP - E]).then_inc(ext_in, 16)
            sp.wait_ge(ext_in, 16 * 6)
            sp.dma_start(dst_i[:].rearrange("p (b j) -> p b j", j=BJ),
                         dst_ext[0:1, 1:1 + EP].rearrange("a (b p j) -> (a p) b j", p=P, j=BJ)).then_inc(edges_in, 16)
            sp.dma_start(src_e[:, 0:COLS].rearrange("p (b j) -> p b j", j=BJ),
                         src_ext[0:1, :].rearrange("a (b p j) -> (a p) b j", p=P, j=BJ)).then_inc(edges_in, 16)

        def setup_scalar(act):
            for to, of in setup_dmas:
                act.dma_start(to, of).then_inc(const_in, 16)

        def setup_gpsimd(pool):
            pool.memset(dst_b[0:1, 0, :], NP).then_inc(pads_made, 1)
            pool.memset(dst_b[0:1, 1, :], -1).then_inc(pads_made, 1)
            pool.memset(dst_b[0:1, 2, :], 0).then_inc(pads_made, 1)
            pool.iota(iota_n[:], [[1, P]], 0, 0, allow_small_or_imprecise_dtypes=True).then_inc(consts_made, 1)
            pool.iota(part[:], [[0, 1]], 0, 1, allow_small_or_imprecise_dtypes=True).then_inc(consts_made, 1)
            pool.iota(tile_base[:], [[P, NT]], 0, 0, allow_small_or_imprecise_dtypes=True).then_inc(consts_made, 1)
            pool.iota(node_id[:], [[P, NT]], 0, 1, allow_small_or_imprecise_dtypes=True).then_inc(consts_made, 1)
            pool.memset(zero_l[:], 0.0).then_inc(consts_made, 1)
            pool.memset(zero_r[:], 0.0).then_inc(consts_made, 1)
            pool.memset(src_e[:, COLS:], 0).then_inc(consts_made, 1)
            pool.memset(ones_row[:], 1.0).then_inc(consts_made, 1)
            pool.memset(ring[:, :, D:D + 1], 1.0).then_inc(consts_made, 1)
            pool.iota(row_f[0:1, 0:NT + 1], [[P, NT + 1]], 0, 0, allow_small_or_imprecise_dtypes=True).then_inc(consts_made, 1)
            pool.iota(row_f[0:1, NT + 1:], [[1, NB + SLOTS]], -SLOTS, 0, allow_small_or_imprecise_dtypes=True).then_inc(consts_made, 1)
        NCONST = 11

        def setup_vector(dve):
            dve.wait_ge(consts_made, NCONST)
            dve.tensor_scalar(ident[:], iota_n[:], part[:, 0:1], None, ALU.is_equal).then_inc(ident_made, 1)
            dve.wait_ge(edges_in, 32)
            step = [0]

            def link(ins):
                step[0] += 1
                ins.then_inc(walk_made, 1)
                dve.wait_ge(walk_made, step[0])

            link(dve.tensor_copy(dst_e[:], dst_i[:]))
            cmp = arena[0:1, 0:(NT + 1) * NB].rearrange("a (t b) -> a t b", b=NB)
            firsts = dst_e[0:1, 0:COLS:BJ].rearrange("a (o b) -> a o b", o=1).broadcast_to([1, NT + 1, NB])
            starts = row_f[0:1, 0:NT + 1].rearrange("a (t o) -> a t o", o=1).broadcast_to([1, NT + 1, NB])
            link(dve.tensor_tensor(cmp, firsts, starts, ALU.is_lt))
            cnt = small[0:1, 0:NT + 1]
            link(dve.tensor_reduce(cnt, cmp, AX.X, ALU.add))
            link(dve.tensor_scalar(cnt, cnt, -1.0, 0.0, ALU.add, ALU.max))
            link(dve.tensor_copy(tile_block[:], cnt))
            NI = NB + SLOTS
            cmp2 = arena[0:1, 0:NI * NT].rearrange("a (b t) -> a b t", t=NT)
            blocks_row = row_f[0:1, NT + 1:]
            b_b = blocks_row.rearrange("a (b o) -> a b o", o=1).broadcast_to([1, NI, NT])
            t_b = cnt[0:1, 0:NT].rearrange("a (o t) -> a o t", o=1).broadcast_to([1, NI, NT])
            link(dve.tensor_tensor(cmp2, t_b, b_b, ALU.is_le))
            cnt2 = arena[0:1, NI * NT:NI * NT + NI]
            link(dve.tensor_reduce(cnt2, cmp2, AX.X, ALU.add))
            link(dve.tensor_tensor(cnt2, cnt2, blocks_row, ALU.add))
            link(dve.tensor_scalar(cnt2, cnt2, float(BJ), float(BJ), ALU.mult, ALU.add))
            assert step[0] == WALK
            dve.tensor_scalar(need[:], cnt2, float(BJ), None, ALU.max).then_inc(walk_made, 1)

        WALKED = WALK + 1

        ln_loaded = sem("ln_loaded")
        ln_stats = sem("ln_stats")
        ln_aggr = sem("ln_aggr")
        ln_var = sem("ln_var")
        ln_sqrt = sem("ln_sqrt")
        ln_fold = sem("ln_fold")
        ln_done = sem("ln_done")
        x_padded = sem("x_padded")
        pad_zero = sem("pad_zero")
        stored0 = sem("stored0")
        G = 7

        def norm_x_sync(sp):
            sp.wait_ge(walk_made, WALKED)
            xt = x[0:(NT - 1) * P, :].rearrange("(t p) d -> p t d", p=P)
            for g in range(0, NT - 1, 12):
                sp.dma_start(h_nodes[:, g:g + 12, :], xt[:, g:g + 12, :]).then_inc(ln_loaded, 16)
            sp.wait_ge(pad_zero, 1)
            sp.dma_start(h_nodes[0:NL, NT - 1, :], x[(NT - 1) * P:N, :]).then_inc(ln_loaded, 16)
            sp.wait_ge(ln_loaded, 16 * ((NT - 1) // 12 + 1))
            sp.dma_start(x_pad.rearrange("t p d -> p t d"), h_nodes[:, :, :]).then_inc(x_padded, 16)

        def rstd_and_shift(dve, var_sem, sqrt_sem, fold_sem):
            dve.tensor_scalar(rstd[:], bn2[:, :, 1], EPS, None, ALU.add).then_inc(var_sem, 1)
            dve.wait_ge(sqrt_sem, 1)
            dve.reciprocal(rstd[:], rstd[:]).then_inc(fold_sem, 1)
            dve.wait_ge(fold_sem, 1)
            dve.scalar_tensor_tensor(shift[:], bn2[:, :, 0], -1.0, rstd[:], ALU.mult, ALU.mult).then_inc(fold_sem, 1)

        def norm_x_vector(dve):
            dve.wait_ge(walk_made, WALKED)
            dve.memset(h_nodes[:, NT - 1, :], 0.0).then_inc(pad_zero, 1)
            dve.wait_ge(ln_loaded, 16 * ((NT - 1) // 12 + 1))
            with dve.Fori(0, NT) as t:
                dve.bn_stats(bn6[:, 0, t, :], h_nodes[:, t, :]).then_inc(ln_stats, 1)
            dve.wait_ge(ln_stats, NT)
            for t in range(NT):
                dve.bn_aggr(bn2[:, t, :], bn6[:, 0, t, :]).then_inc(ln_aggr, 1)
            dve.wait_ge(ln_aggr, NT)
            rstd_and_shift(dve, ln_var, ln_sqrt, ln_fold)

        def norm_x_scalar(act):
            act.wait_ge(ln_var, 1)
            act.activation(rstd[:], rstd[:], ACT.Sqrt).then_inc(ln_sqrt, 1)
            act.wait_ge(ln_fold, 2)
            act.wait_ge(x_padded, 16)
            with act.Fori(0, NT) as t:
                act.activation(h_nodes[:, t, :], h_nodes[:, t, :], ACT.Relu,
                               bias=shift[:, bass.ds(t, 1)], scale=rstd[:, bass.ds(t, 1)]).then_inc(ln_done, 1)
                act.wait_ge(ln_done, t + 1)
                act.dma_start(tables[0].rearrange("(t p) d -> t p d", p=P)[t], h_nodes[:, t, :]).then_inc(stored0, 16)

        PAIRS = NB + NT - 1
        TOTAL = dict(staged=ROUNDS + 1, slots_free=AHEAD + NB, rows_ready=NB, onehot_used=BJ * PAIRS,
                     onehot_made=BJ * PAIRS, base_moved=NT, agg_done=NT, deg=2 * NT, mean_made=NT, self_made=NT,
                     turned=NT, lhs_made=NT, out_done=NT, h_made=NT, stored=16 * NT, landed=16 * BJ * ROUNDS)
        W = {n: sem(n) for n in TOTAL if n != "landed"}
        landed = [sem(f"landed{s}") for s in range(SLOTS)]
        x_in = sem("x_in")
        x1_stats = sem("x1_stats")

        def since(name, w, v):
            return v + w * TOTAL[name]

        def gathers(pool, w, table, width, may_fill):
            IR = SLOTS * BJ

            def stage_indices(first, half):
                pool.tensor_copy(idx[:, half, :], src_e[:, bass.ds(first, IR)]).then_inc(W["staged"], 1)
            if w:
                pool.wait_ge(W["staged"], since("staged", w, 0))
            stage_indices(0, 0)
            def rounds(i2):
                for half in range(2):
                    i = i2 * 2 + half
                    pool.wait_ge(W["staged"], since("staged", w, i + 1))
                    for s in range(SLOTS):
                        may_fill(i, s)
                        apart(pool)
                        for j in range(BJ):
                            k = s * BJ + j
                            pool.indirect_dma_start(ring[:, k, 0:width], None, table,
                                                    bass.IndirectOffsetOnAxis(idx[:, half, k:k + 1], 0)).then_inc(landed[s], 16)
                    stage_indices((i + 1) * IR, 1 - half)
            first_and_rest(pool, ROUNDS // 2, rounds)

        def pairs_of(eng, i):
            return eng.value_load(need[0:1, bass.ds(i, 1)], min_val=0, max_val=BJ * (NB + NT + 1))

        def relay(sp, w):
            sp.sem_inc(W["slots_free"], AHEAD)
            with sp.Fori(0, ROUNDS) as i:
                for s in range(SLOTS):
                    sp.wait_ge(W["onehot_used"], since("onehot_used", w, pairs_of(sp, i * SLOTS + s + AHEAD)))
                    sp.sem_inc(W["slots_free"], 1)
                    sp.wait_ge(landed[s], since("landed", w, (i + 1) * (16 * BJ)))
                    sp.sem_inc(W["rows_ready"], 1)

        def span(eng, t):
            b0 = eng.value_load(tile_block[0:1, bass.ds(t, 1)], min_val=0, max_val=NB - 1)
            b1 = eng.value_load(tile_block[0:1, bass.ds(t + 1, 1)], min_val=0, max_val=NB - 1)
            return b0, b1

        def base_and_span(dve, w, t):
            b0, b1 = span(dve, t)
            if w > 0 or not isinstance(t, int) or t > 0:
                dve.wait_ge(W["onehot_made"], since("onehot_made", w, (b0 + t) * BJ))
            dve.tensor_scalar(iota_t[:], iota_n[:], tile_base[:, bass.ds(t, 1)], None, ALU.add).then_inc(W["base_moved"], 1)
            return b0, b1

        def onehots(dve, w, t, b0, b1, behind_first=None):
            dve.wait_ge(W["base_moved"], since("base_moved", min(w, 3), t + 1))
            apart(dve)

            def of_block(b):
                for j in range(BJ):
                    dve.wait_ge(W["onehot_used"], since("onehot_used", w, (b + t) * BJ + j + 1))
                    dve.tensor_scalar(onehot[:, j, :], iota_t[:], dst_e[:, bass.ds(b * BJ + j, 1)], None,
                                      ALU.is_equal).then_inc(W["onehot_made"], 1)
            if behind_first is None:
                with dve.Fori(b0, b1 + 1) as b:
                    of_block(b)
            else:
                of_block(b0)
                behind_first()
                with dve.If(b0 < b1):
                    with dve.Fori(b0 + 1, b1 + 1) as b:
                        of_block(b)

        def sage_gpsimd(pool, l):
            pool.wait_ge(*((stored0, 16 * NT) if l == 0 else (W["stored"], l * TOTAL["stored"])))
            pool.wait_ge(consts_made, NCONST)

            def may_fill(i, s):
                pool.wait_ge(W["slots_free"], since("slots_free", l, i * SLOTS + s + 1))
            gathers(pool, l, tables[l], D, may_fill)

        def sage_sync(sp, l):
            relay(sp, l)

        def sage_tensor(pe, l):
            if l == 0:
                pe.wait_ge(walk_made, WALKED)
                pe.wait_ge(ident_made, 1)
                pe.wait_ge(consts_made, NCONST)
                pe.wait_ge(const_in, CONSTS)
                pe.sem_inc(W["onehot_used"], BJ)
            def sums(t):
                b0, b1 = span(pe, t)
                wait(pe, W["mean_made"], since("mean_made", l, t))
                pe.matmul(agg[:, 0:D + 1], zero_l[:], zero_r[:, 0:D + 1], start=True, stop=False)
                with pe.Fori(b0, b1 + 1) as b:
                    pe.wait_ge(W["rows_ready"], since("rows_ready", l, b + 1))
                    for j in range(BJ):
                        pe.wait_ge(W["onehot_made"], since("onehot_made", l, (b + t) * BJ + j + 1))
                        pe.matmul(agg[:, 0:D + 1], onehot[:, j, :], ring[:, (b % SLOTS) * BJ + j, 0:D + 1],
                                  start=False, stop=False).then_inc(W["onehot_used"], 1)
                pe.matmul(agg[:, 0:D + 1], zero_l[:], zero_r[:, 0:D + 1], start=False, stop=True).then_inc(W["agg_done"], 1)

            def turn(t):
                wait(pe, W["lhs_made"], since("lhs_made", l, t))
                pe.wait_ge(W["self_made"], since("self_made", l, t + 1))
                for k in range(KD):
                    pe.transpose(tp[:, KD + k, :], h_self[:, k * P:(k + 1) * P], ident[:])
                pe.wait_ge(W["mean_made"], since("mean_made", l, t + 1))
                for k in range(KD):
                    last = pe.transpose(tp[:, k, :], mean[:, k * P:(k + 1) * P], ident[:])
                last.then_inc(W["turned"], 1)

            def products(t):
                wait(pe, W["h_made"], since("h_made", l, t))
                pe.matmul(dense[:, 0:D], ones_row[:], b_sage[0:1, l, :], start=True, stop=False)
                pe.wait_ge(W["lhs_made"], since("lhs_made", l, t + 1))
                for k in range(2 * KD):
                    last = pe.matmul(dense[:, 0:D], lhs[:, k, :], w_sage[:, l, k, :], start=False, stop=k == 2 * KD - 1)
                last.then_inc(W["out_done"], 1)

            def step(t):
                sums(t)
                turn(t)
                products(t)

            def last_layer_step(t):
                if there(t):
                    sums(t)
                if there(t - 1):
                    turn(t - 1)
                if there(t - 4):
                    turn_normed_tensor(pe, t - 4)
                if there(t - 2):
                    products(t - 2)
                if there(t - 4):
                    project_tensor(pe, t - 4)
            if l < 2:
                first_and_rest(pe, NT, step)
            else:
                pipeline(pe, NT, 4, last_layer_step)

        def sage_vector(dve, l):
            def means(t):
                dve.wait_ge(W["agg_done"], since("agg_done", l, t + 1))
                dve.tensor_scalar(small[:, 0:1], agg[:, D:D + 1], 1.0, None, ALU.max).then_inc(W["deg"], 1)
                dve.wait_ge(W["deg"], since("deg", l, 2 * t + 1))
                dve.reciprocal(small[:, 1:2], small[:, 0:1]).then_inc(W["deg"], 1)
                dve.wait_ge(W["deg"], since("deg", l, 2 * t + 2))
                wait(dve, W["turned"], since("turned", l, t))
                dve.tensor_scalar(mean[:], agg[:, 0:D], small[:, 1:2], None, ALU.mult).then_inc(W["mean_made"], 1)

            def residual(t):
                dve.wait_ge(x_in, 16 * t + 16)
                dve.wait_ge(W["out_done"], since("out_done", l, t + 1))
                dve.tensor_tensor(h_nodes[:, t, :], dense[:, 0:D], x_tile[:], ALU.add).then_inc(W["h_made"], 1)
                dve.wait_ge(W["h_made"], since("h_made", l, t + 1))
                apart(dve)
                dve.bn_stats(stats6, h_nodes[:, t, :]).then_inc(x1_stats, 1)
                dve.wait_ge(x1_stats, 2 * t + 1)
                apart(dve)
                dve.bn_aggr(mean_var, stats6).then_inc(x1_stats, 1)
                dve.wait_ge(x1_stats, 2 * t + 2)
                dve.tensor_scalar(var_eps, mean_var[:, 1:2], EPS, None, ALU.add).then_inc(Q["var"], 1)

            def step(t):
                onehots(dve, l, t, *base_and_span(dve, l, t))
                means(t)

            def last_layer_step(t):
                def between():
                    if there(t - 4):
                        norm_fold_vector(dve, t - 4)
                    if there(t - 3):
                        residual(t - 3)
                if there(t):
                    onehots(dve, l, t, *base_and_span(dve, l, t), behind_first=between)
                    means(t)
                else:
                    between()
                if there(t - 5):
                    project_vector(dve, t - 5)
            if l < 2:
                first_and_rest(dve, NT, step)
            else:
                pipeline(dve, NT, 5, last_layer_step)

        def sage_scalar(act, l):
            to = (tables[l + 1].rearrange("(t p) d -> t p d", p=P) if l < 2 else x1_dram)

            def own_rows(t):
                wait(act, W["turned"], since("turned", l, t))
                act.activation(h_self[:], h_nodes[:, t, :], ACT.Copy).then_inc(W["self_made"], 1)

            def take_turned(t):
                act.wait_ge(W["turned"], since("turned", l, t + 1))
                wait(act, W["out_done"], since("out_done", l, t))
                act.activation(lhs[:], tp, ACT.Copy).then_inc(W["lhs_made"], 1)

            def store(t):
                act.wait_ge(W["h_made"], since("h_made", l, t + 1))
                act.dma_start(to[t], h_nodes[:, t, :]).then_inc(W["stored"], 16)

            def step(t):
                own_rows(t)
                take_turned(t)
                act.wait_ge(W["out_done"], since("out_done", l, t + 1))
                apart(act)
                act.activation(h_nodes[:, t, :], dense[:, 0:D], ACT.Relu).then_inc(W["h_made"], 1)
                store(t)

            def x_load(t):
                wait(act, W["h_made"], since("h_made", l, t))
                act.dma_start(x_tile[:], x_pad[t]).then_inc(x_in, 16)

            def root_of(t):
                act.wait_ge(Q["var"], t + 1)
                act.activation(root, var_eps, ACT.Sqrt).then_inc(Q["sqrt"], 1)

            def last_layer_step(t):
                if there(t - 6):
                    values_out_scalar(act, t - 6)
                if there(t - 1):
                    own_rows(t - 1)
                if there(t - 4):
                    norm_scalar(act, t - 4)
                if there(t - 3):
                    store(t - 3)
                    root_of(t - 3)
                if there(t - 2):
                    x_load(t - 2)
                if there(t - 1):
                    take_turned(t - 1)
                if there(t - 4):
                    take_normed_scalar(act, t - 4)
            if l < 2:
                first_and_rest(act, NT, step)
            else:
                pipeline(act, NT, 6, last_layer_step)
                act.wait_ge(Q["hln_out"], 16 * NT)

        Q = {n: sem(f"q_{n}") for n in ("var", "sqrt", "fold", "h_made", "turned", "lhs_made", "out_done",
                                        "taken", "step", "s_made", "hln_out", "vs_out")}
        stats6, mean_var, var_eps, root, scale1, shift1 = (
            small[:, a:b] for a, b in ((40, 46), (46, 48), (48, 49), (49, 50), (50, 51), (51, 52)))

        def norm_fold_vector(dve, t):
            dve.wait_ge(Q["sqrt"], t + 1)
            wait(dve, Q["h_made"], t)
            apart(dve)
            dve.reciprocal(scale1, root).then_inc(Q["fold"], 1)
            dve.wait_ge(Q["fold"], 2 * t + 1)
            dve.scalar_tensor_tensor(shift1, mean_var[:, 0:1], -1.0, scale1, ALU.mult, ALU.mult).then_inc(Q["fold"], 1)
            dve.wait_ge(Q["fold"], 2 * t + 2)
            apart(dve)

        def norm_scalar(act, t):
            wait(act, Q["turned"], t)
            wait(act, Q["hln_out"], 16 * t)
            act.wait_ge(Q["fold"], 2 * t + 2)
            apart(act)
            act.activation(hln, h_nodes[:, t, :], ACT.Relu, bias=shift1, scale=scale1).then_inc(Q["h_made"], 1)
            act.wait_ge(Q["h_made"], t + 1)
            act.dma_start(hln_dram[t], hln).then_inc(Q["hln_out"], 16)

        def turn_normed_tensor(pe, t):
            pe.wait_ge(Q["h_made"], t + 1)
            wait(pe, Q["lhs_made"], t)
            for k in range(KD):
                last = pe.transpose(tp_q[:, k, :], hln[:, k * P:(k + 1) * P], ident[:])
            last.then_inc(Q["turned"], 1)

        def project_tensor(pe, t):
            pe.wait_ge(Q["lhs_made"], t + 1)
            wait(pe, Q["taken"], t)
            wait(pe, Q["step"], 4 * t)
            for k in range(KD):
                pe.matmul(qk_ps, lhs_q[:, k, :], w_qkv[:, k, 0:2 * D], start=k == 0, stop=k == KD - 1)
            for k in range(KD):
                last = pe.matmul(dense2[:, 0:D], lhs_q[:, k, :], w_qkv[:, k, 2 * D:3 * D], start=k == 0, stop=k == KD - 1)
            last.then_inc(Q["out_done"], 1)

        def take_normed_scalar(act, t):
            act.wait_ge(Q["turned"], t + 1)
            wait(act, Q["out_done"], t)
            act.activation(lhs_q, tp_q[:, 0:KD, :], ACT.Copy).then_inc(Q["lhs_made"], 1)

        def values_out_scalar(act, t):
            act.wait_ge(Q["taken"], t + 1)
            act.wait_ge(Q["s_made"], t + 1)
            act.dma_start(vs_table.rearrange("(t p) d -> t p d", p=P)[t], vs_tile[:]).then_inc(Q["vs_out"], 16)

        def project_vector(dve, t):
            dve.wait_ge(Q["out_done"], t + 1)
            dve.tensor_tensor(qk[:], qk_ps, b_qkv[:, 0:2 * D], ALU.add).then_inc(Q["step"], 1)
            wait(dve, Q["vs_out"], 16 * t)
            dve.tensor_tensor(vs_tile[:, 0:D], dense2[:, 0:D], b_qkv[:, 2 * D:3 * D], ALU.add).then_inc(Q["taken"], 1)
            dve.wait_ge(Q["step"], t * 4 + 1)
            dve.tensor_tensor(qk[:, 0:D], qk[:, 0:D], qk[:, D:2 * D], ALU.mult).then_inc(Q["step"], 1)
            dve.wait_ge(Q["step"], t * 4 + 2)
            dve.tensor_reduce(small[:, 8:8 + HEADS], qk[:, 0:D].rearrange("p (h c) -> p h c", h=HEADS), AX.X,
                              ALU.add).then_inc(Q["step"], 1)
            dve.wait_ge(Q["step"], t * 4 + 3)
            dve.tensor_scalar(s_node[:, t, :], small[:, 8:8 + HEADS], float(C) ** -0.5, None, ALU.mult).then_inc(Q["step"], 1)
            dve.wait_ge(Q["step"], t * 4 + 4)
            apart(dve)
            dve.tensor_copy(vs_tile[:, D:VS], s_node[:, t, :]).then_inc(Q["s_made"], 1)

        A = {n: sem(f"a_{n}") for n in ("s_taken", "zeroed", "sd_added",
                                        "node_made", "dst_ready")}
        a_stored = [sem(f"a_stored{s}") for s in range(SLOTS)]
        sp_in = [sem(f"sp_in{s}") for s in range(SLOTS)]
        VS_DONE = 16 * NT

        def gather_values_gpsimd(pool):
            pool.wait_ge(Q["vs_out"], VS_DONE)

            def may_fill(i, s):
                wait(pool, a_stored[s], i * 16)
                pool.wait_ge(A["s_taken"], i * SLOTS + s + 1)
            gathers(pool, 3, vs_table, VS, may_fill)

        dst_loaded, scan_step = sem("dst_loaded"), sem("scan_step")
        same, ends = ccol[0:CP, 3:4], (ccol[0:CP, 6:7], ccol[0:CP, 7:8])

        def scan_marks_sync(sp):
            sp.wait_ge(Q["out_done"], NT)
            sp.wait_ge(Q["taken"], NT)
            sp.wait_ge(Q["hln_out"], 16 * NT)
            sp.wait_ge(W["stored"], since("stored", 2, 16 * NT))
            for c in range(CHUNKS):
                sp.dma_start(dst_t[c * HEADS:(c + 1) * HEADS, 0:T],
                             dst_ext[0:1, c * CE:c * CE + T].broadcast_to([HEADS, T])).then_inc(dst_loaded, 16)
            sp.dma_start(dst_i[:].rearrange("p (b j) -> p b j", j=BJ),
                         dst_ext[0:1, 0:EP].rearrange("a (b p j) -> (a p) b j", p=P, j=BJ)).then_inc(dst_loaded, 16)

        def scan_marks_vector(dve):
            def link(step, ins):
                ins.then_inc(scan_step, 1)
                dve.wait_ge(scan_step, step)

            dve.wait_ge(dst_loaded, 16 * (CHUNKS + 1))
            link(1, dve.tensor_tensor(keep_t[:, 0:CE + 1], dst_t[:, 1:T], dst_t[:, 0:T - 1], ALU.is_equal))
            link(2, dve.tensor_scalar(keep_t[:, 0:CE + 1], keep_t[:, 0:CE + 1], -1.0, BIG, ALU.add, ALU.mult))
            link(3, dve.tensor_copy(ends[0], dst_t[:, 1:2]))
            link(4, dve.tensor_copy(ends[1], dst_t[:, CE:CE + 1]))
            link(5, dve.tensor_tensor(same, ends[0], ends[1], ALU.is_equal))
            link(6, dve.tensor_scalar(same, same, -1.0, BIG, ALU.add, ALU.mult))

        def gather_values_sync(sp):
            def one_round(i):
                for s in range(SLOTS):
                    b = i * SLOTS + s
                    sp.wait_ge(W["onehot_used"], since("onehot_used", 3, pairs_of(sp, b)))
                    sp.dma_start(dst_b[:, s, :], dst_ext[0:1, bass.ds(b * BE + 1, BE)].broadcast_to([P, BE])).then_inc(sp_in[s], 16)
                    if s > 0 or not isinstance(i, int):
                        sp.wait_ge(sp_in[s - 1], (i + 1) * 16 if s > 0 else i * 16)
                        sp.sem_inc(A["dst_ready"], 1)
            first_and_rest(sp, ROUNDS, one_round)
            sp.wait_ge(sp_in[SLOTS - 1], ROUNDS * 16)
            sp.sem_inc(A["dst_ready"], 1)

        def gather_values_scalar(act):
            act.sem_inc(A["s_taken"], SLOTS)
            with act.Fori(0, ROUNDS) as i:
                for s in range(SLOTS):
                    act.wait_ge(landed[s], since("landed", 3, (i + 1) * (16 * BJ)))
                    act.activation(s_src[:, bass.ds((i * SLOTS + s) * BJ, BJ), :], ring[:, s * BJ:(s + 1) * BJ, D:VS],
                                   ACT.Copy).then_inc(A["s_taken"], 1)
                    act.dma_start(v_edges[i * SLOTS + s].rearrange("p (j d) -> p j d", d=D),
                                  ring[:, s * BJ:(s + 1) * BJ, 0:D]).then_inc(a_stored[s], 16)

        def gather_values_vector(dve):
            dve.memset(s_dst[:], 0.0).then_inc(A["zeroed"], 1)
            dve.wait_ge(A["zeroed"], 1)
            dve.sem_inc(A["sd_added"], 1)
            with dve.Fori(0, NT) as t:
                b0, b1 = span(dve, t)
                dve.tensor_copy(small[:, 16:17], node_id[:, bass.ds(t, 1)]).then_inc(A["node_made"], 1)
                dve.wait_ge(A["node_made"], t + 1)
                apart(dve)

                def one_hots(b, js):
                    for j in js:
                        dve.wait_ge(W["onehot_used"], since("onehot_used", 3, (b + t) * BJ + j + 1))
                        dve.tensor_scalar(onehot[:, j, :], dst_b[:, b % SLOTS, j:BE:BJ], small[:, 16:17], None,
                                          ALU.is_equal).then_inc(W["onehot_made"], 1)

                def add(b):
                    dve.wait_ge(W["onehot_used"], since("onehot_used", 3, (b + t) * BJ + 2 * BJ))
                    at_b = s_dst[:, bass.ds(b * BJ, BJ), :].rearrange("p k h -> p (k h)")
                    dve.tensor_tensor(at_b, at_b, aux_ps[:, 0:BJ * HEADS], ALU.add).then_inc(A["sd_added"], 1)

                dve.wait_ge(A["dst_ready"], b0 + 1)
                one_hots(b0, range(BJ))
                with dve.If(b0 < b1):
                    with dve.Fori(b0 + 1, b1 + 1) as b:
                        dve.wait_ge(A["dst_ready"], b + 1)
                        one_hots(b, range(BJ // 2))
                        add(b - 1)
                        one_hots(b, range(BJ // 2, BJ))
                add(b1)

        def gather_values_tensor(pe):
            pe.wait_ge(Q["step"], 4 * NT)
            with pe.Fori(0, NT) as t:
                b0, b1 = span(pe, t)
                with pe.Fori(b0, b1 + 1) as b:
                    pe.wait_ge(A["sd_added"], b + t + 1)
                    for j in range(BJ):
                        pe.wait_ge(W["onehot_made"], since("onehot_made", 3, (b + t) * BJ + j + 1))
                        pe.matmul(aux_ps[:, j * HEADS:(j + 1) * HEADS], onehot[:, j, :], s_node[:, t, :],
                                  start=True, stop=True, skip_group_check=True).then_inc(W["onehot_used"], 1)

        B = {n: sem(f"b_{n}") for n in ("step", "turned", "taken", "alpha", "scan", "row", "rowps",
                                        "colps", "max_made", "back", "back_taken", "args", "exps", "aux_made")}
        BG = CB

        def turn_bank(g):
            return banks[:, 5 + g % 2, :].rearrange("p (j n) -> p j n", n=P)

        def softmax_tensor(pe):
            pe.wait_ge(B["alpha"], 1)
            for g in range(BG):
                if g >= 2:
                    pe.wait_ge(B["taken"], g - 1)
                for j in range(BJ):
                    last = pe.transpose(turn_bank(g)[0:CP, j, :], alpha_k[:, g * BJ + j, :], ident[:])
                last.then_inc(B["turned"], 1)
            for d in range(2):
                pe.wait_ge(B["scan"], d + 1)
                for k in range(3):
                    last = pe.transpose(aux_ps[0:1, k * CP:(k + 1) * CP], ccol[0:CP, k:k + 1], ident[0:CP, 0:CP])
                last.then_inc(B["rowps"], 1)
                pe.wait_ge(B["row"], d + 1)
                pe.matmul(dense2[0:CP, 0:1], crow[0:1, 5, :], ones_row[0:1, 0:1], start=True, stop=True).then_inc(B["colps"], 1)
            pe.wait_ge(B["max_made"], 1)
            for g in range(BG):
                if g >= 2:
                    pe.wait_ge(B["back_taken"], g - 1)
                for j in range(BJ):
                    last = pe.transpose(turn_bank(g)[:, j, 0:CP], fwd_t[:, g * BE + j:(g + 1) * BE:BJ], ident[0:CP, 0:CP])
                last.then_inc(B["back"], 1)

        def softmax_scalar(act):
            for g in range(BG):
                act.wait_ge(B["turned"], g + 1)
                act.activation(alpha_t[:, g * BE:(g + 1) * BE].rearrange("q (p j) -> q p j", j=BJ),
                               turn_bank(g)[0:CP, :, :].rearrange("q j p -> q p j"), ACT.Copy).then_inc(B["taken"], 1)
            for g in range(BG):
                act.wait_ge(B["back"], g + 1)
                to = max_e.rearrange("p (c k) h -> p k c h", c=CHUNKS)[:, g * BJ:(g + 1) * BJ]
                act.activation(to, turn_bank(g)[:, :, 0:CP].rearrange("p j (c h) -> p j c h", h=HEADS), ACT.Copy).then_inc(B["back_taken"], 1)
            act.wait_ge(B["args"], 1)
            act.activation(aux_e[:, :, 0:HEADS], s_src[:], ACT.Exp).then_inc(B["exps"], 1)
            act.wait_ge(B["args"], 2)
            act.activation(aux_e[:, :, HEADS:2 * HEADS], s_dst[:], ACT.Exp).then_inc(B["exps"], 1)

        def softmax_vector(dve):
            steps = [0]

            def link(ins):
                steps[0] += 1
                ins.then_inc(B["step"], 1)
                dve.wait_ge(B["step"], steps[0])

            dve.wait_ge(A["sd_added"], NB + NT)
            dve.wait_ge(A["s_taken"], SLOTS + NB)
            for s in range(SLOTS):
                dve.wait_ge(a_stored[s], 16 * ROUNDS)
            link(dve.tensor_tensor(s_src[:], s_src[:], s_dst[:], ALU.add))
            link(dve.scalar_tensor_tensor(s_src[:], s_src[:], SLOPE, s_src[:], ALU.mult, ALU.max))
            dve.tensor_copy(alpha_k.rearrange("p k (c h) -> p c k h", c=CHUNKS),
                            s_src.rearrange("p (c k) h -> p c k h", c=CHUNKS)).then_inc(B["alpha"], 1)
            link(dve.tensor_tensor(s_dst[:], s_dst[:], s_dst[:], ALU.add))
            link(dve.scalar_tensor_tensor(s_dst[:], s_dst[:], SLOPE, s_dst[:], ALU.mult, ALU.max))
            dve.wait_ge(B["taken"], BG)
            for d in range(2):
                if d == 0:
                    run, flip = fwd_t, slice(None)
                    keep, out_edge, in_edge = keep_t[:, 0:CE], slice(CE - 1, CE), keep_t[:, 0:1]
                else:
                    run, flip = bwd_t, slice(None, None, -1)
                    keep, out_edge, in_edge = keep_t[:, 1:CE + 1], slice(0, 1), keep_t[:, CE:CE + 1]
                link(dve.tensor_tensor_scan(run[:, flip], keep[:, flip], alpha_t[:, flip], -BIG, ALU.add, ALU.max))
                link(dve.tensor_copy(ccol[0:CP, 0:1], run[:, out_edge]))
                link(dve.tensor_copy(ccol[0:CP, 2:3], in_edge))
                dve.tensor_tensor(ccol[0:CP, 1:2], in_edge, same, ALU.add).then_inc(B["scan"], 1)
                dve.wait_ge(B["rowps"], d + 1)
                link(dve.tensor_copy(crow[0:1, 0:3, :].rearrange("a k (h c) -> a k h c", h=HEADS),
                                     aux_ps[0:1, 0:3 * CP].rearrange("a (k c h) -> a k h c", k=3, h=HEADS)))
                link(dve.tensor_tensor_scan(crow[0:1, 3, flip], crow[0:1, 1, flip], crow[0:1, 0, flip], -BIG, ALU.add, ALU.max))
                link(dve.memset(crow[0:1, 4, :], -BIG))
                to, of = (slice(1, CP), slice(0, CP - 1)) if d == 0 else (slice(0, CP - 1), slice(1, CP))
                link(dve.tensor_tensor(crow[0:1, 4, to], crow[0:1, 3, of], crow[0:1, 2, to], ALU.add))
                dve.tensor_copy(crow[0:1, 5, :].rearrange("a (c h) -> a h c", h=HEADS),
                                crow[0:1, 4, :].rearrange("a (h c) -> a h c", h=HEADS)).then_inc(B["row"], 1)
                dve.wait_ge(B["colps"], d + 1)
                link(dve.tensor_copy(ccol[0:CP, 4:5], dense2[0:CP, 0:1]))
                tmp = bwd_t if d == 0 else alpha_t
                link(dve.tensor_scalar(tmp, dst_t[:, 1:CE + 1], ends[d], -BIG, ALU.not_equal, ALU.mult))
                link(dve.scalar_tensor_tensor(run, tmp, ccol[0:CP, 4:5], run, ALU.add, ALU.max))
            dve.tensor_tensor(fwd_t, fwd_t, bwd_t, ALU.max).then_inc(B["max_made"], 1)
            dve.wait_ge(B["back_taken"], BG)
            link(dve.tensor_tensor(max_e[:], max_e[:], s_dst[:], ALU.max))
            dve.tensor_tensor(s_src[:], s_src[:], max_e[:], ALU.subtract).then_inc(B["args"], 1)
            dve.tensor_tensor(s_dst[:], s_dst[:], max_e[:], ALU.subtract).then_inc(B["args"], 1)
            link(dve.tensor_tensor(aux_e[:, :, 2 * HEADS], dst_i[:], dst_e[:], ALU.is_lt))
            dve.wait_ge(B["exps"], 2)
            own = aux_e[:, :, HEADS:2 * HEADS]
            dve.tensor_tensor(own, own, aux_e[:, :, 2 * HEADS:AUX].broadcast_to([P, COLS, HEADS]),
                              ALU.mult).then_inc(B["aux_made"], 1)

        C2 = {n: sem(f"c_{n}") for n in ("aux_there", "rows_ready", "agg_done", "agg_taken", "step", "attn_made", "v_in", "hln_in",
                                         "turned", "lhs_made", "out_done", "h_made", "stats")}
        late_in = sem("late_in")

        def weigh_sync(sp):
            sp.wait_ge(B["exps"], 2)
            for to, of in ((w_o, Wo), (w_1, W1), (w_2, W2)):
                sp.dma_start(to, of.rearrange("(k p) n -> p k n", p=P)).then_inc(late_in, 16)
            with sp.Fori(0, ROUNDS) as i:
                for s in range(SLOTS):
                    b = i * SLOTS + s
                    sp.wait_ge(W["onehot_used"], since("onehot_used", 4, pairs_of(sp, b)))
                    sp.dma_start(v_ring[:, s * BJ:(s + 1) * BJ, 0:D],
                                 v_edges[b].rearrange("p (j d) -> p j d", d=D)).then_inc(sp_in[s], 16)

        def weigh_gpsimd(pool):
            pool.wait_ge(B["aux_made"], 1)
            with pool.Fori(0, ROUNDS) as i:
                for s in range(SLOTS):
                    pool.wait_ge(sp_in[s], (i + 1) * 16 + 16 * ROUNDS)
                    apart(pool)
                    of_b = bass.ds((i * SLOTS + s) * BJ, BJ)
                    pool.tensor_copy(v_ring[:, s * BJ:(s + 1) * BJ, D:D + AUX], aux_e[:, of_b, :]).then_inc(C2["aux_there"], 1)
                    v = v_ring[:, s * BJ:(s + 1) * BJ, 0:D].rearrange("p j (h c) -> p j h c", h=HEADS)
                    w = aux_e[:, of_b, 0:HEADS].rearrange("p j (h o) -> p j h o", o=1)
                    pool.tensor_tensor(v, v, w.broadcast_to([P, BJ, HEADS, C]), ALU.mult).then_inc(C2["rows_ready"], 1)

        def weigh_tensor(pe):
            pe.wait_ge(late_in, 48)
            AW = D + AUX

            def step(t):
                if there(t):
                    b0, b1 = span(pe, t)
                    wait(pe, C2["agg_taken"], t)
                    pe.matmul(agg[:, 0:AW], zero_l[:], zero_r[:, 0:AW], start=True, stop=False)
                    with pe.Fori(b0, b1 + 1) as b:
                        pe.wait_ge(C2["aux_there"], b + 1)
                        apart(pe)
                        pe.wait_ge(C2["rows_ready"], b + 1)
                        for j in range(BJ):
                            pe.wait_ge(W["onehot_made"], since("onehot_made", 4, (b + t) * BJ + j + 1))
                            pe.matmul(agg[:, 0:AW], onehot[:, j, :], v_ring[:, (b % SLOTS) * BJ + j, :],
                                      start=False, stop=False).then_inc(W["onehot_used"], 1)
                    pe.matmul(agg[:, 0:AW], zero_l[:], zero_r[:, 0:AW], start=False, stop=True).then_inc(C2["agg_done"], 1)
                if there(t - 1):
                    pe.wait_ge(C2["attn_made"], t)
                    wait(pe, C2["lhs_made"], t - 1)
                    for k in range(KD):
                        last = pe.transpose(tp[:, k, :], mean[:, k * P:(k + 1) * P], ident[:])
                    last.then_inc(C2["turned"], 1)
                if there(t - 2):
                    pe.wait_ge(C2["lhs_made"], t - 1)
                    wait(pe, C2["h_made"], KD * (t - 2))
                    pe.wait_ge(C2["hln_in"], 16 * (t - 1))
                    for f in range(KD):
                        fs = slice(f * P, (f + 1) * P)
                        for k in range(KD):
                            pe.matmul(dense[:, fs], w_o[:, k, fs], lhs[:, k, :], start=k == 0, stop=False)
                        last = pe.matmul(dense[:, fs], h_self[:, fs], ident[:], start=False, stop=True)
                    last.then_inc(C2["out_done"], 1)
            pipeline(pe, NT, 2, step)

        def weigh_vector(dve):
            own, den = small[:, 8:16], small[:, 16:24]
            step = C2["step"]
            STEPS = 5

            def heads(a):
                return a.rearrange("p (h c) -> p h c", h=HEADS)

            def spread(a):
                return a.rearrange("p (h o) -> p h o", o=1).broadcast_to([P, HEADS, C])

            def attention(t):
                dve.wait_ge(C2["agg_taken"], t + 1)
                dve.tensor_scalar(own, sums[:, D + HEADS:D + 2 * HEADS], sums[:, D + 2 * HEADS:D + AUX], 1.0,
                                  ALU.subtract, ALU.add).then_inc(step, 1)
                dve.wait_ge(step, t * STEPS + 1)
                dve.tensor_tensor(den, sums[:, D:D + HEADS], own, ALU.add).then_inc(step, 1)
                dve.wait_ge(C2["v_in"], 16 * t + 16)
                dve.tensor_tensor(heads(x_tile[:]), heads(x_tile[:]), spread(own), ALU.mult).then_inc(step, 1)
                dve.wait_ge(step, t * STEPS + 2)
                dve.reciprocal(den, den).then_inc(step, 1)
                dve.wait_ge(step, t * STEPS + 4)
                dve.tensor_tensor(x_tile[:], x_tile[:], sums[:, 0:D], ALU.add).then_inc(step, 1)
                dve.wait_ge(step, t * STEPS + 5)
                wait(dve, C2["turned"], t)
                dve.tensor_tensor(heads(mean[:]), heads(x_tile[:]), spread(den), ALU.mult).then_inc(C2["attn_made"], 1)

            def tile_step(t):
                if there(t):
                    b0, b1 = base_and_span(dve, 4, t)
                    onehots(dve, 4, t, b0, b1, (lambda: attention(t - 1)) if there(t - 1) else (lambda: None))
                elif there(t - 1):
                    attention(t - 1)
                if there(t - 3):
                    dve.wait_ge(C2["h_made"], KD * (t - 2))
                    apart(dve)
                    tile_stats(dve, t - 3, C2["stats"])
            pipeline(dve, NT, 3, tile_step)

        def tile_stats(dve, t, done):
            nodes = NL if isinstance(t, int) and t == NT - 1 else P
            for f in range(KD):
                dve.bn_stats(bn6[:, f, t, :], h_cols[:, t, f, 0:nodes]).then_inc(done, 1)

        def weigh_scalar(act):
            def step(t):
                if there(t):
                    wait(act, C2["attn_made"], t)
                    act.dma_start(x_tile[:], vs_table.rearrange("(t p) d -> t p d", p=P)[t, :, 0:D]).then_inc(C2["v_in"], 16)
                    act.wait_ge(C2["agg_done"], t + 1)
                    act.activation(sums, agg[:, 0:D + AUX], ACT.Copy).then_inc(C2["agg_taken"], 1)
                if there(t - 1):
                    wait(act, C2["out_done"], t - 1)
                    act.dma_start(h_self[:], hln_dram[t - 1]).then_inc(C2["hln_in"], 16)
                    act.wait_ge(C2["turned"], t)
                    act.activation(lhs[:, 0:KD, :], tp[:, 0:KD, :], ACT.Copy).then_inc(C2["lhs_made"], 1)
                if there(t - 2):
                    act.wait_ge(C2["out_done"], t - 1)
                    apart(act)
                    for f in range(KD):
                        act.activation(h_cols[:, t - 2, f, :], dense[:, f * P:(f + 1) * P], ACT.Identity,
                                       bias=col("bo", f)).then_inc(C2["h_made"], 1)
            pipeline(act, NT, 2, step)

        F = {n: sem(f"f_{n}") for n in ("step", "var", "root", "hb_made", "f1_done", "f1_taken", "z_done", "z_made",
                                        "stats2", "x1_in", "zs_made", "turned", "o_made", "o_out")}
        scale, bias, var = (lambda f, i=i: small[:, 32 + 8 * f + i:33 + 8 * f + i] for i in (3, 4, 2))
        FOLD_STEPS = 5 * KD

        def fold_norm(dve, w, gname, bname):
            n = w * FOLD_STEPS
            for f in range(KD):
                mv = small[:, 32 + 8 * f:34 + 8 * f]
                dve.bn_aggr(mv, bn6[:, f, :, :].rearrange("p t s -> p (t s)")).then_inc(F["step"], 1)
                n += 1
                dve.wait_ge(F["step"], n)
                dve.tensor_scalar(var(f), mv[:, 1:2], EPS, None, ALU.add).then_inc(F["var"], 1)
            dve.wait_ge(F["root"], KD * (w + 1))
            for ins in (lambda f: dve.reciprocal(var(f), var(f)),
                        lambda f: dve.tensor_tensor(scale(f), var(f), col(gname, f), ALU.mult),
                        lambda f: dve.tensor_tensor(bias(f), small[:, 32 + 8 * f:33 + 8 * f], scale(f), ALU.mult),
                        lambda f: dve.tensor_tensor(bias(f), col(bname, f), bias(f), ALU.subtract)):
                for f in range(KD):
                    ins(f).then_inc(F["step"], 1)
                n += KD
                dve.wait_ge(F["step"], n)

        def roots(act, w):
            act.wait_ge(F["var"], KD * (w + 1))
            for f in range(KD):
                act.activation(var(f), var(f), ACT.Sqrt).then_inc(F["root"], 1)

        def batch(i, f):
            if isinstance(i, int) and i == BATCHES:
                return h_cols[:, i * BT:NT, f, :]
            return h_cols[:, bass.ds(i * BT, BT), f, :]

        def nodes_of(i):
            return (NT - BATCHES * BT) * P if isinstance(i, int) and i == BATCHES else BN

        def tiles_of(a, i):
            return a[:, 0:nodes_of(i)].rearrange("p (t n) -> p t n", n=P)

        def feed_forward_vector(dve):
            dve.wait_ge(C2["stats"], KD * NT)
            fold_norm(dve, 0, "g1", "b1n")
            def norm(i):
                for f in range(KD):
                    dve.tensor_scalar(batch(i, f), batch(i, f), scale(f), bias(f), ALU.mult, ALU.add).then_inc(F["hb_made"], 1)
            with dve.Fori(0, BATCHES) as i:
                norm(i)
            norm(BATCHES)
            def residual(i):
                for f in range(KD):
                    dve.wait_ge(F["z_done"], i * KD + f + 1)
                    apart(dve)
                    dve.scalar_tensor_tensor(batch(i, f), tiles_of(banks[:, 4 + f, :], i), col("b2", f), batch(i, f),
                                             ALU.add, ALU.add).then_inc(F["z_made"], 1)
                dve.wait_ge(F["z_made"], (i + 1) * KD)
                apart(dve)
                for t in range(nodes_of(i) // P):
                    tile_stats(dve, i * BT + t, F["stats2"])
            dve.wait_ge(F["hb_made"], (BATCHES + 1) * KD)
            with dve.Fori(0, BATCHES) as i:
                residual(i)
            residual(BATCHES)
            dve.wait_ge(F["stats2"], KD * NT)
            fold_norm(dve, 1, "g2", "b2n")
            dve.sem_inc(F["step"], 1)
            dve.wait_ge(F["x1_in"], 16 * NT // GO)
            for g in range(NT // GO):
                dve.wait_ge(F["turned"], g + 1)
                x1_g = h_nodes[:, g * GO:(g + 1) * GO, :].rearrange("p t d -> p (t d)")
                dve.tensor_tensor(x1_g, x1_g, turned_bank(g)[:, 0:GO * D], ALU.add).then_inc(F["o_made"], 1)

        def turned_bank(g):
            return banks[:, g % 2 * 4:g % 2 * 4 + 4, :].rearrange("p k n -> p (k n)")

        def feed_forward_tensor(pe):
            def first(i, half):
                for m in range(KF):
                    wait(pe, F["f1_taken"], KF * (i - 1) + m + 1)
                    for k in range(KD):
                        if m == 0:
                            pe.wait_ge(F["hb_made"], i * KD + k + 1)
                        last = pe.matmul(banks[:, m, 0:nodes_of(i)], w_1[:, k, m * P:(m + 1) * P], batch(i, k),
                                         start=k == 0, stop=k == KD - 1)
                    last.then_inc(F["f1_done"], 1)

            def second(i, half):
                for f in range(KD):
                    wait(pe, F["z_made"], KD * (i - 1) + f + 1)
                    for m in range(KF):
                        if f == 0:
                            pe.wait_ge(F["f1_taken"], i * KF + m + 1)
                        last = pe.matmul(banks[:, 4 + f, 0:nodes_of(i)], w_2[:, m, f * P:(f + 1) * P],
                                         f1[:, half, m, 0:nodes_of(i)], start=m == 0, stop=m == KF - 1)
                    last.then_inc(F["z_done"], 1)

            def two(i2):
                for half in range(2):
                    i = i2 * 2 + half
                    first(i, half)
                    if not (isinstance(i, int) and i == 0):
                        second(i - 1, 1 - half)
            first_and_rest(pe, BATCHES // 2, two)
            first(BATCHES, 0)
            second(BATCHES - 1, 1)
            second(BATCHES, 0)
            for g in range(NT // GO):
                pe.wait_ge(F["zs_made"], KD * g + KD)
                if g == 0:
                    pe.wait_ge(F["z_made"], KD * (BATCHES + 1))
                    pe.wait_ge(F["f1_taken"], KF * (BATCHES + 1))
                wait(pe, F["o_made"], g - 1)
                for t in range(GO):
                    for f in range(KD):
                        at = t * D + f * P
                        last = pe.transpose(turned_bank(g)[:, at:at + P], h_cols[:, g * GO + t, f, :], ident[:])
                last.then_inc(F["turned"], 1)

        def feed_forward_scalar(act):
            roots(act, 0)
            def take(i, half):
                for m in range(KF):
                    act.wait_ge(F["f1_done"], i * KF + m + 1)
                    if m == 0:
                        wait(act, F["z_done"], (i - 1) * KD)
                    act.activation(f1[:, half, m, 0:nodes_of(i)], banks[:, m, 0:nodes_of(i)], ACT.Relu,
                                   bias=col("b1", m)).then_inc(F["f1_taken"], 1)

            def two(i2):
                for half in range(2):
                    take(i2 * 2 + half, half)
            first_and_rest(act, BATCHES // 2, two)
            take(BATCHES, 0)
            roots(act, 1)
            act.wait_ge(F["step"], 2 * FOLD_STEPS + 1)
            for g in range(NT // GO):
                for f in range(KD):
                    of = h_cols[:, g * GO:(g + 1) * GO, f, :]
                    act.activation(of, of, ACT.Identity, bias=bias(f), scale=scale(f)).then_inc(F["zs_made"], 1)

        def feed_forward_sync(sp):
            sp.wait_ge(C2["rows_ready"], NB)
            sp.wait_ge(C2["aux_there"], NB)
            for g in range(NT // GO):
                gs = slice(g * GO, (g + 1) * GO)
                sp.dma_start(h_nodes[:, gs, :], x1_dram.rearrange("t p d -> p t d")[:, gs, :]).then_inc(F["x1_in"], 16)
            out_t = out[0:(NT - 1) * P, :].rearrange("(t p) d -> p t d", p=P)
            for g in range(NT // GO):
                sp.wait_ge(F["o_made"], g + 1)
                g1 = min((g + 1) * GO, NT - 1)
                sp.dma_start(out_t[:, g * GO:g1, :], h_nodes[:, g * GO:g1, :]).then_inc(F["o_out"], 16)
            sp.dma_start(out[(NT - 1) * P:N, :], h_nodes[0:NL, NT - 1, :]).then_inc(F["o_out"], 16)
            sp.wait_ge(F["o_out"], 16 * (NT // GO + 1))

        @block.sync
        def _(sp):
            setup_sync(sp)
            norm_x_sync(sp)
            for l in range(3):
                sage_sync(sp, l)
            scan_marks_sync(sp)
            gather_values_sync(sp)
            weigh_sync(sp)
            feed_forward_sync(sp)

        @block.scalar
        def _(act):
            setup_scalar(act)
            norm_x_scalar(act)
            for l in range(3):
                sage_scalar(act, l)
            gather_values_scalar(act)
            softmax_scalar(act)
            weigh_scalar(act)
            feed_forward_scalar(act)

        @block.vector
        def _(dve):
            setup_vector(dve)
            norm_x_vector(dve)
            for l in range(3):
                sage_vector(dve, l)
            scan_marks_vector(dve)
            gather_values_vector(dve)
            softmax_vector(dve)
            weigh_vector(dve)
            feed_forward_vector(dve)

        @block.tensor
        def _(pe):
            for l in range(3):
                sage_tensor(pe, l)
            gather_values_tensor(pe)
            softmax_tensor(pe)
            weigh_tensor(pe)
            feed_forward_tensor(pe)

        @block.gpsimd
        def _(pool):
            setup_gpsimd(pool)
            for l in range(3):
                sage_gpsimd(pool, l)
            gather_values_gpsimd(pool)
            weigh_gpsimd(pool)


_INS = ["x", "src", "dst"] + [f"L0_gnn_{n}" for i in range(3) for n in (f"W{i}_self", f"W{i}_neigh", f"b{i}")] + [
    f"L1_gnn_{n}" for n in ("Wq", "bq", "Wk", "bk", "Wv", "bv", "Wo", "bo", "W1", "b1", "W2", "b2",
                            "bn1_g", "bn1_b", "bn2_g", "bn2_b")]


def kernel(**inputs):
    import numpy as _np
    import concourse.bacc as _bacc
    from concourse import mybir as _mybir
    from concourse.bass_utils import run_bass_kernel_spmd as _run

    nc = _bacc.Bacc("TRN2", target_bir_lowering=False, num_devices=1)
    arrays, a = {}, {}
    for name in _INS:
        v = _np.ascontiguousarray(inputs[name])
        arrays[f"in_{name}_dram"] = v
        a[name] = nc.dram_tensor(f"in_{name}_dram", v.shape, _mybir.dt.from_np(v.dtype), kind="ExternalInput").ap()
    out = nc.dram_tensor("out_0_dram", inputs["x"].shape, _mybir.dt.float32, kind="ExternalOutput").ap()
    g = {n[len("L1_gnn_"):]: a[n] for n in _INS if n.startswith("L1_gnn_")}
    gnn_kernel(nc, a["x"], a["src"], a["dst"],
               [(a[f"L0_gnn_W{i}_neigh"], a[f"L0_gnn_W{i}_self"]) for i in range(3)],
               [a[f"L0_gnn_b{i}"] for i in range(3)], out=out, **g)
    r = _run(nc, [arrays], core_ids=[0])
    return r.results[0]["out_0_dram"]
```

```python
from contextlib import ExitStack

import concourse.bass as bass
from concourse import mybir

P = 128
ALU = mybir.AluOpType
ACT = mybir.ActivationFunctionType
AX = mybir.AxisListType
F32 = mybir.dt.float32
BF16 = mybir.dt.bfloat16
I32 = mybir.dt.int32

BIG = 1.0e30
EPS = 1e-5
SLOPE = 0.2
HEADS = 8
BJ = 4
BE = P * BJ
SLOTS = 7
AHEAD = 4
CHUNKS = 14


def gnn_kernel(nc, x, src, dst, sage_w, sage_b, Wq, bq, Wk, bk, Wv, bv, Wo, bo, W1, b1, W2, b2,
               bn1_g, bn1_b, bn2_g, bn2_b, out):
    N, D = x.shape
    E = src.shape[0]
    DF = W1.shape[1]
    C = D // HEADS
    KD, KF = D // P, DF // P
    NT = -(-N // P)
    NP = NT * P
    NL = N - (NT - 1) * P
    NB = -(-E // BE)
    EP = NB * BE
    VS = D + HEADS
    AUX = 2 * HEADS + 1
    CB = NB // CHUNKS
    CE = CB * BE
    CP = CHUNKS * HEADS
    COLS = NB * BJ
    BT = 4
    BN = BT * P
    BATCHES = NT // BT
    GO = 7
    ROUNDS = NB // SLOTS
    assert NB % SLOTS == 0 and NB % CHUNKS == 0 and KD == 2 and CP <= P
    assert NT % GO == 0 and BATCHES % 2 == 0 and NT - BATCHES * BT == 1

    def dram(name, shape, dt=F32):
        return nc.dram_tensor(name, shape, dt, kind="Internal").ap()

    tables = [dram(f"h_table{i}", (NP, D)) for i in range(3)]
    x1_dram = dram("x1_dram", (NT, P, D))
    hln_dram = dram("hln_dram", (NT, P, D))
    vs_table = dram("vs_table", (NP, VS))
    v_edges = dram("v_edges", (NB, P, BJ * D))
    dst_ext = dram("dst_ext", (1, EP + 2), I32)
    src_ext = dram("src_ext", (1, EP), I32)

    with ExitStack() as ctx:
        def sb(name, shape, dt=F32):
            return ctx.enter_context(nc.sbuf_tensor(name, shape, dt))

        def ps(name, shape):
            return ctx.enter_context(nc.psum_tensor(name, shape, F32))

        def sem(name):
            return ctx.enter_context(nc.semaphore(name))

        hN_words, ring_words = NT * D, SLOTS * BJ * VS
        T = CE + 2
        arena_words = 4 * T + T // 2 + 2 * COLS * HEADS
        arena = sb("arena", [P, arena_words])
        o_late = 2 * T
        h_nodes = arena[:, 0:hN_words].rearrange("p (t d) -> p t d", d=D)
        o_ring = hN_words
        ring = arena[:, o_ring:o_ring + ring_words].rearrange("p (s w) -> p s w", w=VS)
        o_w = o_ring + ring_words
        w_sage = arena[:, o_w:o_w + 3 * 2 * KD * D].rearrange("p (l k d) -> p l k d", l=3, k=2 * KD)
        o_q = o_w + 3 * 2 * KD * D
        w_qkv = arena[:, o_q:o_q + KD * 3 * D].rearrange("p (k d) -> p k d", k=KD)
        o_proj = o_q + KD * 3 * D
        dst_b = arena[:, 0:SLOTS * BE].bitcast(I32).rearrange("p (s e) -> p s e", e=BE)
        alpha_t = arena[0:CP, 0:CE]
        fwd_t = arena[0:CP, T:T + CE]
        bwd_t = arena[0:CP, 2 * T:2 * T + CE]
        dst_t = arena[0:CP, 3 * T:4 * T].bitcast(I32)
        keep_t = arena[0:CP, 4 * T:4 * T + T // 2].bitcast(BF16)
        alpha_k = arena[:, T:T + COLS * HEADS].rearrange("p (k q) -> p k q", q=CP)
        max_e = arena[:, 3 * T:3 * T + COLS * HEADS].rearrange("p (k h) -> p k h", h=HEADS)
        o_se = 4 * T + T // 2
        s_src = arena[:, o_se:o_se + COLS * HEADS].rearrange("p (k h) -> p k h", h=HEADS)
        s_dst = arena[:, o_se + COLS * HEADS:o_se + 2 * COLS * HEADS].rearrange("p (k h) -> p k h", h=HEADS)
        aux_e = arena[:, 0:COLS * AUX].rearrange("p (k a) -> p k a", a=AUX)
        assert COLS * AUX <= 2 * T and o_proj + 7 * D <= o_se and ring_words <= 2 * COLS * HEADS
        h_cols = arena[:, o_late:o_late + hN_words].rearrange("p (t f n) -> p t f n", f=KD, n=P)
        v_ring = arena[:, o_se:o_se + SLOTS * BJ * (D + AUX)].rearrange("p (s w) -> p s w", w=D + AUX)
        o_f1 = o_late + hN_words
        f1 = arena[:, o_f1:o_f1 + 2 * KF * BN].rearrange("p (i m n) -> p i m n", i=2, m=KF)
        sums = arena[:, COLS * AUX:COLS * AUX + D + AUX]
        assert o_f1 + 2 * KF * BN <= o_se and COLS * AUX + D + AUX <= o_late

        o_late_w = o_se + SLOTS * BJ * (D + AUX)
        w_o = arena[:, o_late_w:o_late_w + KD * D].rearrange("p (k d) -> p k d", k=KD)
        w_1 = arena[:, o_late_w + KD * D:o_late_w + KD * (D + DF)].rearrange("p (k d) -> p k d", k=KD)
        w_2 = arena[:, o_late_w + KD * (D + DF):o_late_w + KD * (D + DF) + KF * D].rearrange("p (k d) -> p k d", k=KF)
        assert o_late_w + KD * (D + DF) + KF * D <= arena_words
        b_sage = sb("b_sage", [1, 3, D])
        b_qkv = arena[:, o_proj:o_proj + 3 * D]
        hln = arena[:, o_proj + 3 * D:o_proj + 4 * D]
        lhs_q = arena[:, o_proj + 4 * D:o_proj + 5 * D].rearrange("p (k n) -> p k n", n=P)
        cols = sb("cols", [P, 5 * KD + KF + KD])
        ident = sb("ident", [P, P])
        iota_n = sb("iota_n", [P, P])
        part = sb("part", [P, 1])
        tile_base = sb("tile_base", [P, NT])
        node_id = sb("node_id", [P, NT])
        iota_t = sb("iota_t", [P, P])
        zero_l = sb("zero_l", [P, P], BF16)
        zero_r = sb("zero_r", [P, D + AUX], BF16)
        ones_row = sb("ones_row", [1, P])
        src_e = sb("src_e", [P, COLS + SLOTS * BJ], I32)
        dst_i = sb("dst_i", [P, COLS], I32)
        dst_e = sb("dst_e", [P, COLS])
        idx = sb("idx", [P, 2, SLOTS * BJ], I32)
        onehot = sb("onehot", [P, BJ, P])
        s_node = sb("s_node", [P, NT, HEADS])
        tile_span = sb("tile_span", [1, NT], I32)
        need = sb("need", [1, NB + SLOTS], I32)
        NI = NB + SLOTS
        blocks_c = arena[:, o_se:o_se + NI]
        cmp_c = arena[:, o_se + NI:o_se + 2 * NI]
        starts_c, count_c, ones_c = (arena[:, o_se + 2 * NI + i:o_se + 2 * NI + i + 1] for i in range(3))
        need_f = arena[0:1, o_se + 3 * NI:o_se + 4 * NI]
        row_f = arena[0:1, o_se + 5 * NI + 3 * BE:o_se + 5 * NI + 3 * BE + NT + 1]
        HB = NB // 2
        o_raw = o_se + 6 * NI + 3 * BE
        raw_i = arena[0:HB, o_raw:o_raw + 4 * BE].bitcast(I32).rearrange("p (k h e) -> p k h e", k=2, h=2)
        raw_f = arena[0:HB, o_raw + 4 * BE:o_raw + 8 * BE].rearrange("p (k h e) -> p k h e", k=2, h=2)
        assert NB % 2 == 0 and HB <= P and HB * BJ <= 512 and o_raw + 8 * BE <= arena_words
        pads = arena[0:1, o_se + 4 * NI:o_se + 4 * NI + 3 * BE].bitcast(I32).rearrange("a (i e) -> a i e", e=BE)
        tiles3 = sb("tiles3", [P, 3 * D])
        mean, h_self, x_tile = (tiles3[:, i * D:(i + 1) * D] for i in range(3))
        lhs = sb("lhs", [P, 2 * KD, P])
        qk = sb("qk", [P, 2 * D])
        vs_tile = sb("vs_tile", [P, VS])
        small = sb("small", [P, 64])
        bn6 = sb("bn6", [P, KD, NT, 6])
        bn2 = sb("bn2", [P, NT, 2])
        rstd = sb("rstd", [P, NT])
        shift = sb("shift", [P, NT])
        crow = tiles3[0:1, 0:6 * CP].rearrange("a (k q) -> a k q", k=6)
        ccol = sb("ccol", [P, 8])

        banks = ps("banks", [P, 8, 512])
        agg, dense, dense2, aux_ps = (banks[:, i, :] for i in (0, 2, 3, 4))
        tp, tp_q = (banks[:, i, :].rearrange("p (k n) -> p k n", n=P) for i in (1, 5))
        qk_ps = banks[:, 6, :]

        col_of, at = {}, 0
        for name, v, k in (("bo", bo, KD), ("g1", bn1_g, KD), ("b1n", bn1_b, KD), ("g2", bn2_g, KD),
                           ("b2n", bn2_b, KD), ("b2", b2, KD), ("b1", b1, KF)):
            col_of[name] = (at, k, v)
            at += k

        def col(name, k):
            return cols[:, col_of[name][0] + k:col_of[name][0] + k + 1]

        const_in = sem("const_in")
        ext_in = sem("ext_in")
        edges_in = sem("edges_in")
        pads_made = sem("pads_made")
        passed = sem("passed")
        consts_made = sem("consts_made")
        ident_made = sem("ident_made")
        walk_made = sem("walk_made")
        walk_turned = sem("walk_turned")
        block = ctx.enter_context(nc.Block())
        def wait(eng, semaphore, value):
            if not isinstance(value, int) or value > 0:
                eng.wait_ge(semaphore, value)

        def first_and_rest(eng, n, body):
            body(0)
            with eng.Fori(1, n) as t:
                body(t)

        def pipeline(eng, n, depth, step):
            for t in range(depth):
                step(t)
            with eng.Fori(depth, n) as t:
                step(t)
            for t in range(n, n + depth):
                step(t)

        def there(t):
            return not isinstance(t, int) or 0 <= t < NT

        def apart(eng):
            eng.sem_inc(passed, 1)

        setup_dmas = []
        for l in range(3):
            for m in range(2):
                setup_dmas.append((w_sage[:, l, m * KD:(m + 1) * KD, :], sage_w[l][m].rearrange("(k p) n -> p k n", p=P)))
            setup_dmas.append((b_sage[0:1, l, :], sage_b[l].rearrange("(a d) -> a d", a=1)))
        for i, (w, b) in enumerate(((Wq, bq), (Wk, bk), (Wv, bv))):
            setup_dmas.append((w_qkv[:, :, i * D:(i + 1) * D], w.rearrange("(k p) n -> p k n", p=P)))
            setup_dmas.append((b_qkv[:, i * D:(i + 1) * D], b.rearrange("(a d) -> a d", a=1).broadcast_to([P, D])))
        for name, (at, k, v) in col_of.items():
            for i in range(k):
                setup_dmas.append((cols[:, at + i:at + i + 1], v[i * P:(i + 1) * P].rearrange("(p a) -> p a", a=1)))
        CONSTS = 16 * len(setup_dmas)

        def setup_sync(sp):
            sp.dma_start(dst_ext[0:1, 1:1 + E].rearrange("a (r c) -> (a r) c", r=32),
                         dst.rearrange("(r c) -> r c", r=32)).then_inc(ext_in, 16)
            sp.dma_start(src_ext[0:1, 0:E].rearrange("a (r c) -> (a r) c", r=32),
                         src.rearrange("(r c) -> r c", r=32)).then_inc(ext_in, 16)
            sp.wait_ge(pads_made, 3)
            sp.dma_start(dst_ext[0:1, 0:1], pads[:, 1, 0:1]).then_inc(ext_in, 16)
            sp.dma_start(dst_ext[0:1, 1 + EP:2 + EP], pads[:, 1, 0:1]).then_inc(ext_in, 16)
            sp.dma_start(dst_ext[0:1, 1 + E:1 + EP], pads[:, 0, 0:EP - E]).then_inc(ext_in, 16)
            sp.dma_start(src_ext[0:1, E:EP], pads[:, 2, 0:EP - E]).then_inc(ext_in, 16)
            norm_x_sync(sp)
            sp.wait_ge(ext_in, 16 * 6)
            for k, of in ((0, dst_ext[0:1, 1:1 + EP]), (1, src_ext[0:1, :])):
                for h in range(2):
                    sp.dma_start(raw_i[:, k, h, :],
                                 of[:, h * HB * BE:(h + 1) * HB * BE].rearrange("a (b e) -> (a b) e", e=BE)).then_inc(edges_in, 16)

        def setup_scalar(act):
            for to, of in setup_dmas:
                act.dma_start(to, of).then_inc(const_in, 16)

        def setup_gpsimd(pool):
            pool.memset(pads[:, 0, :], NP).then_inc(pads_made, 1)
            pool.memset(pads[:, 1, :], -1).then_inc(pads_made, 1)
            pool.memset(pads[:, 2, :], 0).then_inc(pads_made, 1)
            pool.iota(iota_n[:], [[1, P]], 0, 0, allow_small_or_imprecise_dtypes=True).then_inc(consts_made, 1)
            pool.iota(part[:], [[0, 1]], 0, 1, allow_small_or_imprecise_dtypes=True).then_inc(consts_made, 1)
            pool.iota(tile_base[:], [[P, NT]], 0, 0, allow_small_or_imprecise_dtypes=True).then_inc(consts_made, 1)
            pool.iota(node_id[:], [[P, NT]], 0, 1, allow_small_or_imprecise_dtypes=True).then_inc(consts_made, 1)
            pool.memset(zero_l[:], 0.0).then_inc(consts_made, 1)
            pool.memset(zero_r[:], 0.0).then_inc(consts_made, 1)
            pool.memset(src_e[:, COLS:], 0).then_inc(consts_made, 1)
            pool.memset(ones_row[:], 1.0).then_inc(consts_made, 1)
            pool.memset(ring[:, :, D:D + 1], 1.0).then_inc(consts_made, 1)
            pool.memset(ones_c, 1.0).then_inc(consts_made, 1)
            pool.iota(starts_c, [[0, 1]], 0, P, allow_small_or_imprecise_dtypes=True).then_inc(consts_made, 1)
            pool.iota(blocks_c, [[1, NI]], -SLOTS, 0, allow_small_or_imprecise_dtypes=True).then_inc(consts_made, 1)
        NCONST = 12

        def setup_vector(dve):
            dve.wait_ge(consts_made, NCONST)
            dve.tensor_scalar(ident[:], iota_n[:], part[:, 0:1], None, ALU.is_equal).then_inc(ident_made, 1)

        def walk_tables_vector(dve):
            TC = NT + 1
            dve.wait_ge(edges_in, 64)
            step = [0]

            def link(ins):
                step[0] += 1
                ins.then_inc(walk_made, 1)
                dve.wait_ge(walk_made, step[0])

            link(dve.tensor_copy(raw_f, raw_i))
            for k, to in ((0, dst_e[:]), (1, src_e[:, 0:COLS])):
                dve.wait_ge(walk_turned, k + 1)
                for h in range(2):
                    link(dve.tensor_copy(to[:, h * HB * BJ:(h + 1) * HB * BJ].rearrange("p (b j) -> p j b", j=BJ),
                                         banks[:, 2 * k + h, 0:HB * BJ].rearrange("p (j b) -> p j b", j=BJ)))
            assert step[0] == EDGES_TURNED
            dve.wait_ge(walk_turned, 3)
            link(dve.tensor_scalar(cmp_c[0:TC, 0:NB], banks[0:TC, 7, 0:NB], starts_c[0:TC], None, ALU.is_lt))
            link(dve.tensor_reduce(count_c[0:TC], cmp_c[0:TC, 0:NB], AX.X, ALU.add))
            link(dve.tensor_scalar(count_c[0:TC], count_c[0:TC], -1.0, 0.0, ALU.add, ALU.max))
            link(dve.tensor_scalar(cmp_c[0:NT], blocks_c[0:NT], count_c[0:NT], None, ALU.is_ge))
            dve.wait_ge(walk_turned, 4)
            link(dve.tensor_copy(row_f, banks[0:1, 6, 0:TC]))
            link(dve.scalar_tensor_tensor(tile_span[:], row_f[0:1, 1:TC], float(NB), row_f[0:1, 0:NT], ALU.mult, ALU.add))
            dve.wait_ge(walk_turned, 5)
            link(dve.tensor_tensor(need_f, banks[0:1, 5, 0:NI], blocks_c[0:1], ALU.add))
            link(dve.tensor_scalar(need_f, need_f, float(BJ), float(BJ), ALU.mult, ALU.add))
            assert step[0] == WALKED - 1
            dve.tensor_scalar(need[:], need_f, float(BJ), None, ALU.max).then_inc(walk_made, 1)

        EDGES_TURNED = 5
        WALKED = EDGES_TURNED + 9

        def walk_tables_tensor(pe):
            TC = NT + 1
            pe.wait_ge(consts_made, NCONST)
            pe.wait_ge(ident_made, 1)
            pe.wait_ge(walk_made, 1)
            for k in range(2):
                for h in range(2):
                    for j in range(BJ):
                        last = pe.transpose(banks[:, 2 * k + h, j * HB:(j + 1) * HB], raw_f[:, k, h, j:BE:BJ], ident[0:HB, 0:HB])
                last.then_inc(walk_turned, 1)
            pe.wait_ge(walk_made, EDGES_TURNED)
            pe.matmul(banks[0:TC, 7, 0:NB], ones_row[0:1, 0:TC], dst_e[0:1, 0:COLS:BJ], start=True, stop=True).then_inc(walk_turned, 1)
            pe.wait_ge(walk_made, EDGES_TURNED + 3)
            pe.matmul(banks[0:1, 6, 0:TC], count_c[0:TC], ident[0:TC, 0:TC], start=True, stop=True).then_inc(walk_turned, 1)
            pe.wait_ge(walk_made, EDGES_TURNED + 4)
            pe.matmul(banks[0:1, 5, 0:NI], ones_c[0:NT], cmp_c[0:NT], start=True, stop=True).then_inc(walk_turned, 1)

        ln_groups = [(t, min(t + 12, NT - 1)) for t in range(0, NT - 1, 12)]
        ln_groups[-1] = (ln_groups[-1][0], NT)
        ln_in = [sem(f"ln_in{g}") for g in range(len(ln_groups))]
        ln_stats = sem("ln_stats")
        ln_aggr = sem("ln_aggr")
        ln_var = sem("ln_var")
        ln_sqrt = sem("ln_sqrt")
        ln_fold = sem("ln_fold")
        ln_done = sem("ln_done")
        pad_zero = sem("pad_zero")
        stored0 = sem("stored0")
        x_tiles = x[0:(NT - 1) * P, :].rearrange("(t p) d -> p t d", p=P)

        def norm_x_sync(sp):
            for g, (t0, t1) in enumerate(ln_groups):
                t1 = min(t1, NT - 1)
                sp.dma_start(h_nodes[:, t0:t1, :], x_tiles[:, t0:t1, :]).then_inc(ln_in[g], 16)
            sp.wait_ge(pad_zero, 1)
            sp.dma_start(h_nodes[0:NL, NT - 1, :], x[(NT - 1) * P:N, :]).then_inc(ln_in[-1], 16)

        def norm_x_vector(dve):
            dve.memset(h_nodes[:, NT - 1, :], 0.0).then_inc(pad_zero, 1)

            def fold(g):
                t0, t1 = ln_groups[g]
                dve.wait_ge(ln_sqrt, g + 1)
                dve.reciprocal(rstd[:, t0:t1], rstd[:, t0:t1]).then_inc(ln_fold, 1)
                dve.wait_ge(ln_fold, 2 * g + 1)
                dve.scalar_tensor_tensor(shift[:, t0:t1], bn2[:, t0:t1, 0], -1.0, rstd[:, t0:t1],
                                         ALU.mult, ALU.mult).then_inc(ln_fold, 1)

            for g, (t0, t1) in enumerate(ln_groups):
                dve.wait_ge(ln_in[g], 32 if t1 == NT else 16)
                for t in range(t0, t1):
                    dve.bn_stats(bn6[:, 0, t, :], h_nodes[:, t, :]).then_inc(ln_stats, 1)
                dve.wait_ge(ln_stats, t1)
                for t in range(t0, t1):
                    dve.bn_aggr(bn2[:, t, :], bn6[:, 0, t, :]).then_inc(ln_aggr, 1)
                dve.wait_ge(ln_aggr, t1)
                dve.tensor_scalar(rstd[:, t0:t1], bn2[:, t0:t1, 1], EPS, None, ALU.add).then_inc(ln_var, 1)
                if g:
                    fold(g - 1)
            fold(len(ln_groups) - 1)

        def norm_x_scalar(act):
            rows = tables[0].rearrange("(t p) d -> p t d", p=P)
            for g in range(len(ln_groups) + 1):
                if g < len(ln_groups):
                    t0, t1 = ln_groups[g]
                    act.wait_ge(ln_var, g + 1)
                    act.activation(rstd[:, t0:t1], rstd[:, t0:t1], ACT.Sqrt).then_inc(ln_sqrt, 1)
                if g:
                    t0, t1 = ln_groups[g - 1]
                    act.wait_ge(ln_fold, 2 * g)
                    for t in range(t0, t1):
                        act.activation(h_nodes[:, t, :], h_nodes[:, t, :], ACT.Relu, bias=shift[:, t:t + 1],
                                       scale=rstd[:, t:t + 1]).then_inc(ln_done, 1)
                    act.wait_ge(ln_done, t1)
                    act.dma_start(rows[:, t0:t1, :], h_nodes[:, t0:t1, :]).then_inc(stored0, 16)

        PAIRS = NB + NT - 1
        TOTAL = dict(staged=ROUNDS + 1, slots_free=AHEAD + NB, rows_ready=NB, onehot_used=BJ * PAIRS,
                     onehot_made=BJ * PAIRS, base_moved=NT, agg_done=NT, deg=2 * NT, mean_made=NT, self_made=NT,
                     turned=NT, lhs_made=NT, out_done=NT, h_made=NT, stored=16 * NT, landed=16 * BJ * ROUNDS)
        W = {n: sem(n) for n in TOTAL if n != "landed"}
        landed = [sem(f"landed{s}") for s in range(SLOTS)]
        x_in = sem("x_in")
        x1_stats = sem("x1_stats")

        def since(name, w, v):
            return v + w * TOTAL[name]

        def gathers(pool, w, table, width, may_fill):
            IR = SLOTS * BJ

            def stage_indices(first, half):
                pool.tensor_copy(idx[:, half, :], src_e[:, bass.ds(first, IR)]).then_inc(W["staged"], 1)
            if w:
                pool.wait_ge(W["staged"], since("staged", w, 0))
            stage_indices(0, 0)
            def rounds(i2):
                for half in range(2):
                    i = i2 * 2 + half
                    pool.wait_ge(W["staged"], since("staged", w, i + 1))
                    for s in range(SLOTS):
                        may_fill(i, s)
                        apart(pool)
                        for j in range(BJ):
                            k = s * BJ + j
                            pool.indirect_dma_start(ring[:, k, 0:width], None, table,
                                                    bass.IndirectOffsetOnAxis(idx[:, half, k:k + 1], 0)).then_inc(landed[s], 16)
                    stage_indices((i + 1) * IR, 1 - half)
            first_and_rest(pool, ROUNDS // 2, rounds)

        def pairs_of(eng, i):
            return eng.value_load(need[0:1, bass.ds(i, 1)], min_val=0, max_val=BJ * (NB + NT + 1))

        def relay(sp, w):
            sp.sem_inc(W["slots_free"], AHEAD)
            with sp.Fori(0, ROUNDS) as i:
                for s in range(SLOTS):
                    sp.wait_ge(W["onehot_used"], since("onehot_used", w, pairs_of(sp, i * SLOTS + s + AHEAD)))
                    sp.sem_inc(W["slots_free"], 1)
                    sp.wait_ge(landed[s], since("landed", w, (i + 1) * (16 * BJ)))
                    sp.sem_inc(W["rows_ready"], 1)

        def span(eng, t):
            both = eng.value_load(tile_span[0:1, bass.ds(t, 1)], min_val=0, max_val=NB * NB - 1)
            return both % NB, both // NB

        def base_and_span(dve, w, t):
            b0, b1 = span(dve, t)
            if w > 0 or not isinstance(t, int) or t > 0:
                dve.wait_ge(W["onehot_made"], since("onehot_made", w, (b0 + t) * BJ))
            dve.tensor_scalar(iota_t[:], iota_n[:], tile_base[:, bass.ds(t, 1)], None, ALU.add).then_inc(W["base_moved"], 1)
            return b0, b1

        def onehots(dve, w, t, b0, b1, behind_first=None):
            dve.wait_ge(W["base_moved"], since("base_moved", min(w, 3), t + 1))
            apart(dve)

            def of_block(b):
                for j in range(BJ):
                    dve.wait_ge(W["onehot_used"], since("onehot_used", w, (b + t) * BJ + j + 1))
                    dve.tensor_scalar(onehot[:, j, :], iota_t[:], dst_e[:, bass.ds(b * BJ + j, 1)], None,
                                      ALU.is_equal).then_inc(W["onehot_made"], 1)
            if behind_first is None:
                with dve.Fori(b0, b1 + 1) as b:
                    of_block(b)
            else:
                of_block(b0)
                behind_first()
                with dve.If(b0 < b1):
                    with dve.Fori(b0 + 1, b1 + 1) as b:
                        of_block(b)

        def sage_gpsimd(pool, l):
            if l == 0:
                pool.wait_ge(stored0, 16 * len(ln_groups))
            else:
                pool.wait_ge(W["stored"], since("stored", l, 0))
            pool.wait_ge(consts_made, NCONST)
            pool.wait_ge(walk_made, EDGES_TURNED)

            def may_fill(i, s):
                pool.wait_ge(W["slots_free"], since("slots_free", l, i * SLOTS + s + 1))
            gathers(pool, l, tables[l], D, may_fill)

        def sage_sync(sp, l):
            relay(sp, l)

        def sage_tensor(pe, l):
            if l == 0:
                walk_tables_tensor(pe)
                pe.wait_ge(walk_made, WALKED)
                pe.wait_ge(const_in, CONSTS)
                pe.sem_inc(W["onehot_used"], BJ)
            def sums(t):
                b0, b1 = span(pe, t)
                wait(pe, W["mean_made"], since("mean_made", l, t))
                pe.matmul(agg[:, 0:D + 1], zero_l[:], zero_r[:, 0:D + 1], start=True, stop=False)
                with pe.Fori(b0, b1 + 1) as b:
                    pe.wait_ge(W["rows_ready"], since("rows_ready", l, b + 1))
                    for j in range(BJ):
                        pe.wait_ge(W["onehot_made"], since("onehot_made", l, (b + t) * BJ + j + 1))
                        pe.matmul(agg[:, 0:D + 1], onehot[:, j, :], ring[:, (b % SLOTS) * BJ + j, 0:D + 1],
                                  start=False, stop=False).then_inc(W["onehot_used"], 1)
                pe.matmul(agg[:, 0:D + 1], zero_l[:], zero_r[:, 0:D + 1], start=False, stop=True).then_inc(W["agg_done"], 1)

            def turn(t):
                wait(pe, W["lhs_made"], since("lhs_made", l, t))
                pe.wait_ge(W["self_made"], since("self_made", l, t + 1))
                for k in range(KD):
                    pe.transpose(tp[:, KD + k, :], h_self[:, k * P:(k + 1) * P], ident[:])
                pe.wait_ge(W["mean_made"], since("mean_made", l, t + 1))
                for k in range(KD):
                    last = pe.transpose(tp[:, k, :], mean[:, k * P:(k + 1) * P], ident[:])
                last.then_inc(W["turned"], 1)

            def products(t):
                wait(pe, W["h_made"], since("h_made", l, t))
                pe.matmul(dense[:, 0:D], ones_row[:], b_sage[0:1, l, :], start=True, stop=False)
                pe.wait_ge(W["lhs_made"], since("lhs_made", l, t + 1))
                for k in range(2 * KD):
                    last = pe.matmul(dense[:, 0:D], lhs[:, k, :], w_sage[:, l, k, :], start=False, stop=k == 2 * KD - 1)
                last.then_inc(W["out_done"], 1)

            def step(t):
                sums(t)
                turn(t)
                products(t)

            def last_layer_step(t):
                if there(t):
                    sums(t)
                if there(t - 1):
                    turn(t - 1)
                if there(t - 4):
                    turn_normed_tensor(pe, t - 4)
                if there(t - 2):
                    products(t - 2)
                if there(t - 4):
                    project_tensor(pe, t - 4)
            if l < 2:
                first_and_rest(pe, NT, step)
            else:
                pipeline(pe, NT, 4, last_layer_step)

        def sage_vector(dve, l):
            def means(t):
                dve.wait_ge(W["agg_done"], since("agg_done", l, t + 1))
                dve.tensor_scalar(small[:, 0:1], agg[:, D:D + 1], 1.0, None, ALU.max).then_inc(W["deg"], 1)
                dve.wait_ge(W["deg"], since("deg", l, 2 * t + 1))
                dve.reciprocal(small[:, 1:2], small[:, 0:1]).then_inc(W["deg"], 1)
                dve.wait_ge(W["deg"], since("deg", l, 2 * t + 2))
                wait(dve, W["turned"], since("turned", l, t))
                dve.tensor_scalar(mean[:], agg[:, 0:D], small[:, 1:2], None, ALU.mult).then_inc(W["mean_made"], 1)

            def residual(t):
                dve.wait_ge(x_in, 16 * t + 16)
                dve.wait_ge(W["out_done"], since("out_done", l, t + 1))
                dve.tensor_tensor(h_nodes[:, t, :], dense[:, 0:D], x_tile[:], ALU.add).then_inc(W["h_made"], 1)
                dve.wait_ge(W["h_made"], since("h_made", l, t + 1))
                apart(dve)
                dve.bn_stats(stats6, h_nodes[:, t, :]).then_inc(x1_stats, 1)
                dve.wait_ge(x1_stats, 2 * t + 1)
                apart(dve)
                dve.bn_aggr(mean_var, stats6).then_inc(x1_stats, 1)
                dve.wait_ge(x1_stats, 2 * t + 2)
                dve.tensor_scalar(var_eps, mean_var[:, 1:2], EPS, None, ALU.add).then_inc(Q["var"], 1)

            def step(t):
                onehots(dve, l, t, *base_and_span(dve, l, t))
                means(t)

            def last_layer_step(t):
                def between():
                    if there(t - 4):
                        norm_fold_vector(dve, t - 4)
                    if there(t - 3):
                        residual(t - 3)
                if there(t):
                    onehots(dve, l, t, *base_and_span(dve, l, t), behind_first=between)
                    means(t)
                else:
                    between()
                if there(t - 5):
                    project_vector(dve, t - 5)
            if l < 2:
                first_and_rest(dve, NT, step)
            else:
                pipeline(dve, NT, 5, last_layer_step)

        def sage_scalar(act, l):
            to = (tables[l + 1].rearrange("(t p) d -> t p d", p=P) if l < 2 else x1_dram)

            def own_rows(t):
                wait(act, W["turned"], since("turned", l, t))
                act.activation(h_self[:], h_nodes[:, t, :], ACT.Copy).then_inc(W["self_made"], 1)

            def take_turned(t):
                act.wait_ge(W["turned"], since("turned", l, t + 1))
                wait(act, W["out_done"], since("out_done", l, t))
                act.activation(lhs[:], tp, ACT.Copy).then_inc(W["lhs_made"], 1)

            def store(t):
                act.wait_ge(W["h_made"], since("h_made", l, t + 1))
                act.dma_start(to[t], h_nodes[:, t, :]).then_inc(W["stored"], 16)

            def step(t):
                own_rows(t)
                take_turned(t)
                act.wait_ge(W["out_done"], since("out_done", l, t + 1))
                apart(act)
                act.activation(h_nodes[:, t, :], dense[:, 0:D], ACT.Relu).then_inc(W["h_made"], 1)
                store(t)

            def x_load(t):
                wait(act, W["h_made"], since("h_made", l, t))
                if isinstance(t, int) and t == NT - 1:
                    act.dma_start(x_tile[0:NL, :], x[(NT - 1) * P:N, :]).then_inc(x_in, 16)
                else:
                    act.dma_start(x_tile[:], x[0:(NT - 1) * P, :].rearrange("(t p) d -> t p d", p=P)[t]).then_inc(x_in, 16)

            def root_of(t):
                act.wait_ge(Q["var"], t + 1)
                act.activation(root, var_eps, ACT.Sqrt).then_inc(Q["sqrt"], 1)

            def last_layer_step(t):
                if there(t - 6):
                    values_out_scalar(act, t - 6)
                if there(t - 1):
                    own_rows(t - 1)
                if there(t - 4):
                    norm_scalar(act, t - 4)
                if there(t - 3):
                    store(t - 3)
                    root_of(t - 3)
                if there(t - 2):
                    x_load(t - 2)
                if there(t - 1):
                    take_turned(t - 1)
                if there(t - 4):
                    take_normed_scalar(act, t - 4)
            if l < 2:
                first_and_rest(act, NT, step)
            else:
                pipeline(act, NT, 6, last_layer_step)
                act.wait_ge(Q["hln_out"], 16 * NT)

        Q = {n: sem(f"q_{n}") for n in ("var", "sqrt", "fold", "h_made", "turned", "lhs_made", "out_done",
                                        "taken", "step", "s_made", "hln_out", "vs_out")}
        stats6, mean_var, var_eps, root, scale1, shift1 = (
            small[:, a:b] for a, b in ((40, 46), (46, 48), (48, 49), (49, 50), (50, 51), (51, 52)))

        def norm_fold_vector(dve, t):
            dve.wait_ge(Q["sqrt"], t + 1)
            wait(dve, Q["h_made"], t)
            apart(dve)
            dve.reciprocal(scale1, root).then_inc(Q["fold"], 1)
            dve.wait_ge(Q["fold"], 2 * t + 1)
            dve.scalar_tensor_tensor(shift1, mean_var[:, 0:1], -1.0, scale1, ALU.mult, ALU.mult).then_inc(Q["fold"], 1)
            dve.wait_ge(Q["fold"], 2 * t + 2)
            apart(dve)

        def norm_scalar(act, t):
            wait(act, Q["turned"], t)
            wait(act, Q["hln_out"], 16 * t)
            act.wait_ge(Q["fold"], 2 * t + 2)
            apart(act)
            act.activation(hln, h_nodes[:, t, :], ACT.Relu, bias=shift1, scale=scale1).then_inc(Q["h_made"], 1)
            act.wait_ge(Q["h_made"], t + 1)
            act.dma_start(hln_dram[t], hln).then_inc(Q["hln_out"], 16)

        def turn_normed_tensor(pe, t):
            pe.wait_ge(Q["h_made"], t + 1)
            wait(pe, Q["lhs_made"], t)
            for k in range(KD):
                last = pe.transpose(tp_q[:, k, :], hln[:, k * P:(k + 1) * P], ident[:])
            last.then_inc(Q["turned"], 1)

        def project_tensor(pe, t):
            pe.wait_ge(Q["lhs_made"], t + 1)
            wait(pe, Q["taken"], t)
            wait(pe, Q["step"], 4 * t)
            for k in range(KD):
                pe.matmul(qk_ps, lhs_q[:, k, :], w_qkv[:, k, 0:2 * D], start=k == 0, stop=k == KD - 1)
            for k in range(KD):
                last = pe.matmul(dense2[:, 0:D], lhs_q[:, k, :], w_qkv[:, k, 2 * D:3 * D], start=k == 0, stop=k == KD - 1)
            last.then_inc(Q["out_done"], 1)

        def take_normed_scalar(act, t):
            act.wait_ge(Q["turned"], t + 1)
            wait(act, Q["out_done"], t)
            act.activation(lhs_q, tp_q[:, 0:KD, :], ACT.Copy).then_inc(Q["lhs_made"], 1)

        def values_out_scalar(act, t):
            act.wait_ge(Q["taken"], t + 1)
            act.wait_ge(Q["s_made"], t + 1)
            act.dma_start(vs_table.rearrange("(t p) d -> t p d", p=P)[t], vs_tile[:]).then_inc(Q["vs_out"], 16)

        def project_vector(dve, t):
            dve.wait_ge(Q["out_done"], t + 1)
            dve.tensor_tensor(qk[:], qk_ps, b_qkv[:, 0:2 * D], ALU.add).then_inc(Q["step"], 1)
            wait(dve, Q["vs_out"], 16 * t)
            dve.tensor_tensor(vs_tile[:, 0:D], dense2[:, 0:D], b_qkv[:, 2 * D:3 * D], ALU.add).then_inc(Q["taken"], 1)
            dve.wait_ge(Q["step"], t * 4 + 1)
            dve.tensor_tensor(qk[:, 0:D], qk[:, 0:D], qk[:, D:2 * D], ALU.mult).then_inc(Q["step"], 1)
            dve.wait_ge(Q["step"], t * 4 + 2)
            dve.tensor_reduce(small[:, 8:8 + HEADS], qk[:, 0:D].rearrange("p (h c) -> p h c", h=HEADS), AX.X,
                              ALU.add).then_inc(Q["step"], 1)
            dve.wait_ge(Q["step"], t * 4 + 3)
            dve.tensor_scalar(s_node[:, t, :], small[:, 8:8 + HEADS], float(C) ** -0.5, None, ALU.mult).then_inc(Q["step"], 1)
            dve.wait_ge(Q["step"], t * 4 + 4)
            apart(dve)
            dve.tensor_copy(vs_tile[:, D:VS], s_node[:, t, :]).then_inc(Q["s_made"], 1)

        A = {n: sem(f"a_{n}") for n in ("s_taken", "zeroed", "sd_added",
                                        "node_made", "dst_ready")}
        a_stored = [sem(f"a_stored{s}") for s in range(SLOTS)]
        sp_in = [sem(f"sp_in{s}") for s in range(SLOTS)]
        VS_DONE = 16 * NT

        def gather_values_gpsimd(pool):
            pool.wait_ge(Q["vs_out"], VS_DONE)

            def may_fill(i, s):
                wait(pool, a_stored[s], i * 16)
                pool.wait_ge(A["s_taken"], i * SLOTS + s + 1)
            gathers(pool, 3, vs_table, VS, may_fill)

        dst_loaded, scan_step = sem("dst_loaded"), sem("scan_step")
        same, ends = ccol[0:CP, 3:4], (ccol[0:CP, 6:7], ccol[0:CP, 7:8])

        def scan_marks_sync(sp):
            sp.wait_ge(Q["out_done"], NT)
            sp.wait_ge(Q["taken"], NT)
            sp.wait_ge(Q["hln_out"], 16 * NT)
            sp.wait_ge(W["stored"], since("stored", 2, 16 * NT))
            for c in range(CHUNKS):
                sp.dma_start(dst_t[c * HEADS:(c + 1) * HEADS, 0:T],
                             dst_ext[0:1, c * CE:c * CE + T].broadcast_to([HEADS, T])).then_inc(dst_loaded, 16)
            sp.dma_start(dst_i[:].rearrange("p (b j) -> p b j", j=BJ),
                         dst_ext[0:1, 0:EP].rearrange("a (b p j) -> (a p) b j", p=P, j=BJ)).then_inc(dst_loaded, 16)

        def scan_marks_vector(dve):
            def link(step, ins):
                ins.then_inc(scan_step, 1)
                dve.wait_ge(scan_step, step)

            dve.wait_ge(dst_loaded, 16 * (CHUNKS + 1))
            link(1, dve.tensor_tensor(keep_t[:, 0:CE + 1], dst_t[:, 1:T], dst_t[:, 0:T - 1], ALU.is_equal))
            link(2, dve.tensor_scalar(keep_t[:, 0:CE + 1], keep_t[:, 0:CE + 1], -1.0, BIG, ALU.add, ALU.mult))
            link(3, dve.tensor_copy(ends[0], dst_t[:, 1:2]))
            link(4, dve.tensor_copy(ends[1], dst_t[:, CE:CE + 1]))
            link(5, dve.tensor_tensor(same, ends[0], ends[1], ALU.is_equal))
            link(6, dve.tensor_scalar(same, same, -1.0, BIG, ALU.add, ALU.mult))

        def gather_values_sync(sp):
            def one_round(i):
                for s in range(SLOTS):
                    b = i * SLOTS + s
                    sp.wait_ge(W["onehot_used"], since("onehot_used", 3, pairs_of(sp, b)))
                    sp.dma_start(dst_b[:, s, :], dst_ext[0:1, bass.ds(b * BE + 1, BE)].broadcast_to([P, BE])).then_inc(sp_in[s], 16)
                    if s > 0 or not isinstance(i, int):
                        sp.wait_ge(sp_in[s - 1], (i + 1) * 16 if s > 0 else i * 16)
                        sp.sem_inc(A["dst_ready"], 1)
            first_and_rest(sp, ROUNDS, one_round)
            sp.wait_ge(sp_in[SLOTS - 1], ROUNDS * 16)
            sp.sem_inc(A["dst_ready"], 1)

        def gather_values_scalar(act):
            act.sem_inc(A["s_taken"], SLOTS)
            with act.Fori(0, ROUNDS) as i:
                for s in range(SLOTS):
                    act.wait_ge(landed[s], since("landed", 3, (i + 1) * (16 * BJ)))
                    act.activation(s_src[:, bass.ds((i * SLOTS + s) * BJ, BJ), :], ring[:, s * BJ:(s + 1) * BJ, D:VS],
                                   ACT.Copy).then_inc(A["s_taken"], 1)
                    act.dma_start(v_edges[i * SLOTS + s].rearrange("p (j d) -> p j d", d=D),
                                  ring[:, s * BJ:(s + 1) * BJ, 0:D]).then_inc(a_stored[s], 16)

        def gather_values_vector(dve):
            dve.memset(s_dst[:], 0.0).then_inc(A["zeroed"], 1)
            dve.wait_ge(A["zeroed"], 1)
            dve.sem_inc(A["sd_added"], 1)
            with dve.Fori(0, NT) as t:
                b0, b1 = span(dve, t)
                dve.tensor_copy(small[:, 16:17], node_id[:, bass.ds(t, 1)]).then_inc(A["node_made"], 1)
                dve.wait_ge(A["node_made"], t + 1)
                apart(dve)

                def one_hots(b, js):
                    for j in js:
                        dve.wait_ge(W["onehot_used"], since("onehot_used", 3, (b + t) * BJ + j + 1))
                        dve.tensor_scalar(onehot[:, j, :], dst_b[:, b % SLOTS, j:BE:BJ], small[:, 16:17], None,
                                          ALU.is_equal).then_inc(W["onehot_made"], 1)

                def add(b):
                    dve.wait_ge(W["onehot_used"], since("onehot_used", 3, (b + t) * BJ + 2 * BJ))
                    at_b = s_dst[:, bass.ds(b * BJ, BJ), :].rearrange("p k h -> p (k h)")
                    dve.tensor_tensor(at_b, at_b, aux_ps[:, 0:BJ * HEADS], ALU.add).then_inc(A["sd_added"], 1)

                dve.wait_ge(A["dst_ready"], b0 + 1)
                one_hots(b0, range(BJ))
                with dve.If(b0 < b1):
                    with dve.Fori(b0 + 1, b1 + 1) as b:
                        dve.wait_ge(A["dst_ready"], b + 1)
                        one_hots(b, range(BJ // 2))
                        add(b - 1)
                        one_hots(b, range(BJ // 2, BJ))
                add(b1)

        def gather_values_tensor(pe):
            pe.wait_ge(Q["step"], 4 * NT)
            with pe.Fori(0, NT) as t:
                b0, b1 = span(pe, t)
                with pe.Fori(b0, b1 + 1) as b:
                    pe.wait_ge(A["sd_added"], b + t + 1)
                    for j in range(BJ):
                        pe.wait_ge(W["onehot_made"], since("onehot_made", 3, (b + t) * BJ + j + 1))
                        pe.matmul(aux_ps[:, j * HEADS:(j + 1) * HEADS], onehot[:, j, :], s_node[:, t, :],
                                  start=True, stop=True, skip_group_check=True).then_inc(W["onehot_used"], 1)

        B = {n: sem(f"b_{n}") for n in ("step", "turned", "taken", "alpha", "scan", "row", "rowps",
                                        "colps", "max_made", "back", "back_taken", "args", "exps", "aux_made")}
        BG = CB

        def turn_bank(g):
            return banks[:, 5 + g % 2, :].rearrange("p (j n) -> p j n", n=P)

        def softmax_tensor(pe):
            pe.wait_ge(B["alpha"], 1)
            for g in range(BG):
                if g >= 2:
                    pe.wait_ge(B["taken"], g - 1)
                for j in range(BJ):
                    last = pe.transpose(turn_bank(g)[0:CP, j, :], alpha_k[:, g * BJ + j, :], ident[:])
                last.then_inc(B["turned"], 1)
            for d in range(2):
                pe.wait_ge(B["scan"], d + 1)
                for k in range(3):
                    last = pe.transpose(aux_ps[0:1, k * CP:(k + 1) * CP], ccol[0:CP, k:k + 1], ident[0:CP, 0:CP])
                last.then_inc(B["rowps"], 1)
                pe.wait_ge(B["row"], d + 1)
                pe.matmul(dense2[0:CP, 0:1], crow[0:1, 5, :], ones_row[0:1, 0:1], start=True, stop=True).then_inc(B["colps"], 1)
            for g in range(BG):
                pe.wait_ge(B["max_made"], g + 1)
                if g >= 2:
                    pe.wait_ge(B["back_taken"], g - 1)
                for j in range(BJ):
                    last = pe.transpose(turn_bank(g)[:, j, 0:CP], fwd_t[:, g * BE + j:(g + 1) * BE:BJ], ident[0:CP, 0:CP])
                last.then_inc(B["back"], 1)

        def softmax_scalar(act):
            for g in range(BG):
                act.wait_ge(B["turned"], g + 1)
                act.activation(alpha_t[:, g * BE:(g + 1) * BE].rearrange("q (p j) -> q p j", j=BJ),
                               turn_bank(g)[0:CP, :, :].rearrange("q j p -> q p j"), ACT.Copy).then_inc(B["taken"], 1)
            for g in range(BG):
                act.wait_ge(B["back"], g + 1)
                to = max_e.rearrange("p (c k) h -> p k c h", c=CHUNKS)[:, g * BJ:(g + 1) * BJ]
                act.activation(to, turn_bank(g)[:, :, 0:CP].rearrange("p j (c h) -> p j c h", h=HEADS), ACT.Copy).then_inc(B["back_taken"], 1)
            act.wait_ge(B["args"], 1)
            act.activation(aux_e[:, :, HEADS:2 * HEADS], s_dst[:], ACT.Exp).then_inc(B["exps"], 1)
            act.wait_ge(B["args"], 2)
            act.activation(aux_e[:, :, 0:HEADS], s_src[:], ACT.Exp).then_inc(B["exps"], 1)

        def softmax_vector(dve):
            steps = [0]

            def link(ins):
                steps[0] += 1
                ins.then_inc(B["step"], 1)
                dve.wait_ge(B["step"], steps[0])

            def loops(part):
                link(dve.tensor_tensor(s_dst[:, part], s_dst[:, part], s_dst[:, part], ALU.add))
                link(dve.scalar_tensor_tensor(s_dst[:, part], s_dst[:, part], SLOPE, s_dst[:, part], ALU.mult, ALU.max))

            dve.wait_ge(A["sd_added"], NB + NT)
            early = slice(0, (NB - CB) * BJ)
            dve.wait_ge(A["s_taken"], SLOTS + NB - CB)
            link(dve.tensor_tensor(s_src[:, early], s_src[:, early], s_dst[:, early], ALU.add))
            link(dve.scalar_tensor_tensor(s_src[:, early], s_src[:, early], SLOPE, s_src[:, early], ALU.mult, ALU.max))
            loops(early)
            late = slice((NB - CB) * BJ, COLS)
            dve.wait_ge(A["s_taken"], SLOTS + NB)
            for s in range(SLOTS):
                dve.wait_ge(a_stored[s], 16 * ROUNDS)
            link(dve.tensor_tensor(s_src[:, late], s_src[:, late], s_dst[:, late], ALU.add))
            link(dve.scalar_tensor_tensor(s_src[:, late], s_src[:, late], SLOPE, s_src[:, late], ALU.mult, ALU.max))
            dve.tensor_copy(alpha_k.rearrange("p k (c h) -> p c k h", c=CHUNKS),
                            s_src.rearrange("p (c k) h -> p c k h", c=CHUNKS)).then_inc(B["alpha"], 1)
            loops(late)
            dve.wait_ge(B["taken"], BG)
            for d in range(2):
                if d == 0:
                    run, flip = fwd_t, slice(None)
                    keep, out_edge, in_edge = keep_t[:, 0:CE], slice(CE - 1, CE), keep_t[:, 0:1]
                else:
                    run, flip = bwd_t, slice(None, None, -1)
                    keep, out_edge, in_edge = keep_t[:, 1:CE + 1], slice(0, 1), keep_t[:, CE:CE + 1]
                link(dve.tensor_tensor_scan(run[:, flip], keep[:, flip], alpha_t[:, flip], -BIG, ALU.add, ALU.max))
                link(dve.tensor_copy(ccol[0:CP, 0:1], run[:, out_edge]))
                link(dve.tensor_copy(ccol[0:CP, 2:3], in_edge))
                dve.tensor_tensor(ccol[0:CP, 1:2], in_edge, same, ALU.add).then_inc(B["scan"], 1)
                dve.wait_ge(B["rowps"], d + 1)
                link(dve.tensor_copy(crow[0:1, 0:3, :].rearrange("a k (h c) -> a k h c", h=HEADS),
                                     aux_ps[0:1, 0:3 * CP].rearrange("a (k c h) -> a k h c", k=3, h=HEADS)))
                link(dve.tensor_tensor_scan(crow[0:1, 3, flip], crow[0:1, 1, flip], crow[0:1, 0, flip], -BIG, ALU.add, ALU.max))
                link(dve.memset(crow[0:1, 4, :], -BIG))
                to, of = (slice(1, CP), slice(0, CP - 1)) if d == 0 else (slice(0, CP - 1), slice(1, CP))
                link(dve.tensor_tensor(crow[0:1, 4, to], crow[0:1, 3, of], crow[0:1, 2, to], ALU.add))
                dve.tensor_copy(crow[0:1, 5, :].rearrange("a (c h) -> a h c", h=HEADS),
                                crow[0:1, 4, :].rearrange("a (h c) -> a h c", h=HEADS)).then_inc(B["row"], 1)
                dve.wait_ge(B["colps"], d + 1)
                link(dve.tensor_copy(ccol[0:CP, 4:5], dense2[0:CP, 0:1]))
                tmp = bwd_t if d == 0 else alpha_t
                link(dve.tensor_scalar(tmp, dst_t[:, 1:CE + 1], ends[d], -BIG, ALU.not_equal, ALU.mult))
                link(dve.scalar_tensor_tensor(run, tmp, ccol[0:CP, 4:5], run, ALU.add, ALU.max))
            for g in range(BG):
                of = slice(g * BE, (g + 1) * BE)
                dve.tensor_tensor(fwd_t[:, of], fwd_t[:, of], bwd_t[:, of], ALU.max).then_inc(B["max_made"], 1)
            dve.wait_ge(B["back_taken"], BG)
            link(dve.tensor_tensor(max_e[:], max_e[:], s_dst[:], ALU.max))
            dve.tensor_tensor(s_dst[:], s_dst[:], max_e[:], ALU.subtract).then_inc(B["args"], 1)
            dve.tensor_tensor(s_src[:], s_src[:], max_e[:], ALU.subtract).then_inc(B["args"], 1)
            link(dve.tensor_tensor(aux_e[:, :, 2 * HEADS], dst_i[:], dst_e[:], ALU.is_lt))
            dve.wait_ge(B["exps"], 1)
            own = aux_e[:, :, HEADS:2 * HEADS]
            dve.tensor_tensor(own, own, aux_e[:, :, 2 * HEADS:AUX].broadcast_to([P, COLS, HEADS]),
                              ALU.mult).then_inc(B["aux_made"], 1)

        C2 = {n: sem(f"c_{n}") for n in ("aux_there", "rows_ready", "agg_done", "agg_taken", "step", "attn_made", "v_in", "hln_in",
                                         "turned", "lhs_made", "out_done", "h_made", "stats")}
        late_in = sem("late_in")

        def weigh_sync(sp):
            sp.wait_ge(B["exps"], 2)
            def one_round(i):
                for s in range(SLOTS):
                    b = i * SLOTS + s
                    sp.wait_ge(W["onehot_used"], since("onehot_used", 4, pairs_of(sp, b)))
                    sp.dma_start(v_ring[:, s * BJ:(s + 1) * BJ, 0:D],
                                 v_edges[b].rearrange("p (j d) -> p j d", d=D)).then_inc(sp_in[s], 16)
                if isinstance(i, int):
                    for to, of in ((w_o, Wo), (w_1, W1), (w_2, W2)):
                        sp.dma_start(to, of.rearrange("(k p) n -> p k n", p=P)).then_inc(late_in, 16)
            first_and_rest(sp, ROUNDS, one_round)

        def weigh_gpsimd(pool):
            pool.wait_ge(B["aux_made"], 1)
            pool.wait_ge(B["exps"], 2)
            with pool.Fori(0, ROUNDS) as i:
                for s in range(SLOTS):
                    pool.wait_ge(sp_in[s], (i + 1) * 16 + 16 * ROUNDS)
                    apart(pool)
                    of_b = bass.ds((i * SLOTS + s) * BJ, BJ)
                    pool.tensor_copy(v_ring[:, s * BJ:(s + 1) * BJ, D:D + AUX], aux_e[:, of_b, :]).then_inc(C2["aux_there"], 1)
                    v = v_ring[:, s * BJ:(s + 1) * BJ, 0:D].rearrange("p j (h c) -> p j h c", h=HEADS)
                    w = aux_e[:, of_b, 0:HEADS].rearrange("p j (h o) -> p j h o", o=1)
                    pool.tensor_tensor(v, v, w.broadcast_to([P, BJ, HEADS, C]), ALU.mult).then_inc(C2["rows_ready"], 1)

        def weigh_tensor(pe):
            AW = D + AUX

            def step(t):
                if there(t):
                    b0, b1 = span(pe, t)
                    wait(pe, C2["agg_taken"], t)
                    pe.matmul(agg[:, 0:AW], zero_l[:], zero_r[:, 0:AW], start=True, stop=False)
                    with pe.Fori(b0, b1 + 1) as b:
                        pe.wait_ge(C2["aux_there"], b + 1)
                        apart(pe)
                        pe.wait_ge(C2["rows_ready"], b + 1)
                        for j in range(BJ):
                            pe.wait_ge(W["onehot_made"], since("onehot_made", 4, (b + t) * BJ + j + 1))
                            pe.matmul(agg[:, 0:AW], onehot[:, j, :], v_ring[:, (b % SLOTS) * BJ + j, :],
                                      start=False, stop=False).then_inc(W["onehot_used"], 1)
                    pe.matmul(agg[:, 0:AW], zero_l[:], zero_r[:, 0:AW], start=False, stop=True).then_inc(C2["agg_done"], 1)
                if there(t - 1):
                    pe.wait_ge(C2["attn_made"], t)
                    wait(pe, C2["lhs_made"], t - 1)
                    for k in range(KD):
                        last = pe.transpose(tp[:, k, :], mean[:, k * P:(k + 1) * P], ident[:])
                    last.then_inc(C2["turned"], 1)
                if isinstance(t, int) and t == 1:
                    pe.wait_ge(late_in, 48)
                if there(t - 2):
                    pe.wait_ge(C2["lhs_made"], t - 1)
                    wait(pe, C2["h_made"], KD * (t - 2))
                    pe.wait_ge(C2["hln_in"], 16 * (t - 1))
                    for f in range(KD):
                        fs = slice(f * P, (f + 1) * P)
                        for k in range(KD):
                            pe.matmul(dense[:, fs], w_o[:, k, fs], lhs[:, k, :], start=k == 0, stop=False)
                        last = pe.matmul(dense[:, fs], h_self[:, fs], ident[:], start=False, stop=True)
                    last.then_inc(C2["out_done"], 1)
            pipeline(pe, NT, 2, step)

        def weigh_vector(dve):
            own, den = small[:, 8:16], small[:, 16:24]
            step = C2["step"]
            STEPS = 5

            def heads(a):
                return a.rearrange("p (h c) -> p h c", h=HEADS)

            def spread(a):
                return a.rearrange("p (h o) -> p h o", o=1).broadcast_to([P, HEADS, C])

            def attention(t):
                dve.wait_ge(C2["agg_taken"], t + 1)
                dve.tensor_scalar(own, sums[:, D + HEADS:D + 2 * HEADS], sums[:, D + 2 * HEADS:D + AUX], 1.0,
                                  ALU.subtract, ALU.add).then_inc(step, 1)
                dve.wait_ge(step, t * STEPS + 1)
                dve.tensor_tensor(den, sums[:, D:D + HEADS], own, ALU.add).then_inc(step, 1)
                dve.wait_ge(C2["v_in"], 16 * t + 16)
                dve.tensor_tensor(heads(x_tile[:]), heads(x_tile[:]), spread(own), ALU.mult).then_inc(step, 1)
                dve.wait_ge(step, t * STEPS + 2)
                dve.reciprocal(den, den).then_inc(step, 1)
                dve.wait_ge(step, t * STEPS + 4)
                dve.tensor_tensor(x_tile[:], x_tile[:], sums[:, 0:D], ALU.add).then_inc(step, 1)
                dve.wait_ge(step, t * STEPS + 5)
                wait(dve, C2["turned"], t)
                dve.tensor_tensor(heads(mean[:]), heads(x_tile[:]), spread(den), ALU.mult).then_inc(C2["attn_made"], 1)

            def tile_step(t):
                def between():
                    if there(t - 1):
                        attention(t - 1)
                if there(t):
                    onehots(dve, 4, t, *base_and_span(dve, 4, t), behind_first=between)
                else:
                    between()
                if there(t - 3):
                    dve.wait_ge(C2["h_made"], KD * (t - 2))
                    apart(dve)
                    tile_stats(dve, t - 3, C2["stats"])
            pipeline(dve, NT, 3, tile_step)

        def tile_stats(dve, t, done):
            nodes = NL if isinstance(t, int) and t == NT - 1 else P
            for f in range(KD):
                dve.bn_stats(bn6[:, f, t, :], h_cols[:, t, f, 0:nodes]).then_inc(done, 1)

        def weigh_scalar(act):
            def step(t):
                if there(t):
                    wait(act, C2["attn_made"], t)
                    act.dma_start(x_tile[:], vs_table.rearrange("(t p) d -> t p d", p=P)[t, :, 0:D]).then_inc(C2["v_in"], 16)
                    act.wait_ge(C2["agg_done"], t + 1)
                    act.activation(sums, agg[:, 0:D + AUX], ACT.Copy).then_inc(C2["agg_taken"], 1)
                if there(t - 1):
                    wait(act, C2["out_done"], t - 1)
                    act.dma_start(h_self[:], hln_dram[t - 1]).then_inc(C2["hln_in"], 16)
                    act.wait_ge(C2["turned"], t)
                    act.activation(lhs[:, 0:KD, :], tp[:, 0:KD, :], ACT.Copy).then_inc(C2["lhs_made"], 1)
                if there(t - 2):
                    act.wait_ge(C2["out_done"], t - 1)
                    apart(act)
                    for f in range(KD):
                        act.activation(h_cols[:, t - 2, f, :], dense[:, f * P:(f + 1) * P], ACT.Identity,
                                       bias=col("bo", f)).then_inc(C2["h_made"], 1)
            pipeline(act, NT, 2, step)

        F = {n: sem(f"f_{n}") for n in ("step", "var", "root", "hb_made", "f1_done", "f1_taken", "z_done", "z_made",
                                        "stats2", "x1_in", "zs_made", "turned", "o_made", "o_out")}
        scale, bias, var = (lambda f, i=i: small[:, 32 + 8 * f + i:33 + 8 * f + i] for i in (3, 4, 2))
        FOLD_STEPS = 5 * KD

        def fold_norm(dve, w, gname, bname):
            n = w * FOLD_STEPS
            for f in range(KD):
                mv = small[:, 32 + 8 * f:34 + 8 * f]
                dve.bn_aggr(mv, bn6[:, f, :, :].rearrange("p t s -> p (t s)")).then_inc(F["step"], 1)
                n += 1
                dve.wait_ge(F["step"], n)
                dve.tensor_scalar(var(f), mv[:, 1:2], EPS, None, ALU.add).then_inc(F["var"], 1)
            dve.wait_ge(F["root"], KD * (w + 1))
            for ins in (lambda f: dve.reciprocal(var(f), var(f)),
                        lambda f: dve.tensor_tensor(scale(f), var(f), col(gname, f), ALU.mult),
                        lambda f: dve.tensor_tensor(bias(f), small[:, 32 + 8 * f:33 + 8 * f], scale(f), ALU.mult),
                        lambda f: dve.tensor_tensor(bias(f), col(bname, f), bias(f), ALU.subtract)):
                for f in range(KD):
                    ins(f).then_inc(F["step"], 1)
                n += KD
                dve.wait_ge(F["step"], n)

        def roots(act, w):
            act.wait_ge(F["var"], KD * (w + 1))
            for f in range(KD):
                act.activation(var(f), var(f), ACT.Sqrt).then_inc(F["root"], 1)

        def batch(i, f):
            if isinstance(i, int) and i == BATCHES:
                return h_cols[:, i * BT:NT, f, :]
            return h_cols[:, bass.ds(i * BT, BT), f, :]

        def nodes_of(i):
            return (NT - BATCHES * BT) * P if isinstance(i, int) and i == BATCHES else BN

        def tiles_of(a, i):
            return a[:, 0:nodes_of(i)].rearrange("p (t n) -> p t n", n=P)

        def feed_forward_vector(dve):
            dve.wait_ge(C2["stats"], KD * NT)
            fold_norm(dve, 0, "g1", "b1n")
            def norm(i):
                for f in range(KD):
                    dve.tensor_scalar(batch(i, f), batch(i, f), scale(f), bias(f), ALU.mult, ALU.add).then_inc(F["hb_made"], 1)
            with dve.Fori(0, BATCHES) as i:
                norm(i)
            norm(BATCHES)
            def residual(i):
                for f in range(KD):
                    dve.wait_ge(F["z_done"], i * KD + f + 1)
                    apart(dve)
                    dve.scalar_tensor_tensor(batch(i, f), tiles_of(banks[:, 4 + f, :], i), col("b2", f), batch(i, f),
                                             ALU.add, ALU.add).then_inc(F["z_made"], 1)
                dve.wait_ge(F["z_made"], (i + 1) * KD)
                apart(dve)
                for t in range(nodes_of(i) // P):
                    tile_stats(dve, i * BT + t, F["stats2"])
            dve.wait_ge(F["hb_made"], (BATCHES + 1) * KD)
            with dve.Fori(0, BATCHES) as i:
                residual(i)
            residual(BATCHES)
            dve.wait_ge(F["stats2"], KD * NT)
            fold_norm(dve, 1, "g2", "b2n")
            dve.sem_inc(F["step"], 1)
            dve.wait_ge(F["x1_in"], 16 * NT // GO)
            for g in range(NT // GO):
                dve.wait_ge(F["turned"], g + 1)
                x1_g = h_nodes[:, g * GO:(g + 1) * GO, :].rearrange("p t d -> p (t d)")
                dve.tensor_tensor(x1_g, x1_g, turned_bank(g)[:, 0:GO * D], ALU.add).then_inc(F["o_made"], 1)

        def turned_bank(g):
            return banks[:, g % 2 * 4:g % 2 * 4 + 4, :].rearrange("p k n -> p (k n)")

        def feed_forward_tensor(pe):
            def first(i, half):
                for m in range(KF):
                    wait(pe, F["f1_taken"], KF * (i - 1) + m + 1)
                    for k in range(KD):
                        if m == 0:
                            pe.wait_ge(F["hb_made"], i * KD + k + 1)
                        last = pe.matmul(banks[:, m, 0:nodes_of(i)], w_1[:, k, m * P:(m + 1) * P], batch(i, k),
                                         start=k == 0, stop=k == KD - 1)
                    last.then_inc(F["f1_done"], 1)

            def second(i, half):
                for f in range(KD):
                    wait(pe, F["z_made"], KD * (i - 1) + f + 1)
                    for m in range(KF):
                        if f == 0:
                            pe.wait_ge(F["f1_taken"], i * KF + m + 1)
                        last = pe.matmul(banks[:, 4 + f, 0:nodes_of(i)], w_2[:, m, f * P:(f + 1) * P],
                                         f1[:, half, m, 0:nodes_of(i)], start=m == 0, stop=m == KF - 1)
                    last.then_inc(F["z_done"], 1)

            def two(i2):
                for half in range(2):
                    i = i2 * 2 + half
                    first(i, half)
                    if not (isinstance(i, int) and i == 0):
                        second(i - 1, 1 - half)
            first_and_rest(pe, BATCHES // 2, two)
            first(BATCHES, 0)
            second(BATCHES - 1, 1)
            second(BATCHES, 0)
            for g in range(NT // GO):
                pe.wait_ge(F["zs_made"], KD * g + KD)
                if g == 0:
                    pe.wait_ge(F["z_made"], KD * (BATCHES + 1))
                    pe.wait_ge(F["f1_taken"], KF * (BATCHES + 1))
                wait(pe, F["o_made"], g - 1)
                for t in range(GO):
                    for f in range(KD):
                        at = t * D + f * P
                        last = pe.transpose(turned_bank(g)[:, at:at + P], h_cols[:, g * GO + t, f, :], ident[:])
                last.then_inc(F["turned"], 1)

        def feed_forward_scalar(act):
            roots(act, 0)
            def take(i, half):
                for m in range(KF):
                    act.wait_ge(F["f1_done"], i * KF + m + 1)
                    if m == 0:
                        wait(act, F["z_done"], (i - 1) * KD)
                    act.activation(f1[:, half, m, 0:nodes_of(i)], banks[:, m, 0:nodes_of(i)], ACT.Relu,
                                   bias=col("b1", m)).then_inc(F["f1_taken"], 1)

            def two(i2):
                for half in range(2):
                    take(i2 * 2 + half, half)
            first_and_rest(act, BATCHES // 2, two)
            take(BATCHES, 0)
            roots(act, 1)
            act.wait_ge(F["step"], 2 * FOLD_STEPS + 1)
            for g in range(NT // GO):
                for f in range(KD):
                    of = h_cols[:, g * GO:(g + 1) * GO, f, :]
                    act.activation(of, of, ACT.Identity, bias=bias(f), scale=scale(f)).then_inc(F["zs_made"], 1)

        def feed_forward_sync(sp):
            sp.wait_ge(C2["rows_ready"], NB)
            sp.wait_ge(C2["aux_there"], NB)
            for g in range(NT // GO):
                gs = slice(g * GO, (g + 1) * GO)
                sp.dma_start(h_nodes[:, gs, :], x1_dram.rearrange("t p d -> p t d")[:, gs, :]).then_inc(F["x1_in"], 16)
            out_t = out[0:(NT - 1) * P, :].rearrange("(t p) d -> p t d", p=P)
            for g in range(NT // GO):
                sp.wait_ge(F["o_made"], g + 1)
                g1 = min((g + 1) * GO, NT - 1)
                sp.dma_start(out_t[:, g * GO:g1, :], h_nodes[:, g * GO:g1, :]).then_inc(F["o_out"], 16)
            sp.dma_start(out[(NT - 1) * P:N, :], h_nodes[0:NL, NT - 1, :]).then_inc(F["o_out"], 16)
            sp.wait_ge(F["o_out"], 16 * (NT // GO + 1))

        @block.sync
        def _(sp):
            setup_sync(sp)
            sp.wait_ge(walk_made, WALKED)
            for l in range(3):
                sage_sync(sp, l)
            scan_marks_sync(sp)
            gather_values_sync(sp)
            weigh_sync(sp)
            feed_forward_sync(sp)

        @block.scalar
        def _(act):
            norm_x_scalar(act)
            setup_scalar(act)
            for l in range(3):
                sage_scalar(act, l)
            gather_values_scalar(act)
            softmax_scalar(act)
            weigh_scalar(act)
            feed_forward_scalar(act)

        @block.vector
        def _(dve):
            setup_vector(dve)
            norm_x_vector(dve)
            walk_tables_vector(dve)
            for l in range(3):
                sage_vector(dve, l)
            scan_marks_vector(dve)
            gather_values_vector(dve)
            softmax_vector(dve)
            weigh_vector(dve)
            feed_forward_vector(dve)

        @block.tensor
        def _(pe):
            for l in range(3):
                sage_tensor(pe, l)
            gather_values_tensor(pe)
            softmax_tensor(pe)
            weigh_tensor(pe)
            feed_forward_tensor(pe)

        @block.gpsimd
        def _(pool):
            setup_gpsimd(pool)
            for l in range(3):
                sage_gpsimd(pool, l)
            gather_values_gpsimd(pool)
            weigh_gpsimd(pool)


_INS = ["x", "src", "dst"] + [f"L0_gnn_{n}" for i in range(3) for n in (f"W{i}_self", f"W{i}_neigh", f"b{i}")] + [
    f"L1_gnn_{n}" for n in ("Wq", "bq", "Wk", "bk", "Wv", "bv", "Wo", "bo", "W1", "b1", "W2", "b2",
                            "bn1_g", "bn1_b", "bn2_g", "bn2_b")]


def kernel(**inputs):
    import numpy as _np
    import concourse.bacc as _bacc
    from concourse import mybir as _mybir
    from concourse.bass_utils import run_bass_kernel_spmd as _run

    nc = _bacc.Bacc("TRN2", target_bir_lowering=False, num_devices=1)
    arrays, a = {}, {}
    for name in _INS:
        v = _np.ascontiguousarray(inputs[name])
        arrays[f"in_{name}_dram"] = v
        a[name] = nc.dram_tensor(f"in_{name}_dram", v.shape, _mybir.dt.from_np(v.dtype), kind="ExternalInput").ap()
    out = nc.dram_tensor("out_0_dram", inputs["x"].shape, _mybir.dt.float32, kind="ExternalOutput").ap()
    g = {n[len("L1_gnn_"):]: a[n] for n in _INS if n.startswith("L1_gnn_")}
    gnn_kernel(nc, a["x"], a["src"], a["dst"],
               [(a[f"L0_gnn_W{i}_neigh"], a[f"L0_gnn_W{i}_self"]) for i in range(3)],
               [a[f"L0_gnn_b{i}"] for i in range(3)], out=out, **g)
    r = _run(nc, [arrays], core_ids=[0])
    return r.results[0]["out_0_dram"]
```
